# Optimizing a Trainium2 kernel written in Bass

```python
import numpy as np
import jax
import jax.numpy as jnp

def _softmax(x, axis=-1):
    return jax.nn.softmax(x, axis=axis)

def _gelu(x):
    return jax.nn.gelu(x, approximate=True)

def _silu(x):
    return jax.nn.silu(x)

def _sigmoid(x):
    return jax.nn.sigmoid(x)

def _layernorm(x, axis=-1, eps=1e-05):
    m = jnp.mean(x, axis=axis, keepdims=True)
    v = jnp.var(x, axis=axis, keepdims=True)
    return (x - m) / jnp.sqrt(v + eps)

def _scatter_add(tgt, idx, src, axis=0):
    return tgt.at[idx].add(src)

def _segment_sum(src, seg, n):
    return jax.ops.segment_sum(src, seg, n)
kernel_name = 'mk_decoder_preln_d1_seqx_r4_c11409'

def setup_inputs(seed: int=0):
    np.random.seed(seed)
    _w = jnp.asarray

    def _rec_inputs():
        import jax
        import jax.numpy as jnp
        _rk = jax.random.key(seed)
        x = -0.0002928 + 1 * jax.random.normal(jax.random.fold_in(_rk, 1), (8, 256, 256), jnp.float32)
        _lenS = 256 - jax.random.randint(jax.random.fold_in(_rk, 7), (8,), 0, max(1, 256 // 4) + 1, jnp.int32)
        _lenS2 = 256 - jax.random.randint(jax.random.fold_in(_rk, 8), (8,), 0, max(1, 256 // 4) + 1, jnp.int32)
        _ctx_768P = jax.random.normal(jax.random.fold_in(_rk, 11), (8, 16, 192), jnp.float32)
        _ctx_768c = jax.random.dirichlet(jax.random.fold_in(_rk, 511), 0.3 * jnp.ones((16,), jnp.float32), (8, 256))
        _ctx_768t = jnp.einsum('bsk,bkd->bsd', _ctx_768c, _ctx_768P)
        _ctx_768t = _ctx_768t * jax.lax.rsqrt(jnp.mean(jnp.square(_ctx_768t)) + 1e-12) * 0.953939
        ctx_768 = 2.09791e-05 + 1.00001 * (_ctx_768t + 0.3 * jax.random.normal(jax.random.fold_in(_rk, 611), (8, 256, 192), jnp.float32))
        return (x, ctx_768)
    x, ctx_768 = _rec_inputs()

    def _L0_attn_setup():
        import jax, jax.numpy as jnp
        import numpy as np
        SLEN, BSZ, D_MODEL = (256, 8, 256)
        N_HEAD, D_HEAD = (16, 64)
        EPS_LN = 1e-05
        SCALE = 1.0 / np.sqrt(D_HEAD)

        def _fast_weight_memory(q, k, v, beta):
            bsz = q.shape[1]
            W0 = jnp.zeros((bsz, N_HEAD, D_HEAD, D_HEAD), q.dtype)

            def step(W, xs):
                qt, kt, vt, bt = xs
                v_old = jnp.einsum('bhij,bhj->bhi', W, kt)
                delta = bt * (vt - v_old)
                W = W + delta[..., :, None] * kt[..., None, :]
                out = jnp.einsum('bhij,bhj->bhi', W, qt)
                return (W, out)
            _, outs = jax.lax.scan(step, W0, (q, k, v, beta))
            return outs
        key = jax.random.key(seed)
        k1, k2, k3 = jax.random.split(key, 3)
        h = jax.random.normal(k1, (SLEN, BSZ, D_MODEL), jnp.float32)
        W_qkvb = jax.random.normal(k2, (D_MODEL, N_HEAD * (3 * D_HEAD + 1)), jnp.float32) * 0.02
        W_o = jax.random.normal(k3, (N_HEAD * D_HEAD, D_MODEL), jnp.float32) * 0.02
        ln_g = jnp.ones((D_MODEL,), jnp.float32)
        ln_b = jnp.zeros((D_MODEL,), jnp.float32)
        return {'h': h, 'W_qkvb': W_qkvb, 'W_o': W_o, 'ln_g': ln_g, 'ln_b': ln_b}
    _L0_attn_all = _L0_attn_setup()
    _L0_attn_in = {k: v for k, v in _L0_attn_all.items() if k in ('W_qkvb', 'W_o', 'ln_g', 'ln_b')}
    del _L0_attn_all

    def _L0_xattn_setup():
        import jax, jax.numpy as jnp
        import numpy as np
        HEADS = 8
        DIM_HEAD = 128
        ATTN_MATRIX_SCALE = 1.5
        SCALE = DIM_HEAD ** (-0.5)

        def _split_heads(t):
            b, n, _ = t.shape
            t = t.reshape(b, n, HEADS, DIM_HEAD)
            return t.transpose(2, 0, 1, 3).reshape(HEADS, b * n, DIM_HEAD)
        key = jax.random.key(seed)
        ks = jax.random.split(key, 7)
        b, n, m = (2, 512, 512)
        qd, cd, inner = (256, 192, HEADS * DIM_HEAD)
        x = jax.random.normal(ks[0], (b, n, qd), dtype=jnp.float32)
        context = jax.random.normal(ks[1], (b, m, cd), dtype=jnp.float32)
        Wq = jax.random.normal(ks[2], (qd, inner), dtype=jnp.float32) * qd ** (-0.5)
        Wk = jax.random.normal(ks[3], (cd, inner), dtype=jnp.float32) * cd ** (-0.5)
        Wv = jax.random.normal(ks[4], (cd, inner), dtype=jnp.float32) * cd ** (-0.5)
        Wout = jax.random.normal(ks[5], (inner, qd), dtype=jnp.float32) * inner ** (-0.5)
        bout = jnp.zeros((qd,), dtype=jnp.float32)
        return {'x': x, 'context': context, 'Wq': Wq, 'Wk': Wk, 'Wv': Wv, 'Wout': Wout, 'bout': bout}
    _L0_xattn_all = _L0_xattn_setup()
    _L0_xattn_in = {k: v for k, v in _L0_xattn_all.items() if k in ('Wq', 'Wk', 'Wv', 'Wout', 'bout')}
    del _L0_xattn_all

    def _L0_ffn_setup():
        import jax, jax.numpy as jnp
        import numpy as np
        NUM_EXPERTS = 8
        CAPACITY_FACTOR = 1.0
        key = jax.random.key(seed)
        k1, k2, k3, k4 = jax.random.split(key, 4)
        B, S, D, E, F = (8, 512, 256, NUM_EXPERTS, 1024)
        x = jax.random.normal(k1, (B, S, D), dtype=jnp.float32)
        router_w = jax.random.normal(k2, (D, E), dtype=jnp.float32) * D ** (-0.5)
        w1 = jax.random.normal(k3, (E, D, F), dtype=jnp.float32) * D ** (-0.5)
        w2 = jax.random.normal(k4, (E, F, D), dtype=jnp.float32) * F ** (-0.5)
        return {'x': x, 'router_w': router_w, 'w1': w1, 'w2': w2}
    _L0_ffn_all = _L0_ffn_setup()
    _L0_ffn_in = {k: v for k, v in _L0_ffn_all.items() if k in ('router_w', 'w1', 'w2')}
    del _L0_ffn_all
    return {'x': x, 'ctx_768': ctx_768, 'L0_attn_W_qkvb': _L0_attn_in['W_qkvb'], 'L0_attn_W_o': _L0_attn_in['W_o'], 'L0_attn_ln_g': _L0_attn_in['ln_g'], 'L0_attn_ln_b': _L0_attn_in['ln_b'], 'L0_xattn_Wq': _L0_xattn_in['Wq'], 'L0_xattn_Wk': _L0_xattn_in['Wk'], 'L0_xattn_Wv': _L0_xattn_in['Wv'], 'L0_xattn_Wout': _L0_xattn_in['Wout'], 'L0_xattn_bout': _L0_xattn_in['bout'], 'L0_ffn_router_w': _L0_ffn_in['router_w'], 'L0_ffn_w1': _L0_ffn_in['w1'], 'L0_ffn_w2': _L0_ffn_in['w2']}

def reference(x, ctx_768, L0_attn_W_qkvb, L0_attn_W_o, L0_attn_ln_g, L0_attn_ln_b, L0_xattn_Wq, L0_xattn_Wk, L0_xattn_Wv, L0_xattn_Wout, L0_xattn_bout, L0_ffn_router_w, L0_ffn_w1, L0_ffn_w2):
    import jax
    import jax.numpy as jnp

    def _L0_attn_ref(h, W_qkvb, W_o, ln_g, ln_b):
        import jax, jax.numpy as jnp
        import numpy as np
        SLEN, BSZ, D_MODEL = (256, 8, 256)
        N_HEAD, D_HEAD = (16, 64)
        EPS_LN = 1e-05
        SCALE = 1.0 / np.sqrt(D_HEAD)

        def _fast_weight_memory(q, k, v, beta):
            bsz = q.shape[1]
            W0 = jnp.zeros((bsz, N_HEAD, D_HEAD, D_HEAD), q.dtype)

            def step(W, xs):
                qt, kt, vt, bt = xs
                v_old = jnp.einsum('bhij,bhj->bhi', W, kt)
                delta = bt * (vt - v_old)
                W = W + delta[..., :, None] * kt[..., None, :]
                out = jnp.einsum('bhij,bhj->bhi', W, qt)
                return (W, out)
            _, outs = jax.lax.scan(step, W0, (q, k, v, beta))
            return outs
        slen, bsz, _ = h.shape
        qkvb = (h @ W_qkvb).reshape(slen, bsz, N_HEAD, 3 * D_HEAD + 1)
        q = qkvb[..., :D_HEAD]
        k = qkvb[..., D_HEAD:2 * D_HEAD]
        v = qkvb[..., 2 * D_HEAD:3 * D_HEAD]
        beta = jax.nn.sigmoid(qkvb[..., 3 * D_HEAD:])
        q = jax.nn.elu(q) + 1.0
        k = jax.nn.elu(k) + 1.0
        q = q / q.sum(-1, keepdims=True)
        k = k / k.sum(-1, keepdims=True)
        outs = _fast_weight_memory(q, k, v, beta)
        layer_out = (SCALE * outs).reshape(slen, bsz, N_HEAD * D_HEAD)
        attn_out = layer_out @ W_o
        x = h + attn_out
        mu = x.mean(-1, keepdims=True)
        var = jnp.mean((x - mu) ** 2, axis=-1, keepdims=True)
        return (x - mu) / jnp.sqrt(var + EPS_LN) * ln_g + ln_b

    def _L0_xattn_ref(x, context, Wq, Wk, Wv, Wout, bout):
        import jax, jax.numpy as jnp
        import numpy as np
        HEADS = 8
        DIM_HEAD = 128
        ATTN_MATRIX_SCALE = 1.5
        SCALE = DIM_HEAD ** (-0.5)

        def _split_heads(t):
            b, n, _ = t.shape
            t = t.reshape(b, n, HEADS, DIM_HEAD)
            return t.transpose(2, 0, 1, 3).reshape(HEADS, b * n, DIM_HEAD)
        b, n, _ = x.shape
        qh = _split_heads(jnp.einsum('bnq,qi->bni', x, Wq))
        kh = _split_heads(jnp.einsum('bmc,ci->bmi', context, Wk))
        vh = _split_heads(jnp.einsum('bmc,ci->bmi', context, Wv))
        sim = jnp.einsum('hid,hjd->hij', qh, kh) * SCALE
        mean = jnp.mean(sim, axis=-1, keepdims=True)
        sim = (sim - mean) * ATTN_MATRIX_SCALE + mean
        attn = jax.nn.softmax(sim, axis=-1)
        out = jnp.einsum('hij,hjd->hid', attn, vh)
        out = out.reshape(HEADS, b, n, DIM_HEAD).transpose(1, 2, 0, 3)
        out = out.reshape(b, n, HEADS * DIM_HEAD)
        return jnp.einsum('bni,iq->bnq', out, Wout) + bout

    def _L0_ffn_ref(x, router_w, w1, w2):
        import jax, jax.numpy as jnp
        import numpy as np
        NUM_EXPERTS = 8
        CAPACITY_FACTOR = 1.0
        B, S, D = x.shape
        E = router_w.shape[1]
        T = B * S
        C = int(CAPACITY_FACTOR * T / E)
        x_flat = x.reshape(T, D)
        logits = x_flat @ router_w
        probs = jax.nn.softmax(logits, axis=-1)
        expert_idx = jnp.argmax(probs, axis=-1)
        gate = jnp.take_along_axis(probs, expert_idx[:, None], axis=1)[:, 0]
        onehot = jax.nn.one_hot(expert_idx, E, dtype=jnp.float32)
        pos_all = jnp.cumsum(onehot, axis=0) - 1.0
        pos = jnp.take_along_axis(pos_all, expert_idx[:, None], axis=1)[:, 0]
        pos = pos.astype(jnp.int32)
        keep = (pos < C).astype(x_flat.dtype)
        pos_c = jnp.clip(pos, 0, C - 1)
        expert_in = jnp.zeros((E, C, D), dtype=x_flat.dtype)
        expert_in = expert_in.at[expert_idx, pos_c].add(x_flat * keep[:, None])
        hidden = jax.nn.gelu(jnp.einsum('ecd,edf->ecf', expert_in, w1))
        expert_out = jnp.einsum('ecf,efd->ecd', hidden, w2)
        y = expert_out[expert_idx, pos_c] * (gate * keep)[:, None]
        return y.reshape(B, S, D)
    x = x + _L0_attn_ref(_layernorm(x, axis=-1), L0_attn_W_qkvb, L0_attn_W_o, L0_attn_ln_g, L0_attn_ln_b)
    x = x + _L0_xattn_ref(_layernorm(x, axis=-1), ctx_768, L0_xattn_Wq, L0_xattn_Wk, L0_xattn_Wv, L0_xattn_Wout, L0_xattn_bout)
    x = x + _L0_ffn_ref(_layernorm(x, axis=-1), L0_ffn_router_w, L0_ffn_w1, L0_ffn_w2)
    return x

_drawn_inputs = setup_inputs


def setup_inputs(seed=0):
    import zlib

    import numpy as np

    out = dict(_drawn_inputs(seed))
    spreads = {'L0_attn_ln_g': (1.0, 0.2), 'L0_attn_ln_b': (0.0, 0.1), 'L0_xattn_bout': (0.0, 0.1)}
    factors = {'L0_attn_W_qkvb': 21.883, 'L0_attn_W_o': 22.107}
    for name, (base, spread) in spreads.items():
        noise = np.random.default_rng([zlib.crc32(name.encode()), seed]).standard_normal(out[name].shape)
        drawn = base * np.exp(spread * noise) if base else spread * noise
        out[name] = jnp.asarray(drawn.astype(out[name].dtype))
    for name, factor in factors.items():
        out[name] = (out[name] * factor).astype(out[name].dtype)
    return out
```

```python
from contextlib import ExitStack

import concourse.bass as bass
from concourse import mybir

F32 = mybir.dt.float32
F32R = mybir.dt.float32r
I32 = mybir.dt.int32
ALU = mybir.AluOpType
ACT = mybir.ActivationFunctionType
AX = mybir.AxisListType.X

P = 128
D = 256
DC = D // P
T, B = 8, 256
HALVES = B // P
TILES = T * HALVES
TOK = T * B
EPS = 1e-5

NH, DH = 16, 64
HW = 3 * DH + 1
INNER = NH * DH
FAST_SCALE = 1.0 / 8.0
GH = 4
GROUPS = NH // GH

XH, XD = 8, 128
CD = 192
C2 = CD - P
JT = TOK // P
SOFT_SCALE = 1.5 * XD ** -0.5

E, F = 8, 1024
FC = F // P
CAP = TOK // E
CT = CAP // P


def newton_rsqrt(dve, ve, y, t, done, base):
    dve.tensor_tensor(t, y, y, ALU.mult).then_inc(done, 1)
    dve.wait_ge(done, base + 1)
    dve.tensor_tensor(t, t, ve, ALU.mult).then_inc(done, 1)
    dve.wait_ge(done, base + 2)
    dve.tensor_scalar(t, t, -0.5, 1.5, ALU.mult, ALU.add).then_inc(done, 1)
    dve.wait_ge(done, base + 3)
    dve.tensor_tensor(y, y, t, ALU.mult).then_inc(done, 1)
    dve.wait_ge(done, base + 4)


def fast_weight_block(nc, x, w_qkvb, w_o, ident, hall):
    with ExitStack() as ctx:
        def sb(name, shape, dt=F32):
            return ctx.enter_context(nc.sbuf_tensor(name, shape, dt))

        def pb(name, shape):
            return ctx.enter_context(nc.psum_tensor(name, shape, F32))

        def sem(name):
            return ctx.enter_context(nc.semaphore(name))

        wq = sb("fw_wqkvb", [P, DC, NH * HW])
        wo = sb("fw_wo", [P, INNER // P, D])
        hcur = sb("fw_hcur", [P, 2, D])
        hT = sb("fw_hT", [P, 2, DC, P])
        ebuf = sb("fw_ebuf", [P, 2, GH, 2 * DH])
        vbuf = sb("fw_vbuf", [P, NH, DH])
        qcur = sb("fw_qcur", [P, 2, NH, DH])
        kall = sb("fw_kall", [P, T, NH, DH])
        dall = sb("fw_dall", [P, T, NH, DH])
        prod = sb("fw_prod", [P, T, NH, DH])
        prodp = sb("fw_prodp", [P, T, NH, DH])
        oT = sb("fw_oT", [P, INNER // P, P])
        eb = sb("fw_eb", [P, NH])
        beta = sb("fw_beta", [P, NH])
        nrm = sb("fw_nrm", [P, 2, NH])
        rq = sb("fw_rq", [P, NH])
        rk = sb("fw_rk", [P, T, NH])
        nbk = sb("fw_nbk", [P, NH])
        ck = sb("fw_ck", [P, T, NH])
        cq = sb("fw_cq", [P, 2, T, NH])
        st = sb("fw_st", [P, TILES, 6])
        mv = sb("fw_mv", [P, TILES, 2])
        ve = sb("fw_ve", [P, TILES])
        rstd = sb("fw_rstd", [P, TILES])
        tmp = sb("fw_tmp", [P, TILES])

        pp = [pb(f"fw_pp{i}", [P, GH, 256]) for i in range(2)]
        po = pb("fw_po", [P, INNER // P, P])
        ph = pb("fw_ph", [P, DC, P])
        pa = pb("fw_pa", [P, D])

        x_in = [sem(f"x_in{s}") for s in range(HALVES)]
        wq_in, wo_in = sem("wq_in"), sem("wo_in")
        id_ready = sem("id_ready")
        ln = sem("ln")
        var_ready, sd_ready = sem("var_ready"), sem("sd_ready")
        h_ready = sem("h_ready")
        hcur_free, hcur_ready = sem("hcur_free"), sem("hcur_ready")
        hT_ps, hT_ready = sem("hT_ps"), sem("hT_ready")
        proj_done = sem("proj_done")
        u_ready = sem("u_ready")
        e_ready = sem("e_ready")
        vb_ready = sem("vb_ready")
        f_done = sem("f_done")
        norm = sem("norm")
        beta_ready = sem("beta_ready")
        bv_ready = sem("bv_ready")
        kk = sem("kk")
        delta_ready = sem("delta_ready")
        qk_mul = sem("qk_mul")
        cq_step = sem("cq_step")
        cq_ready = sem("cq_ready")
        po_slot = sem("po_slot")
        po_done = sem("po_done")
        oT_ready = sem("oT_ready")
        att_done = sem("att_done")

        cum = [t * (t + 1) // 2 for t in range(T + 1)]
        xs = x.rearrange("t (s p) d -> s p t d", p=P)
        block = ctx.enter_context(nc.Block())

        @block.sync
        def _(sp):
            for s in range(HALVES):
                sp.dma_start(hall[:, s * T:(s + 1) * T, :], xs[s]).then_inc(x_in[s], 16)
            sp.dma_start(wq[:], w_qkvb.rearrange("(c p) n -> p c n", p=P)).then_inc(wq_in, 16)
            sp.dma_start(wo[:], w_o.rearrange("(c p) n -> p c n", p=P)).then_inc(wo_in, 16)

        @block.gpsimd
        def _(pool):
            pool.memset(ident[:], 0.0).then_inc(id_ready, 1)
            pool.wait_ge(id_ready, 1)
            pool.affine_select(out=ident[:], in_=ident[:], compare_op=ALU.not_equal, fill=1.0, base=0,
                               pattern=[[-1, P]], channel_multiplier=1).then_inc(id_ready, 1)
            pool.sem_inc(bv_ready, 1)
            with pool.Fori(0, HALVES) as s:
                for t in range(T):
                    pool.wait_ge(vb_ready, 1 + (s * T + t + 1) * GROUPS)
                    pool.wait_ge(beta_ready, s * T + t + 1)
                    dst = prod[:, t] if t else dall[:, 0]
                    pool.tensor_tensor(dst, vbuf[:], beta[:].unsqueeze(2).to_broadcast([P, NH, DH]),
                                       ALU.mult).then_inc(bv_ready, 1)
                    pool.wait_ge(f_done, 1 + (s * T + t + 1) * GROUPS)
                    pool.wait_ge(po_done, 1 + s * T + t)
                    pool.tensor_tensor(prodp[:, 0:t + 1], kall[:, 0:t + 1],
                                       qcur[:, t % 2].unsqueeze(1).to_broadcast([P, t + 1, NH, DH]),
                                       ALU.mult).then_inc(qk_mul, 1)
                    pool.wait_ge(cq_ready, s * T + t + 1)
                    pool.wait_ge(delta_ready, s * T + t + 1)
                    for i in range(t + 1):
                        pool.tensor_tensor(prodp[:, i], dall[:, i],
                                           cq[:, t % 2, i].unsqueeze(2).to_broadcast([P, NH, DH]),
                                           ALU.mult).then_inc(po_slot, 1)

        @block.scalar
        def _(act):
            act.wait_ge(var_ready, 1)
            act.activation(rstd[:], ve[:], ACT.Sqrt).then_inc(sd_ready, 1)
            act.sem_inc(vb_ready, 1)
            act.sem_inc(hT_ready, 1)
            act.sem_inc(oT_ready, 1)
            with act.Fori(0, HALVES) as s:
                def copy_h(t):
                    act.wait_ge(h_ready, 1)
                    act.wait_ge(hcur_free, s * T + t + 1)
                    act.activation(hcur[:, t % 2], hall[:, bass.ds(s * T + t, 1), :], ACT.Copy) \
                        .then_inc(hcur_ready, 1)

                def copy_oT(t):
                    act.wait_ge(po_done, 1 + s * T + t + 1)
                    act.activation(oT[:], po[:], ACT.Copy).then_inc(oT_ready, 1)

                for t in range(T):
                    n = s * T + t
                    copy_h(t)
                    act.wait_ge(hT_ps, n + 1)
                    act.activation(hT[:, t % 2], ph[:], ACT.Copy).then_inc(hT_ready, 1)
                    for g in range(GROUPS):
                        ps = pp[g % 2]
                        act.wait_ge(proj_done, n * GROUPS + g + 1)
                        if g >= 2:
                            act.wait_ge(f_done, 1 + n * GROUPS + g - 1)
                        elif t:
                            act.wait_ge(f_done, 1 + n * GROUPS + g - 1)
                        else:
                            act.wait_ge(f_done, 1 + n * GROUPS)
                        act.activation(ebuf[:, g % 2], ps[:, :, 0:2 * DH], ACT.Relu, scale=-1.0) \
                            .then_inc(u_ready, 1)
                        if g == 0:
                            act.wait_ge(bv_ready, 1 + n)
                        hs = slice(GH * g, GH * g + GH)
                        act.activation(vbuf[:, hs],
                                       ps[:, :, 2 * DH:3 * DH], ACT.Copy)
                        act.activation(eb[:, hs].unsqueeze(2),
                                       ps[:, :, 3 * DH:HW], ACT.Exp, scale=-1.0).then_inc(vb_ready, 1)
                        act.wait_ge(u_ready, n * GROUPS + g + 1)
                        act.activation(ebuf[:, g % 2], ebuf[:, g % 2], ACT.Exp, scale=-1.0) \
                            .then_inc(e_ready, 1)
                    if t:
                        copy_oT(t - 1)
                copy_oT(T - 1)

        @block.tensor
        def _(pe):
            pe.wait_ge(id_ready, 2)
            pe.wait_ge(wq_in, 16)
            pe.wait_ge(wo_in, 16)
            pe.sem_inc(po_done, 1)
            with pe.Fori(0, HALVES) as s:
                def project(t):
                    n = s * T + t
                    pe.wait_ge(hcur_ready, n + 1)
                    pe.wait_ge(hT_ready, 1 + n)
                    for c in range(DC):
                        last = pe.transpose(ph[:, c], hcur[:, t % 2, c * P:(c + 1) * P], ident[:])
                    last.then_inc(hT_ps, 1)
                    pe.wait_ge(hT_ready, 1 + n + 1)
                    for g in range(GROUPS):
                        if g >= 2 or t:
                            pe.wait_ge(f_done, 1 + n * GROUPS + g - 1)
                            pe.wait_ge(vb_ready, 1 + n * GROUPS + g - 1)
                        else:
                            pe.wait_ge(f_done, 1 + n * GROUPS)
                            pe.wait_ge(vb_ready, 1 + n * GROUPS)
                        for b in range(2):
                            c0 = (GH * g + 2 * b) * HW
                            for c in range(DC):
                                last = pe.matmul(pp[g % 2][:, 2 * b:2 * b + 2, 0:HW], hT[:, t % 2, c],
                                                 wq[:, c, c0:c0 + 2 * HW].rearrange("p (h n) -> p h n", n=HW), start=(c == 0), stop=(c == DC - 1))
                        last.then_inc(proj_done, 1)

                def read_out(t):
                    n = s * T + t
                    pe.wait_ge(oT_ready, 1 + n)
                    for i in range(t + 1):
                        pe.wait_ge(po_slot, s * cum[T] + cum[t] + i + 1)
                        row = prodp[:, i].rearrange("p h c -> p (h c)")
                        for c in range(INNER // P):
                            last = pe.matmul(po[:, c], row[:, c * P:(c + 1) * P], ident[:],
                                             start=(i == 0 and c % 4 == 0), stop=(i == t),
                                             skip_group_check=True)
                    last.then_inc(po_done, 1)
                    pe.wait_ge(oT_ready, 1 + n + 1)
                    pe.wait_ge(hcur_free, n + 2)
                    for c in range(INNER // P):
                        last = pe.matmul(pa[:], oT[:, c], wo[:, c], start=(c == 0), stop=(c == INNER // P - 1))
                    last.then_inc(att_done, 1)

                for t in range(T):
                    project(t)
                    if t:
                        read_out(t - 1)
                read_out(T - 1)

        @block.vector
        def _(dve):
            for m in range(TILES):
                if m % T == 0:
                    dve.wait_ge(x_in[m // T], 16)
                dve.bn_stats(st[:, m], hall[:, m]).then_inc(ln, 1)
            for m in range(TILES):
                dve.wait_ge(ln, TILES if m == 0 else TILES + m)
                dve.bn_aggr(mv[:, m], st[:, m]).then_inc(ln, 1)
            dve.wait_ge(ln, 2 * TILES)
            dve.tensor_scalar(ve[:], mv[:, :, 1], EPS, None, ALU.add).then_inc(var_ready, 1)
            dve.wait_ge(sd_ready, 1)
            dve.reciprocal(rstd[:], rstd[:]).then_inc(ln, 1)
            dve.wait_ge(ln, 2 * TILES + 1)
            newton_rsqrt(dve, ve[:], rstd[:], tmp[:], ln, 2 * TILES + 1)
            for m in range(TILES):
                last = dve.tensor_scalar(hall[:, m], hall[:, m], mv[:, m, 0:1], rstd[:, m:m + 1],
                                         ALU.subtract, ALU.mult)
            last.then_inc(h_ready, 1)
            dve.sem_inc(hcur_free, 2)
            dve.sem_inc(f_done, 1)

            with dve.Fori(0, HALVES) as s:
                def features(t, g):
                    n = s * T + t
                    ps = pp[g % 2]
                    hs = slice(GH * g, GH * g + GH)
                    dve.wait_ge(e_ready, n * GROUPS + g + 1)
                    dve.scalar_tensor_tensor(qcur[:, t % 2, hs],
                                             ps[:, :, 0:DH], 1.0, ebuf[:, g % 2, :, 0:DH],
                                             ALU.add, ALU.max)
                    dve.scalar_tensor_tensor(kall[:, t, hs],
                                             ps[:, :, DH:2 * DH], 1.0, ebuf[:, g % 2, :, DH:2 * DH],
                                             ALU.add, ALU.max).then_inc(f_done, 1)

                def residual(t):
                    dve.wait_ge(att_done, s * T + t + 1)
                    dve.tensor_tensor(hall[:, bass.ds(s * T + t, 1), :], pa[:].unsqueeze(1),
                                      hcur[:, t % 2].unsqueeze(1), ALU.add).then_inc(hcur_free, 1)

                for t in range(T):
                    n = s * T + t
                    for g in range(0 if t == 0 else 2, GROUPS):
                        features(t, g)
                    dve.wait_ge(vb_ready, 1 + (n + 1) * GROUPS)
                    dve.wait_ge(bv_ready, 1 + n)
                    dve.tensor_scalar(eb[:], eb[:], 1.0, None, ALU.add).then_inc(norm, 1)
                    dve.wait_ge(f_done, 1 + (n + 1) * GROUPS)
                    dve.reduce_sum(nrm[:, 0], qcur[:, t % 2], AX)
                    dve.reduce_sum(nrm[:, 1], kall[:, t], AX).then_inc(norm, 1)
                    dve.wait_ge(norm, 6 * n + 2)
                    dve.reciprocal(beta[:], eb[:]).then_inc(beta_ready, 1)
                    dve.reciprocal(rq[:], nrm[:, 0]).then_inc(norm, 1)
                    dve.reciprocal(rk[:, t], nrm[:, 1]).then_inc(norm, 1)
                    dve.wait_ge(norm, 6 * n + 4)
                    dve.wait_ge(beta_ready, n + 1)
                    dve.tensor_scalar(rq[:], rq[:], FAST_SCALE, None, ALU.mult).then_inc(norm, 1)
                    dve.scalar_tensor_tensor(nbk[:], beta[:], -1.0, rk[:, t], ALU.mult, ALU.mult) \
                        .then_inc(norm, 1)
                    if t:
                        residual(t - 1)
                        k0 = (s * (T - 1) + t - 1) * 5
                        dve.tensor_tensor(prod[:, 0:t], kall[:, 0:t],
                                          kall[:, t].unsqueeze(1).to_broadcast([P, t, NH, DH]),
                                          ALU.mult).then_inc(kk, 1)
                        dve.wait_ge(kk, k0 + 1)
                        dve.reduce_sum(ck[:, 0:t], prod[:, 0:t], AX).then_inc(kk, 1)
                        dve.wait_ge(kk, k0 + 2)
                        dve.tensor_tensor(ck[:, 0:t], ck[:, 0:t], rk[:, 0:t], ALU.mult).then_inc(kk, 1)
                        dve.wait_ge(kk, k0 + 3)
                        dve.wait_ge(norm, 6 * n + 6)
                        dve.tensor_tensor(ck[:, 0:t], ck[:, 0:t],
                                          nbk[:].unsqueeze(1).to_broadcast([P, t, NH]),
                                          ALU.mult).then_inc(kk, 1)
                        dve.wait_ge(kk, k0 + 4)
                        dve.tensor_tensor(prod[:, 0:t], dall[:, 0:t],
                                          ck[:, 0:t].unsqueeze(3).to_broadcast([P, t, NH, DH]),
                                          ALU.mult).then_inc(kk, 1)
                        dve.wait_ge(kk, k0 + 5)
                        dve.wait_ge(bv_ready, 1 + n + 1)
                        dve.reduce_sum(dall[:, t].rearrange("p h c -> p (h c)"),
                                       prod[:, 0:t + 1].rearrange("p s h c -> p (h c) s"),
                                       AX).then_inc(delta_ready, 1)
                    else:
                        dve.wait_ge(norm, 6 * n + 6)
                        dve.wait_ge(bv_ready, 1 + n + 1)
                        dve.sem_inc(delta_ready, 1)
                    dve.wait_ge(delta_ready, n + 1)
                    if t < T - 1:
                        features(t + 1, 0)
                        features(t + 1, 1)
                    dve.wait_ge(qk_mul, n + 1)
                    dve.reduce_sum(cq[:, t % 2, 0:t + 1], prodp[:, 0:t + 1], AX).then_inc(cq_step, 1)
                    dve.wait_ge(cq_step, 2 * n + 1)
                    dve.tensor_tensor(cq[:, t % 2, 0:t + 1], cq[:, t % 2, 0:t + 1], rk[:, 0:t + 1],
                                      ALU.mult).then_inc(cq_step, 1)
                    dve.wait_ge(cq_step, 2 * n + 2)
                    dve.tensor_tensor(cq[:, t % 2, 0:t + 1], cq[:, t % 2, 0:t + 1],
                                      rq[:].unsqueeze(1).to_broadcast([P, t + 1, NH]),
                                      ALU.mult).then_inc(cq_ready, 1)
                residual(T - 1)


def cross_inputs_block(nc, x, ctx_in, ln_g, ln_b, bout, ident, hall, zT, cT0, cT1):
    with ExitStack() as ctx:
        def sb(name, shape, dt=F32):
            return ctx.enter_context(nc.sbuf_tensor(name, shape, dt))

        def sem(name):
            return ctx.enter_context(nc.semaphore(name))

        xres = sb("ci_x", [P, TILES, D])
        z = sb("ci_z", [P, TILES, D])
        cnat = sb("ci_ctx", [P, JT, CD])
        gam = sb("ci_gamma", [P, D])
        bet = sb("ci_beta", [P, D])
        bo = sb("ci_bout", [P, D])
        st = sb("ci_st", [P, TILES, 6])
        mv = sb("ci_mv", [P, TILES, 2])
        ve = sb("ci_ve", [P, 2, TILES])
        rstd = sb("ci_rstd", [P, 2, TILES])
        tmp = sb("ci_tmp", [P, TILES])
        tp = [ctx.enter_context(nc.psum_tensor(f"ci_tp{i}", [P, 512], F32)) for i in range(4)]

        x_in, c_in, v_in = sem("ci_x_in"), sem("ci_c_in"), sem("ci_v_in")
        xb_ready = sem("ci_xb")
        ln = sem("ci_ln")
        var_ready, sd_ready = sem("ci_var"), sem("ci_sd")
        z_ready = sem("ci_z_ready")
        x1_ready = sem("ci_x1")
        tp_full, tp_copied = sem("ci_full"), sem("ci_copied")
        bout_added = sem("ci_bout_added")
        xs = x.rearrange("t (s p) d -> s p t d", p=P)
        CTX_BANKS = 2 * JT // 4
        Z_BANKS = DC * TILES // 4
        block = ctx.enter_context(nc.Block())

        @block.sync
        def _(sp):
            sp.dma_start(cnat[:], ctx_in.rearrange("a b c -> (a b) c").rearrange("(m p) c -> p m c", p=P)) \
                .then_inc(c_in, 16)
            for s in range(HALVES):
                sp.dma_start(xres[:, s * T:(s + 1) * T, :], xs[s]).then_inc(x_in, 16)
            for dst, src in ((gam, ln_g), (bet, ln_b), (bo, bout)):
                sp.dma_start(dst[:], src.unsqueeze(0).to_broadcast([P, D])).then_inc(v_in, 16)

        @block.gpsimd
        def _(pool):
            pool.wait_ge(x_in, 32)
            pool.wait_ge(v_in, 48)
            pool.tensor_tensor(xres[:], xres[:], bet[:].unsqueeze(1).to_broadcast([P, TILES, D]),
                               ALU.add).then_inc(xb_ready, 1)
            pool.wait_ge(z_ready, 1)
            pool.tensor_tensor(hall[:], hall[:], bo[:].unsqueeze(1).to_broadcast([P, TILES, D]),
                               ALU.add).then_inc(bout_added, 1)

        @block.vector
        def _(dve):
            base = 0
            for stage in range(2):
                for m in range(TILES):
                    dve.bn_stats(st[:, m], hall[:, m]).then_inc(ln, 1)
                for m in range(TILES):
                    dve.wait_ge(ln, base + TILES + m)
                    dve.bn_aggr(mv[:, m], st[:, m]).then_inc(ln, 1)
                dve.wait_ge(ln, base + 2 * TILES)
                dve.tensor_scalar(ve[:, stage], mv[:, :, 1], EPS, None, ALU.add).then_inc(var_ready, 1)
                dve.wait_ge(sd_ready, stage + 1)
                dve.reciprocal(rstd[:, stage], rstd[:, stage]).then_inc(ln, 1)
                dve.wait_ge(ln, base + 2 * TILES + 1)
                newton_rsqrt(dve, ve[:, stage], rstd[:, stage], tmp[:], ln, base + 2 * TILES + 1)
                base += 2 * TILES + 5
                dst = hall if stage == 0 else z
                for m in range(TILES):
                    last = dve.tensor_scalar(dst[:, m], hall[:, m], mv[:, m, 0:1], rstd[:, stage, m:m + 1],
                                             ALU.subtract, ALU.mult)
                if stage == 0:
                    last.then_inc(x1_ready, 1)
                    dve.wait_ge(x1_ready, 1)
                    dve.wait_ge(v_in, 48)
                    dve.tensor_tensor(hall[:], hall[:], gam[:].unsqueeze(1).to_broadcast([P, TILES, D]),
                                      ALU.mult).then_inc(x1_ready, 1)
                    dve.wait_ge(x1_ready, 2)
                    dve.wait_ge(xb_ready, 1)
                    dve.tensor_tensor(hall[:], hall[:], xres[:], ALU.add).then_inc(x1_ready, 1)
                    dve.wait_ge(x1_ready, 3)
                else:
                    last.then_inc(z_ready, 1)

        @block.tensor
        def _(pe):
            pe.wait_ge(c_in, 16)
            for n in range(CTX_BANKS + Z_BANKS):
                if n == CTX_BANKS:
                    pe.wait_ge(z_ready, 1)
                if n >= 4:
                    pe.wait_ge(tp_copied, n - 3)
                for k in range(4):
                    if n < CTX_BANKS:
                        c, m = n // (JT // 4), n % (JT // 4) * 4 + k
                        w = P if c == 0 else C2
                        src = cnat[:, m, c * P:c * P + w]
                    else:
                        c, m = (n - CTX_BANKS) // (TILES // 4), (n - CTX_BANKS) % (TILES // 4) * 4 + k
                        w = P
                        src = z[:, m, c * P:(c + 1) * P]
                    last = pe.transpose(tp[n % 4][0:w, k * P:(k + 1) * P], src, ident[:])
                last.then_inc(tp_full, 1)

        @block.scalar
        def _(act):
            for stage in range(2):
                act.wait_ge(var_ready, stage + 1)
                act.activation(rstd[:, stage], ve[:, stage], ACT.Sqrt).then_inc(sd_ready, 1)
            for n in range(CTX_BANKS + Z_BANKS):
                q = n % 4 * 512
                act.wait_ge(tp_full, n + 1)
                if n < JT // 4:
                    act.activation(cT0[:, q:q + 512], tp[n % 4][:], ACT.Copy).then_inc(tp_copied, 1)
                elif n < CTX_BANKS:
                    act.activation(cT1[:, q:q + 512], tp[n % 4][0:C2, :], ACT.Copy).then_inc(tp_copied, 1)
                else:
                    act.activation(zT[:, (n - CTX_BANKS) // 4, q:q + 512], tp[n % 4][:], ACT.Copy) \
                        .then_inc(tp_copied, 1)


def cross_attention_block(nc, w_q, w_k, w_v, w_out, ident, hall, zT, cT0, cT1):
    with ExitStack() as ctx:
        def sb(name, shape, dt=F32):
            return ctx.enter_context(nc.sbuf_tensor(name, shape, dt))

        def sem(name):
            return ctx.enter_context(nc.semaphore(name))

        HI, LO = 0, 1
        wqh = sb("xa_wq", [P, DC, XD])
        wk0, wk1 = sb("xa_wk0", [P, XD]), sb("xa_wk1", [C2, XD])
        wv0, wv1 = sb("xa_wv0", [P, XD]), sb("xa_wv1", [C2, XD])
        woh = sb("xa_wout", [P, D])
        qT = [sb(f"xa_qT{i}", [P, TOK], F32R) for i in (HI, LO)]
        kT = [sb(f"xa_kT{i}", [P, TOK], F32R) for i in (HI, LO)]
        v = [sb(f"xa_v{i}", [P, TOK], F32R) for i in (HI, LO)]
        probs = sb("xa_probs", [P, 2, TOK])
        pT = [sb(f"xa_pT{i}", [P, 2, JT, 2 * P], F32R) for i in (HI, LO)]
        oT = sb("xa_oT", [P, 2 * P])
        mx = sb("xa_mx", [P, 2])
        nb = sb("xa_nb", [P, 2])
        rs = sb("xa_rs", [P, TILES, 2])
        rinv = sb("xa_rinv", [P, TILES])

        S = ctx.enter_context(nc.psum_tensor("xa_S", [P, 4, 512], F32))
        tb = [ctx.enter_context(nc.psum_tensor(f"xa_tb{i}", [P, 512], F32)) for i in range(2)]
        O = ctx.enter_context(nc.psum_tensor("xa_O", [P, 2 * P], F32))
        Y = ctx.enter_context(nc.psum_tensor("xa_Y", [P, 2, D], F32))

        w_in, wo_in = sem("xa_w_in"), sem("xa_wo_in")
        proj_mm, proj_hi, proj_lo = sem("xa_proj_mm"), sem("xa_proj_hi"), sem("xa_proj_lo")
        sim_done = sem("xa_sim")
        mx_ready = sem("xa_mx_ready")
        nb_ready = sem("xa_nb_ready")
        exp_done = sem("xa_exp")
        t_mm = sem("xa_t_mm")
        hi_ready, lo_ready = sem("xa_hi"), sem("xa_lo")
        av_done = sem("xa_av")
        oT_ready = sem("xa_oT_ready")
        y_mm, y_used = sem("xa_y_mm"), sem("xa_y_used")
        r_step = sem("xa_r_step")

        UNITS = 12
        PAIRS = TILES // 2
        STEPS = TILES + 4
        block = ctx.enter_context(nc.Block())

        @block.sync
        def _(sp):
            with sp.Fori(0, XH) as h:
                cols = bass.ds(h * XD, XD)
                sp.wait_ge(proj_mm, 1 + h * UNITS)
                sp.dma_start(wqh[:], w_q.rearrange("(c p) n -> p c n", p=P)[:, :, cols]).then_inc(w_in, 16)
                sp.dma_start(wk0[:], w_k[0:P, cols]).then_inc(w_in, 16)
                sp.dma_start(wk1[:], w_k[P:CD, cols]).then_inc(w_in, 16)
                sp.dma_start(wv0[:], w_v[0:P, cols]).then_inc(w_in, 16)
                sp.dma_start(wv1[:], w_v[P:CD, cols]).then_inc(w_in, 16)
                sp.wait_ge(y_mm, 1 + h * PAIRS)
                sp.dma_start(woh[:], w_out[cols, :]).then_inc(wo_in, 16)

        @block.tensor
        def _(pe):
            pe.sem_inc(proj_mm, 1)
            pe.sem_inc(y_mm, 1)
            with pe.Fori(0, XH) as h:
                def project():
                    pe.wait_ge(w_in, h * 80 + 80)
                    pe.wait_ge(exp_done, 1 + h * 2 * TILES)
                    for u in range(UNITS):
                        if u >= 4:
                            pe.wait_ge(proj_lo, h * UNITS + u - 3)
                        blk = slice(u % 4 * 512, u % 4 * 512 + 512)
                        if u < 4:
                            for c in range(DC):
                                last = pe.matmul(S[:, u % 4], wqh[:, c], zT[:, c, blk], start=(c == 0), stop=(c == DC - 1))
                        elif u < 8:
                            pe.matmul(S[:, u % 4], wk0[:], cT0[:, blk], start=True, stop=False)
                            last = pe.matmul(S[:, u % 4], wk1[:], cT1[:, blk], start=False, stop=True)
                        else:
                            for k in range(4):
                                j = slice(u % 4 * 512 + k * P, u % 4 * 512 + (k + 1) * P)
                                pe.matmul(S[:, u % 4, k * P:(k + 1) * P], cT0[:, j], wv0[:], start=True, stop=False)
                                last = pe.matmul(S[:, u % 4, k * P:(k + 1) * P], cT1[:, j], wv1[:], start=False, stop=True)
                        last.then_inc(proj_mm, 1)

                def scores(i):
                    q = slice(i * P, (i + 1) * P)
                    for u in range(2):
                        if i:
                            pe.wait_ge(exp_done, 1 + h * 2 * TILES + 2 * i - 1 + u)
                        for n, (a, b) in enumerate(((HI, HI), (HI, LO), (LO, HI))):
                            for k in (2 * u, 2 * u + 1):
                                last = pe.matmul(S[:, k], qT[a][:, q], kT[b][:, k * 512:(k + 1) * 512],
                                                 start=(n == 0), stop=(n == 2))
                        last.then_inc(sim_done, 1)

                def transposes(i, q):
                    if q % 2 == 0:
                        pe.wait_ge(exp_done, 1 + h * 2 * TILES + 2 * i + q // 2 + 1)
                    if i or q >= 2:
                        pe.wait_ge(lo_ready, h * 4 * TILES + 4 * i + q - 1)
                    for k in range(4):
                        j = (4 * q + k) * P
                        last = pe.transpose(tb[q % 2][:, k * P:(k + 1) * P], probs[:, i % 2, j:j + P], ident[:])
                    last.then_inc(t_mm, 1)

                def weighted(p, half):
                    if half == 0:
                        pe.wait_ge(lo_ready, h * 4 * TILES + 8 * (p + 1))
                        pe.wait_ge(oT_ready, 1 + h * PAIRS + p)
                    for j in range(half * JT // 2, (half + 1) * JT // 2):
                        vj = slice(j * P, (j + 1) * P)
                        for n, (a, b) in enumerate(((HI, HI), (HI, LO), (LO, HI))):
                            last = pe.matmul(O[:], v[a][:, vj], pT[b][:, p % 2, j],
                                             start=(j == 0 and n == 0), stop=(j == JT - 1 and n == 2))
                    if half:
                        last.then_inc(av_done, 1)

                def out_project(p):
                    if p == 0:
                        pe.wait_ge(wo_in, h * 16 + 16)
                    pe.wait_ge(oT_ready, 1 + h * PAIRS + p + 1)
                    pe.wait_ge(y_used, 1 + h * PAIRS + p)
                    for k in range(2):
                        last = pe.matmul(Y[:, k], oT[:, k * P:(k + 1) * P], woh[:], start=True, stop=True)
                    last.then_inc(y_mm, 1)

                project()
                pe.wait_ge(proj_lo, h * UNITS + UNITS)
                for i in range(STEPS):
                    if i < TILES:
                        scores(i)
                    if 1 <= i <= TILES:
                        transposes(i - 1, 0)
                        transposes(i - 1, 1)
                    if 3 <= i < 3 + TILES:
                        weighted((i - 3) // 2, (i - 3) % 2)
                    if 1 <= i <= TILES:
                        transposes(i - 1, 2)
                        transposes(i - 1, 3)
                    if i >= 5 and i % 2:
                        out_project((i - 5) // 2)

        @block.scalar
        def _(act):
            act.sem_inc(exp_done, 1)
            act.sem_inc(oT_ready, 1)
            with act.Fori(0, XH) as h:
                def high_part(i, q):
                    act.wait_ge(t_mm, h * 4 * TILES + 4 * i + q + 1)
                    act.activation(pT[HI][:, i // 2 % 2, 4 * q:4 * q + 4, i % 2 * P:(i % 2 + 1) * P],
                                   tb[q % 2][:].rearrange("p (k n) -> p k n", k=4), ACT.Copy).then_inc(hi_ready, 1)

                for u in range(UNITS):
                    dst = (qT, kT, v)[u // 4][HI]
                    act.wait_ge(proj_mm, 1 + h * UNITS + u + 1)
                    act.activation(dst[:, u % 4 * 512:u % 4 * 512 + 512], S[:, u % 4], ACT.Copy).then_inc(proj_hi, 1)
                for i in range(STEPS):
                    if 1 <= i <= TILES:
                        high_part(i - 1, 0)
                        high_part(i - 1, 1)
                    if i < TILES:
                        act.wait_ge(nb_ready, h * TILES + i + 1)
                        if i >= 2:
                            act.wait_ge(t_mm, h * 4 * TILES + 4 * (i - 1))
                        for u in range(2):
                            act.activation(probs[:, i % 2, u * 1024:(u + 1) * 1024], S[:, 2 * u:2 * u + 2].rearrange("p a b -> p (a b)"),
                                           ACT.Exp, bias=nb[:, i % 2:i % 2 + 1], scale=SOFT_SCALE,
                                           accum_out=rs[:, i, u:u + 1]).then_inc(exp_done, 1)
                    if 1 <= i <= TILES:
                        high_part(i - 1, 2)
                        high_part(i - 1, 3)
                    if i >= 4 and i % 2 == 0:
                        p = (i - 4) // 2
                        act.wait_ge(av_done, h * PAIRS + p + 1)
                        act.wait_ge(y_mm, 1 + h * PAIRS + p)
                        act.activation(oT[:], O[:], ACT.Copy).then_inc(oT_ready, 1)

        @block.vector
        def _(dve):
            dve.sem_inc(y_used, 1)
            with dve.Fori(0, XH) as h:
                def low_part(i, q):
                    dst = (slice(None), i // 2 % 2, slice(4 * q, 4 * q + 4), slice(i % 2 * P, (i % 2 + 1) * P))
                    dve.wait_ge(hi_ready, h * 4 * TILES + 4 * i + q + 1)
                    dve.tensor_tensor(pT[LO][dst], tb[q % 2][:].rearrange("p (k n) -> p k n", k=4),
                                      pT[HI][dst].bitcast(F32), ALU.subtract).then_inc(lo_ready, 1)

                for u in range(UNITS):
                    dst = (qT, kT, v)[u // 4]
                    blk = slice(u % 4 * 512, u % 4 * 512 + 512)
                    dve.wait_ge(proj_hi, h * UNITS + u + 1)
                    dve.tensor_tensor(dst[LO][:, blk], S[:, u % 4], dst[HI][:, blk].bitcast(F32),
                                      ALU.subtract).then_inc(proj_lo, 1)
                for i in range(STEPS):
                    if i < TILES:
                        for u in range(2):
                            dve.wait_ge(sim_done, h * 2 * TILES + 2 * i + u + 1)
                            dve.reduce_max(mx[:, u:u + 1], S[:, 2 * u:2 * u + 2].rearrange("p a b -> p (a b)"),
                                           AX).then_inc(mx_ready, 1)
                        dve.wait_ge(mx_ready, h * 2 * TILES + 2 * i + 2)
                        dve.tensor_scalar(nb[:, i % 2:i % 2 + 1], mx[:, 0:1], mx[:, 1:2], -SOFT_SCALE,
                                          ALU.max, ALU.mult).then_inc(nb_ready, 1)
                    if 1 <= i <= TILES:
                        low_part(i - 1, 0)
                        low_part(i - 1, 1)
                        low_part(i - 1, 2)
                        low_part(i - 1, 3)
                    if i >= 5 and i % 2:
                        p = (i - 5) // 2
                        r0 = h * 2 * PAIRS + 2 * p
                        two = slice(2 * p, 2 * p + 2)
                        dve.wait_ge(exp_done, 1 + h * 2 * TILES + 4 * p + 4)
                        dve.tensor_tensor(rinv[:, two], rs[:, two, 0], rs[:, two, 1], ALU.add).then_inc(r_step, 1)
                        dve.wait_ge(r_step, r0 + 1)
                        dve.reciprocal(rinv[:, two], rinv[:, two]).then_inc(r_step, 1)
                        dve.wait_ge(r_step, r0 + 2)
                        dve.wait_ge(y_mm, 1 + h * PAIRS + p + 1)
                        for k in range(2):
                            m = 2 * p + k
                            last = dve.scalar_tensor_tensor(hall[:, m], Y[:, k], rinv[:, m:m + 1], hall[:, m],
                                                            ALU.mult, ALU.add)
                        last.then_inc(y_used, 1)


def expert_block(nc, r_w, w1, w2, out, ident, hall, xe, ye):
    with ExitStack() as ctx:
        def sb(name, shape, dt=F32):
            return ctx.enter_context(nc.sbuf_tensor(name, shape, dt))

        def pb(name, shape):
            return ctx.enter_context(nc.psum_tensor(name, shape, F32))

        def sem(name):
            return ctx.enter_context(nc.semaphore(name))

        FLAT = [s * T + t for t in range(T) for s in range(HALVES)]
        z = sb("ex_z", [P, TILES, D])
        yg = sb("ex_yg", [P, TILES, D])
        zero = sb("ex_zero", [P, 4 * D])
        zt = sb("ex_zt", [P, 4, 4, P])
        rw = sb("ex_rw", [P, DC, E])
        lg = sb("ex_lg", [P, TILES, E])
        ex = sb("ex_ex", [P, TILES, E])
        oh = sb("ex_oh", [P, TILES, E])
        pre = sb("ex_pre", [P, TILES, E])
        rank = sb("ex_rank", [P, E])
        mx = sb("ex_mx", [P, TILES])
        top = sb("ex_top", [P, TILES])
        gate = sb("ex_gate", [P, TILES])
        pos = sb("ex_pos", [P, TILES])
        slot = sb("ex_slot", [P, TILES])
        sloti = sb("ex_sloti", [P, TILES], I32)
        ones = sb("ex_ones", [P, P])
        before = sb("ex_before", [P, P])
        st = sb("ex_st", [P, TILES, 6])
        mv = sb("ex_mv", [P, TILES, 2])
        ve = sb("ex_ve", [P, TILES])
        rstd = sb("ex_rstd", [P, TILES])
        tmp = sb("ex_tmp", [P, TILES])
        w1b = [sb(f"ex_w1_{i}", [P, DC, F]) for i in range(2)]
        w2b = [sb(f"ex_w2_{i}", [P, FC, D]) for i in range(2)]
        xn = [sb(f"ex_xn{i}", [P, CT, D]) for i in range(2)]
        xT = [sb(f"ex_xT{i}", [P, DC, CAP]) for i in range(2)]
        hid = [sb(f"ex_hid{i}", [P, FC, CAP]) for i in range(2)]
        yb = [sb(f"ex_yb{i}", [P, CT, D]) for i in range(2)]

        tp = [pb(f"ex_tp{i}", [P, 512]) for i in range(2)]
        H = [pb(f"ex_H{i}", [P, 2, CAP]) for i in range(FC // 2)]
        Yp = [pb(f"ex_Y{i}", [P, CT, D]) for i in range(2)]
        rp = Yp[0][:, 0, 0:TILES * E]

        zero_set, zero_out = sem("ex_zero_set"), sem("ex_zero_out")
        consts = sem("ex_consts")
        rw_in = sem("ex_rw_in")
        ln, var_ready, sd_ready = sem("ex_ln"), sem("ex_var"), sem("ex_sd")
        z_ready = sem("ex_z_ready")
        ztp, zt_ready = sem("ex_ztp"), sem("ex_zt_ready")
        logits = sem("ex_logits")
        shifted, expd = sem("ex_shifted"), sem("ex_expd")
        rt = sem("ex_rt")
        oh_ready, pos_mm, slot_ready = sem("ex_oh_ready"), sem("ex_pos_mm"), sem("ex_slot_ready")
        yg_zero = sem("ex_yg_zero")
        scattered = sem("ex_scattered")
        w_in = [sem(f"ex_w_in{i}") for i in range(2)]
        x_in = [sem(f"ex_x_in{i}") for i in range(2)]
        xtp, xT_ready = sem("ex_xtp"), sem("ex_xT_ready")
        h_mm, gelu = sem("ex_h_mm"), sem("ex_gelu")
        y_mm = [sem(f"ex_y_mm{i}") for i in range(2)]
        y_copied = [sem(f"ex_y_copied{i}") for i in range(2)]
        y_out = [sem(f"ex_y_out{i}") for i in range(2)]
        yb_free = [sem(f"ex_yb_free{i}") for i in range(2)]
        gathered = [sem(f"ex_gath{m}") for m in range(TILES)]
        added, stored = sem("ex_added"), sem("ex_stored")

        HU = FC // 2
        block = ctx.enter_context(nc.Block())

        @block.sync
        def _(sp):
            sp.wait_ge(zero_set, 1)
            sp.dma_start(xe.rearrange("(p r) d -> p (r d)", r=4 * 4)[:, 0:4 * D], zero[:]).then_inc(zero_out, 16)
            for k in range(1, 4):
                sp.dma_start(xe.rearrange("(p r) d -> p (r d)", r=4 * 4)[:, k * 4 * D:(k + 1) * 4 * D], zero[:]) \
                    .then_inc(zero_out, 16)
            sp.dma_start(rw[:], r_w.rearrange("(c p) e -> p c e", p=P)).then_inc(rw_in, 16)
            with sp.Fori(0, E // 2) as ep:
                for i in range(2):
                    e = ep * 2 + i
                    sp.wait_ge(y_mm[i], 1 + ep)
                    sp.dma_start(w1b[i][:], w1[bass.ds(e, 1)].rearrange("e (c p) f -> p (e c) f", p=P)) \
                        .then_inc(w_in[i], 16)
                    sp.dma_start(w2b[i][:], w2[bass.ds(e, 1)].rearrange("e (c p) d -> p (e c) d", p=P)) \
                        .then_inc(w_in[i], 16)
                sp.wait_ge(scattered, 16 * TILES)
                for i in range(2):
                    sp.dma_start(xn[i][:], xe[bass.ds((ep * 2 + i) * CAP, CAP)].rearrange("(k p) d -> p k d", p=P)) \
                        .then_inc(x_in[i], 16)

        @block.gpsimd
        def _(pool):
            pool.memset(zero[:], 0.0).then_inc(zero_set, 1)
            pool.memset(ones[:], 1.0).then_inc(consts, 1)
            pool.wait_ge(consts, 1)
            pool.affine_select(out=before[:], in_=ones[:], compare_op=ALU.is_gt, fill=0.0, base=0,
                               pattern=[[1, P]], channel_multiplier=-1).then_inc(consts, 1)
            for e in range(E):
                last = pool.memset(rank[:, e:e + 1], float(E - e))
            last.then_inc(consts, 1)
            pool.memset(yg[:], 0.0).then_inc(yg_zero, 1)
            pool.wait_ge(zero_out, 64)
            pool.wait_ge(slot_ready, 1)
            pool.wait_ge(z_ready, 1)
            for m in range(TILES):
                pool.indirect_dma_start(xe, bass.IndirectOffsetOnAxis(sloti[:, m:m + 1], 0), z[:, m], None,
                                        bounds_check=E * CAP - 1, oob_is_err=False).then_inc(scattered, 16)
            for i in range(2):
                pool.sem_inc(yb_free[i], 1)
            with pool.Fori(0, E // 2) as ep:
                for i in range(2):
                    pool.wait_ge(y_copied[i], 1 + ep + 1)
                    pool.dma_start(ye[bass.ds((ep * 2 + i) * CAP, CAP)].rearrange("(k p) d -> p k d", p=P), yb[i][:]) \
                        .then_inc(y_out[i], 16)
                    pool.wait_ge(y_out[i], 16 * ep + 16)
                    pool.sem_inc(yb_free[i], 1)
            pool.wait_ge(yg_zero, 1)
            for m in range(TILES):
                pool.indirect_dma_start(yg[:, m], None, ye, bass.IndirectOffsetOnAxis(sloti[:, m:m + 1], 0),
                                        bounds_check=E * CAP - 1, oob_is_err=False).then_inc(gathered[m], 16)

        @block.vector
        def _(dve):
            for m in range(TILES):
                dve.bn_stats(st[:, m], hall[:, m]).then_inc(ln, 1)
            for m in range(TILES):
                dve.wait_ge(ln, TILES + m)
                dve.bn_aggr(mv[:, m], st[:, m]).then_inc(ln, 1)
            dve.wait_ge(ln, 2 * TILES)
            dve.tensor_scalar(ve[:], mv[:, :, 1], EPS, None, ALU.add).then_inc(var_ready, 1)
            dve.wait_ge(sd_ready, 1)
            dve.reciprocal(rstd[:], rstd[:]).then_inc(ln, 1)
            dve.wait_ge(ln, 2 * TILES + 1)
            newton_rsqrt(dve, ve[:], rstd[:], tmp[:], ln, 2 * TILES + 1)
            for m in range(TILES):
                last = dve.tensor_scalar(z[:, m], hall[:, m], mv[:, m, 0:1], rstd[:, m:m + 1],
                                         ALU.subtract, ALU.mult)
            last.then_inc(z_ready, 1)
            for n in range(DC * TILES // 4):
                dve.wait_ge(ztp, n + 1)
                if n >= 4:
                    dve.wait_ge(logits, 2 * ((n - 4) // 2 + 1))
                dve.tensor_copy(zt[:, n % 4], tp[n % 2][:].rearrange("p (k n) -> p k n", k=4)).then_inc(zt_ready, 1)

            def wide(a):
                return a.unsqueeze(2).to_broadcast([P, TILES, E])

            dve.wait_ge(logits, TILES // 2)
            dve.tensor_copy(lg[:].rearrange("p m e -> p (m e)"), rp).then_inc(rt, 1)
            dve.wait_ge(rt, 1)
            dve.reduce_max(mx[:], lg[:], AX).then_inc(rt, 1)
            dve.wait_ge(rt, 2)
            dve.tensor_tensor(ex[:], lg[:], wide(mx[:]), ALU.subtract).then_inc(shifted, 1)
            dve.tensor_tensor(oh[:], lg[:], wide(mx[:]), ALU.is_equal).then_inc(rt, 1)
            dve.wait_ge(rt, 3)
            dve.wait_ge(consts, 3)
            dve.tensor_tensor(oh[:], oh[:], rank[:].unsqueeze(1).to_broadcast([P, TILES, E]), ALU.mult).then_inc(rt, 1)
            dve.wait_ge(rt, 4)
            dve.reduce_max(top[:], oh[:], AX).then_inc(rt, 1)
            dve.wait_ge(rt, 5)
            dve.tensor_tensor(oh[:], oh[:], wide(top[:]), ALU.is_equal).then_inc(oh_ready, 1)
            dve.memset(pre[:, FLAT[0]], 0.0).then_inc(rt, 1)
            dve.wait_ge(oh_ready, 1)
            for n in range(1, TILES):
                dve.wait_ge(rt, 5 + n)
                dve.tensor_tensor(pre[:, FLAT[n]], pre[:, FLAT[n - 1]], oh[:, FLAT[n - 1]], ALU.add).then_inc(rt, 1)
            done = 5 + TILES
            dve.wait_ge(expd, 1)
            dve.reduce_sum(gate[:], ex[:], AX).then_inc(rt, 1)
            dve.wait_ge(rt, done + 1)
            dve.reciprocal(gate[:], gate[:]).then_inc(rt, 1)
            dve.wait_ge(pos_mm, 1)
            dve.wait_ge(rt, done + 2)
            dve.tensor_tensor(lg[:].rearrange("p m e -> p (m e)"), rp, oh[:].rearrange("p m e -> p (m e)"),
                              ALU.mult).then_inc(rt, 1)
            dve.wait_ge(rt, done + 3)
            dve.reduce_sum(pos[:], lg[:], AX).then_inc(rt, 1)
            dve.wait_ge(rt, done + 4)
            dve.tensor_scalar(slot[:], pos[:], float(CAP), float(2 * E * CAP), ALU.is_ge, ALU.mult).then_inc(rt, 1)
            dve.tensor_scalar(top[:], top[:], -float(CAP), float(E * CAP), ALU.mult, ALU.add).then_inc(rt, 1)
            dve.wait_ge(rt, done + 6)
            dve.tensor_tensor(slot[:], slot[:], pos[:], ALU.add).then_inc(rt, 1)
            dve.wait_ge(rt, done + 7)
            dve.tensor_tensor(slot[:], slot[:], top[:], ALU.add).then_inc(rt, 1)
            dve.wait_ge(rt, done + 8)
            dve.tensor_copy(sloti[:], slot[:]).then_inc(slot_ready, 1)
            for i in range(2):
                dve.sem_inc(y_copied[i], 1)
            with dve.Fori(0, E // 2) as ep:
                for i in range(2):
                    e = ep * 2 + i
                    for c in range(DC):
                        dve.wait_ge(xtp, e * DC + c + 1)
                        dve.tensor_copy(xT[i][:, c], tp[c][:, 0:CAP]).then_inc(xT_ready, 1)
                    dve.wait_ge(y_mm[i], 1 + ep + 1)
                    dve.wait_ge(yb_free[i], 1 + ep)
                    dve.tensor_copy(yb[i][:], Yp[i][:]).then_inc(y_copied[i], 1)
            for m in range(TILES):
                dve.wait_ge(gathered[m], 16)
                dve.scalar_tensor_tensor(yg[:, m], yg[:, m], gate[:, m:m + 1], hall[:, m],
                                         ALU.mult, ALU.add).then_inc(added, 1)

        @block.scalar
        def _(act):
            act.wait_ge(var_ready, 1)
            act.activation(rstd[:], ve[:], ACT.Sqrt).then_inc(sd_ready, 1)
            act.wait_ge(shifted, 1)
            act.activation(ex[:], ex[:], ACT.Exp).then_inc(expd, 1)
            with act.Fori(0, E // 2) as ep:
                for i in range(2):
                    act.wait_ge(y_mm[i], 1 + ep)
                    for u in range(HU):
                        act.wait_ge(h_mm, (ep * 2 + i) * HU + u + 1)
                        act.activation(hid[i][:, 2 * u:2 * u + 2], H[u][:], ACT.Gelu_apprx_tanh).then_inc(gelu, 1)
            xo = out.rearrange("t (s p) d -> s t p d", p=P)
            for m in range(TILES):
                act.wait_ge(added, m + 1)
                act.dma_start(xo[m // T, m % T], yg[:, m]).then_inc(stored, 16)
            act.wait_ge(stored, 16 * TILES)

        @block.tensor
        def _(pe):
            pe.wait_ge(z_ready, 1)
            pe.wait_ge(rw_in, 16)
            for q in range(TILES // 4):
                for c in range(DC):
                    n = q * DC + c
                    if n >= 2:
                        pe.wait_ge(zt_ready, n - 1)
                    for k in range(4):
                        last = pe.transpose(tp[n % 2][:, k * P:(k + 1) * P], z[:, 4 * q + k, c * P:(c + 1) * P], ident[:])
                    last.then_inc(ztp, 1)
                pe.wait_ge(zt_ready, (q + 1) * DC)
                for k in range(4):
                    m = 4 * q + k
                    for c in range(DC):
                        last = pe.matmul(rp[:, m * E:(m + 1) * E], zt[:, (q * DC + c) % 4, k], rw[:, c],
                                         start=(c == 0), stop=(c == DC - 1))
                    if k % 2:
                        last.then_inc(logits, 1)
            pe.wait_ge(consts, 3)
            pe.wait_ge(oh_ready, 1)
            pe.wait_ge(rt, 5 + TILES)
            pe.matmul(rp, before[:], oh[:].rearrange("p m e -> p (m e)"), start=True, stop=False)
            pe.matmul(rp, ones[:], pre[:].rearrange("p m e -> p (m e)"), start=False, stop=True).then_inc(pos_mm, 1)
            for i in range(2):
                pe.sem_inc(y_mm[i], 1)
            with pe.Fori(0, E // 2) as ep:
                for i in range(2):
                    e = ep * 2 + i
                    pe.wait_ge(x_in[i], ep * 16 + 16)
                    for c in range(DC):
                        for k in range(CT):
                            last = pe.transpose(tp[c][:, k * P:(k + 1) * P], xn[i][:, k, c * P:(c + 1) * P], ident[:])
                        last.then_inc(xtp, 1)
                    pe.wait_ge(w_in[i], ep * 32 + 32)
                    pe.wait_ge(xT_ready, e * DC + DC)
                    for u in range(HU):
                        for k in range(2):
                            f = (2 * u + k) * P
                            for c in range(DC):
                                last = pe.matmul(H[u][:, k], w1b[i][:, c, f:f + P], xT[i][:, c],
                                                 start=(c == 0), stop=(c == DC - 1))
                        last.then_inc(h_mm, 1)
                    pe.wait_ge(y_copied[i], 1 + ep)
                    for f in range(FC):
                        if f % 2 == 0:
                            pe.wait_ge(gelu, e * HU + f // 2 + 1)
                        for k in range(CT):
                            last = pe.matmul(Yp[i][:, k], hid[i][:, f, k * P:(k + 1) * P], w2b[i][:, f],
                                             start=(f == 0 and k == 0), stop=(f == FC - 1), skip_group_check=True)
                    last.then_inc(y_mm[i], 1)


def decoder_kernel(nc, x, context, w_qkvb, w_o, ln_g, ln_b, w_q, w_k, w_v, w_out, b_out, router_w, w1, w2, out):
    xe = nc.dram_tensor("expert_in", [E * CAP, D], F32, kind="Internal").ap()
    ye = nc.dram_tensor("expert_out", [E * CAP, D], F32, kind="Internal").ap()
    with ExitStack() as ctx:
        ident = ctx.enter_context(nc.sbuf_tensor("ident", [P, P], F32))
        hall = ctx.enter_context(nc.sbuf_tensor("hall", [P, TILES, D], F32))
        fast_weight_block(nc, x, w_qkvb, w_o, ident, hall)
        with ExitStack() as cross:
            zT = cross.enter_context(nc.sbuf_tensor("zT", [P, DC, TOK], F32))
            cT0 = cross.enter_context(nc.sbuf_tensor("cT0", [P, TOK], F32))
            cT1 = cross.enter_context(nc.sbuf_tensor("cT1", [C2, TOK], F32))
            cross_inputs_block(nc, x, context, ln_g, ln_b, b_out, ident, hall, zT, cT0, cT1)
            cross_attention_block(nc, w_q, w_k, w_v, w_out, ident, hall, zT, cT0, cT1)
        expert_block(nc, router_w, w1, w2, out, ident, hall, xe, ye)


_INS = ['x', 'ctx_768', 'L0_attn_W_qkvb', 'L0_attn_W_o', 'L0_attn_ln_g', 'L0_attn_ln_b', 'L0_xattn_Wq', 'L0_xattn_Wk',
        'L0_xattn_Wv', 'L0_xattn_Wout', 'L0_xattn_bout', 'L0_ffn_router_w', 'L0_ffn_w1', 'L0_ffn_w2']


def kernel(**inputs):
    import numpy as _np
    import concourse.bacc as _bacc
    from concourse import mybir as _mybir
    from concourse.bass_utils import run_bass_kernel_spmd as _run

    nc = _bacc.Bacc("TRN2", target_bir_lowering=False, num_devices=1)
    arrays, args = {}, []
    for name in _INS:
        a = _np.ascontiguousarray(inputs[name])
        arrays[f"in_{name}_dram"] = a
        args.append(nc.dram_tensor(f"in_{name}_dram", a.shape, _mybir.dt.from_np(a.dtype), kind="ExternalInput").ap())
    args.append(nc.dram_tensor("out_0_dram", (T, B, D), F32, kind="ExternalOutput").ap())
    decoder_kernel(nc, *args)
    r = _run(nc, [arrays], core_ids=[0])
    return r.results[0]["out_0_dram"]
```

```python
from contextlib import ExitStack

import concourse.bass as bass
from concourse import mybir

F32 = mybir.dt.float32
F32R = mybir.dt.float32r
I32 = mybir.dt.int32
ALU = mybir.AluOpType
ACT = mybir.ActivationFunctionType
AX = mybir.AxisListType.X

P = 128
D = 256
DC = D // P
T, B = 8, 256
HALVES = B // P
TILES = T * HALVES
TOK = T * B
EPS = 1e-5

NH, DH = 16, 64
HW = 3 * DH + 1
INNER = NH * DH
FAST_SCALE = 1.0 / 8.0
GH = 4
GROUPS = NH // GH

XH, XD = 8, 128
CD = 192
C2 = CD - P
JT = TOK // P
SOFT_SCALE = 1.5 * XD ** -0.5

HI, LO = 0, 1

E, F = 8, 1024
FC = F // P
CAP = TOK // E
CT = CAP // P


def newton_rsqrt(dve, ve, y, t, done, base):
    dve.tensor_tensor(t, y, y, ALU.mult).then_inc(done, 1)
    dve.wait_ge(done, base + 1)
    dve.tensor_tensor(t, t, ve, ALU.mult).then_inc(done, 1)
    dve.wait_ge(done, base + 2)
    dve.tensor_scalar(t, t, -0.5, 1.5, ALU.mult, ALU.add).then_inc(done, 1)
    dve.wait_ge(done, base + 3)
    dve.tensor_tensor(y, y, t, ALU.mult).then_inc(done, 1)
    dve.wait_ge(done, base + 4)


def fast_weight_block(nc, x, w_qkvb, w_o, ident, hall):
    with ExitStack() as ctx:
        def sb(name, shape, dt=F32):
            return ctx.enter_context(nc.sbuf_tensor(name, shape, dt))

        def pb(name, shape):
            return ctx.enter_context(nc.psum_tensor(name, shape, F32))

        def sem(name):
            return ctx.enter_context(nc.semaphore(name))

        HB = 4
        wq = sb("fw_wqkvb", [P, DC, NH * HW])
        wo = sb("fw_wo", [P, INNER // P, D])
        hcur = sb("fw_hcur", [P, HB, D])
        hT = sb("fw_hT", [P, 2, DC, P])
        ebuf = sb("fw_ebuf", [P, 2, GH, 2 * DH])
        vbuf = sb("fw_vbuf", [P, NH, DH])
        qcur = sb("fw_qcur", [P, 2, NH, DH])
        kall = sb("fw_kall", [P, T, NH, DH])
        dall = sb("fw_dall", [P, T, NH, DH])
        prod = sb("fw_prod", [P, T, NH, DH])
        prodp = sb("fw_prodp", [P, T, NH, DH])
        oT = sb("fw_oT", [P, INNER // P, P])
        eb = sb("fw_eb", [P, NH])
        beta = sb("fw_beta", [P, NH])
        nrm = sb("fw_nrm", [P, 2, NH])
        rq = sb("fw_rq", [P, NH])
        rk = sb("fw_rk", [P, T, NH])
        nbk = sb("fw_nbk", [P, NH])
        ck = sb("fw_ck", [P, T, NH])
        cq = sb("fw_cq", [P, 2, T, NH])
        st = sb("fw_st", [P, TILES, 6])
        mv = sb("fw_mv", [P, TILES, 2])
        ve = sb("fw_ve", [P, TILES])
        rstd = sb("fw_rstd", [P, TILES])
        tmp = sb("fw_tmp", [P, TILES])

        pp = [pb(f"fw_pp{i}", [P, GH, 256]) for i in range(2)]
        po = pb("fw_po", [P, INNER // P, P])
        ph = pb("fw_ph", [P, DC, P])
        pa = pb("fw_pa", [P, D])

        x_in = [sem(f"x_in{s}") for s in range(HALVES)]
        wq_in, wo_in = sem("wq_in"), sem("wo_in")
        id_ready = sem("id_ready")
        ln = sem("ln")
        var_ready, sd_ready = sem("var_ready"), sem("sd_ready")
        h_ready = sem("h_ready")
        hcur_ready, res_done = sem("hcur_ready"), sem("res_done")
        hT_ps, hT_ready = sem("hT_ps"), sem("hT_ready")
        proj_done = sem("proj_done")
        u_ready = sem("u_ready")
        e_ready = sem("e_ready")
        vb_ready = sem("vb_ready")
        f_done = sem("f_done")
        norm = sem("norm")
        beta_ready = sem("beta_ready")
        bv_ready = sem("bv_ready")
        kk = sem("kk")
        delta_ready = sem("delta_ready")
        qk_mul, qk0_mul = sem("qk_mul"), sem("qk0_mul")
        cq_step = sem("cq_step")
        cq_ready = sem("cq_ready")
        po_slot = sem("po_slot")
        po_done = sem("po_done")
        oT_ready = sem("oT_ready")
        att_done = sem("att_done")

        cum = [t * (t + 1) // 2 for t in range(T + 1)]
        xs = x.rearrange("t (s p) d -> s p t d", p=P)
        block = ctx.enter_context(nc.Block())

        @block.sync
        def _(sp):
            for s in range(HALVES):
                sp.dma_start(hall[:, s * T:(s + 1) * T, :], xs[s]).then_inc(x_in[s], 16)
            sp.dma_start(wq[:], w_qkvb.rearrange("(c p) n -> p c n", p=P)).then_inc(wq_in, 16)
            sp.dma_start(wo[:], w_o.rearrange("(c p) n -> p c n", p=P)).then_inc(wo_in, 16)

        @block.gpsimd
        def _(pool):
            pool.memset(ident[:], 0.0).then_inc(id_ready, 1)
            pool.wait_ge(id_ready, 1)
            pool.affine_select(out=ident[:], in_=ident[:], compare_op=ALU.not_equal, fill=1.0, base=0,
                               pattern=[[-1, P]], channel_multiplier=1).then_inc(id_ready, 1)
            for n in range(TILES):
                s, t = n // T, n % T
                if t > 1:
                    pool.wait_ge(vb_ready, (n + 1) * GROUPS)
                    pool.wait_ge(beta_ready, n + 1)
                    pool.tensor_tensor(prod[:, t], vbuf[:], beta[:].unsqueeze(2).to_broadcast([P, NH, DH]),
                                       ALU.mult).then_inc(bv_ready, 1)
                if n:
                    pool.wait_ge(po_done, n)
                if t:
                    pool.wait_ge(f_done, (n + 1) * GROUPS)
                    pool.tensor_tensor(prodp[:, 0:t + 1], kall[:, 0:t + 1],
                                       qcur[:, t % 2].unsqueeze(1).to_broadcast([P, t + 1, NH, DH]),
                                       ALU.mult).then_inc(qk_mul, 1)
                pool.wait_ge(cq_ready, n + 1)
                pool.wait_ge(delta_ready, n + 1)
                for i in range(t + 1):
                    pool.tensor_tensor(prodp[:, i], dall[:, i],
                                       cq[:, t % 2, i].unsqueeze(2).to_broadcast([P, NH, DH]),
                                       ALU.mult).then_inc(po_slot, 1)

        @block.scalar
        def _(act):
            act.wait_ge(var_ready, 1)
            act.activation(rstd[:], ve[:], ACT.Sqrt).then_inc(sd_ready, 1)
            act.wait_ge(h_ready, 1)

            def copy_h(n):
                if n >= HB:
                    act.wait_ge(res_done, n - HB + 1)
                act.activation(hcur[:, n % HB], hall[:, n], ACT.Copy).then_inc(hcur_ready, 1)
                act.wait_ge(hT_ps, n + 1)
                act.activation(hT[:, n % 2], ph[:], ACT.Copy).then_inc(hT_ready, 1)

            def group(n, g):
                m = n * GROUPS + g
                ps = pp[g % 2]
                act.wait_ge(proj_done, m + 1)
                if m >= 2:
                    act.wait_ge(f_done, m - 1)
                act.activation(ebuf[:, g % 2], ps[:, :, 0:2 * DH], ACT.Relu, scale=-1.0).then_inc(u_ready, 1)
                if g == 0 and n:
                    act.wait_ge(bv_ready, n)
                hs = slice(GH * g, GH * g + GH)
                act.activation(vbuf[:, hs], ps[:, :, 2 * DH:3 * DH], ACT.Copy)
                act.activation(eb[:, hs].unsqueeze(2), ps[:, :, 3 * DH:HW], ACT.Exp, scale=-1.0) \
                    .then_inc(vb_ready, 1)
                act.wait_ge(u_ready, m + 1)
                act.activation(ebuf[:, g % 2], ebuf[:, g % 2], ACT.Exp, scale=-1.0).then_inc(e_ready, 1)

            def copy_oT(n):
                act.wait_ge(po_done, n + 1)
                if n:
                    act.wait_ge(att_done, n)
                act.activation(oT[:], po[:], ACT.Copy).then_inc(oT_ready, 1)

            copy_h(0)
            for g in range(GROUPS):
                group(0, g)
            for n in range(TILES):
                if n + 1 < TILES:
                    copy_h(n + 1)
                    for g in range(GROUPS if n % T == 0 else 2):
                        group(n + 1, g)
                if n:
                    copy_oT(n - 1)
                if n + 1 < TILES and n % T:
                    group(n + 1, 2)
                    group(n + 1, 3)
            copy_oT(TILES - 1)

        @block.tensor
        def _(pe):
            pe.wait_ge(id_ready, 2)

            def transpose_h(n):
                pe.wait_ge(hcur_ready, n + 1)
                for c in range(DC):
                    last = pe.transpose(ph[:, c], hcur[:, n % HB, c * P:(c + 1) * P], ident[:])
                last.then_inc(hT_ps, 1)
                pe.wait_ge(hT_ready, n + 1)

            def project(n, g):
                m = n * GROUPS + g
                if m >= 2:
                    pe.wait_ge(f_done, m - 1)
                    pe.wait_ge(vb_ready, m - 1)
                for b in range(2):
                    c0 = (GH * g + 2 * b) * HW
                    for c in range(DC):
                        last = pe.matmul(pp[g % 2][:, 2 * b:2 * b + 2, 0:HW], hT[:, n % 2, c],
                                         wq[:, c, c0:c0 + 2 * HW].rearrange("p (h n) -> p h n", n=HW),
                                         start=(c == 0), stop=(c == DC - 1))
                last.then_inc(proj_done, 1)

            def read_out(n):
                s, t = n // T, n % T
                if n:
                    pe.wait_ge(oT_ready, n)
                for i in range(t + 1):
                    pe.wait_ge(po_slot, s * cum[T] + cum[t] + i + 1)
                    row = prodp[:, i].rearrange("p h c -> p (h c)")
                    for c in range(INNER // P):
                        last = pe.matmul(po[:, c], row[:, c * P:(c + 1) * P], ident[:],
                                         start=(i == 0 and c % 4 == 0), stop=(i == t),
                                         skip_group_check=True)
                last.then_inc(po_done, 1)
                pe.wait_ge(oT_ready, n + 1)
                if n:
                    pe.wait_ge(res_done, n)
                for c in range(INNER // P):
                    last = pe.matmul(pa[:], oT[:, c], wo[:, c], start=(c == 0), stop=(c == INNER // P - 1))
                last.then_inc(att_done, 1)

            transpose_h(0)
            pe.wait_ge(wq_in, 16)
            for g in range(GROUPS):
                project(0, g)
            pe.wait_ge(wo_in, 16)
            for n in range(TILES):
                if n + 1 < TILES:
                    transpose_h(n + 1)
                    for g in range(GROUPS if n % T == 0 else 2):
                        project(n + 1, g)
                if n:
                    read_out(n - 1)
                if n + 1 < TILES and n % T:
                    project(n + 1, 2)
                    project(n + 1, 3)
            read_out(TILES - 1)

        @block.vector
        def _(dve):
            for m in range(TILES):
                if m % T == 0:
                    dve.wait_ge(x_in[m // T], 16)
                dve.bn_stats(st[:, m], hall[:, m]).then_inc(ln, 1)
            for m in range(TILES):
                dve.wait_ge(ln, TILES + m)
                dve.bn_aggr(mv[:, m], st[:, m]).then_inc(ln, 1)
            dve.wait_ge(ln, 2 * TILES)
            dve.tensor_scalar(ve[:], mv[:, :, 1], EPS, None, ALU.add).then_inc(var_ready, 1)
            dve.wait_ge(sd_ready, 1)
            dve.reciprocal(rstd[:], rstd[:]).then_inc(ln, 1)
            dve.wait_ge(ln, 2 * TILES + 1)
            newton_rsqrt(dve, ve[:], rstd[:], tmp[:], ln, 2 * TILES + 1)
            for m in range(TILES):
                last = dve.tensor_scalar(hall[:, m], hall[:, m], mv[:, m, 0:1], rstd[:, m:m + 1],
                                         ALU.subtract, ALU.mult)
            last.then_inc(h_ready, 1)

            def features(n, g):
                t = n % T
                ps = pp[g % 2]
                hs = slice(GH * g, GH * g + GH)
                dve.wait_ge(e_ready, n * GROUPS + g + 1)
                dve.scalar_tensor_tensor(qcur[:, t % 2, hs], ps[:, :, 0:DH], 1.0, ebuf[:, g % 2, :, 0:DH],
                                         ALU.add, ALU.max)
                dve.scalar_tensor_tensor(kall[:, t, hs], ps[:, :, DH:2 * DH], 1.0, ebuf[:, g % 2, :, DH:2 * DH],
                                         ALU.add, ALU.max).then_inc(f_done, 1)

            def residual(n):
                dve.wait_ge(att_done, n + 1)
                dve.tensor_tensor(hall[:, n], pa[:], hcur[:, n % HB], ALU.add).then_inc(res_done, 1)

            for g in range(GROUPS):
                features(0, g)
            for n in range(TILES):
                s, t = n // T, n % T
                dve.wait_ge(vb_ready, (n + 1) * GROUPS)
                dve.tensor_scalar(eb[:], eb[:], 1.0, None, ALU.add).then_inc(norm, 1)
                dve.wait_ge(f_done, (n + 1) * GROUPS)
                dve.reduce_sum(nrm[:, 0], qcur[:, t % 2], AX)
                dve.reduce_sum(nrm[:, 1], kall[:, t], AX).then_inc(norm, 1)
                dve.wait_ge(norm, 6 * n + 2)
                if n:
                    dve.wait_ge(bv_ready, n)
                dve.reciprocal(beta[:], eb[:]).then_inc(beta_ready, 1)
                dve.reciprocal(rq[:], nrm[:, 0]).then_inc(norm, 1)
                dve.reciprocal(rk[:, t], nrm[:, 1]).then_inc(norm, 1)
                dve.wait_ge(norm, 6 * n + 4)
                dve.wait_ge(beta_ready, n + 1)
                dve.tensor_scalar(rq[:], rq[:], FAST_SCALE, None, ALU.mult).then_inc(norm, 1)
                dve.scalar_tensor_tensor(nbk[:], beta[:], -1.0, rk[:, t], ALU.mult, ALU.mult).then_inc(norm, 1)
                if s:
                    dve.wait_ge(po_slot, s * cum[T] - T + t + 1)
                if t == 0:
                    dve.tensor_tensor(dall[:, 0], vbuf[:], beta[:].unsqueeze(2).to_broadcast([P, NH, DH]),
                                      ALU.mult).then_inc(bv_ready, 1)
                    dve.wait_ge(norm, 6 * n + 6)
                    dve.wait_ge(bv_ready, n + 1)
                    dve.sem_inc(delta_ready, 1)
                else:
                    k0 = (s * (T - 1) + t - 1) * 5
                    if t == 1:
                        dve.tensor_tensor(prod[:, 1], vbuf[:], beta[:].unsqueeze(2).to_broadcast([P, NH, DH]),
                                          ALU.mult).then_inc(bv_ready, 1)
                    dve.tensor_tensor(prod[:, 0:t], kall[:, 0:t],
                                      kall[:, t].unsqueeze(1).to_broadcast([P, t, NH, DH]),
                                      ALU.mult).then_inc(kk, 1)
                    dve.wait_ge(kk, k0 + 1)
                    dve.reduce_sum(ck[:, 0:t], prod[:, 0:t], AX).then_inc(kk, 1)
                    dve.wait_ge(kk, k0 + 2)
                    dve.tensor_tensor(ck[:, 0:t], ck[:, 0:t], rk[:, 0:t], ALU.mult).then_inc(kk, 1)
                    dve.wait_ge(kk, k0 + 3)
                    dve.wait_ge(norm, 6 * n + 6)
                    dve.tensor_tensor(ck[:, 0:t], ck[:, 0:t], nbk[:].unsqueeze(1).to_broadcast([P, t, NH]),
                                      ALU.mult).then_inc(kk, 1)
                    dve.wait_ge(kk, k0 + 4)
                    dve.tensor_tensor(prod[:, 0:t], dall[:, 0:t],
                                      ck[:, 0:t].unsqueeze(3).to_broadcast([P, t, NH, DH]),
                                      ALU.mult).then_inc(kk, 1)
                    dve.wait_ge(kk, k0 + 5)
                    dve.wait_ge(bv_ready, n + 1)
                    dve.reduce_sum(dall[:, t].rearrange("p h c -> p (h c)"),
                                   prod[:, 0:t + 1].rearrange("p s h c -> p (h c) s"),
                                   AX).then_inc(delta_ready, 1)
                dve.wait_ge(delta_ready, n + 1)
                early = 0 if t == T - 1 or n + 1 == TILES else GROUPS if t == 0 else 2
                for g in range(early):
                    features(n + 1, g)
                if t == 1 and s:
                    residual(n - 2)
                if t:
                    residual(n - 1)
                if t:
                    dots = prodp[:, 0:t + 1]
                    dve.wait_ge(qk_mul, s * (T - 1) + t)
                else:
                    dots = prod[:, 0:1]
                    dve.tensor_tensor(prod[:, 0], kall[:, 0], qcur[:, 0], ALU.mult).then_inc(qk0_mul, 1)
                    dve.wait_ge(qk0_mul, s + 1)
                dve.reduce_sum(cq[:, t % 2, 0:t + 1], dots, AX).then_inc(cq_step, 1)
                dve.wait_ge(cq_step, 2 * n + 1)
                dve.tensor_tensor(cq[:, t % 2, 0:t + 1], cq[:, t % 2, 0:t + 1], rk[:, 0:t + 1],
                                  ALU.mult).then_inc(cq_step, 1)
                dve.wait_ge(cq_step, 2 * n + 2)
                dve.tensor_tensor(cq[:, t % 2, 0:t + 1], cq[:, t % 2, 0:t + 1],
                                  rq[:].unsqueeze(1).to_broadcast([P, t + 1, NH]),
                                  ALU.mult).then_inc(cq_ready, 1)
                for g in range(early, GROUPS if n + 1 < TILES else 0):
                    features(n + 1, g)
            residual(TILES - 1)


def cross_inputs_block(nc, x, ctx_in, ln_g, ln_b, bout, ident, hall, zT, cT, cS):
    with ExitStack() as ctx:
        def sb(name, shape, dt=F32):
            return ctx.enter_context(nc.sbuf_tensor(name, shape, dt))

        def sem(name):
            return ctx.enter_context(nc.semaphore(name))

        xres = sb("ci_x", [P, TILES, D])
        z = sb("ci_z", [P, TILES, D])
        cnat = sb("ci_ctx", [P, JT, 2 * P])
        gam = sb("ci_gamma", [P, D])
        bet = sb("ci_beta", [P, D])
        bo = sb("ci_bout", [P, D])
        st = sb("ci_st", [P, TILES, 6])
        mv = sb("ci_mv", [P, TILES, 2])
        ve = sb("ci_ve", [P, 2, TILES])
        rstd = sb("ci_rstd", [P, 2, TILES])
        tmp = sb("ci_tmp", [P, TILES])
        tp = [ctx.enter_context(nc.psum_tensor(f"ci_tp{i}", [P, 512], F32)) for i in range(4)]

        x_in, c_in, v_in = sem("ci_x_in"), sem("ci_c_in"), sem("ci_v_in")
        xb_ready = sem("ci_xb")
        ln = sem("ci_ln")
        var_ready, sd_ready = sem("ci_var"), sem("ci_sd")
        z_ready = sem("ci_z_ready")
        x1_ready = sem("ci_x1")
        tp_full, tp_hi, tp_lo = sem("ci_full"), sem("ci_hi"), sem("ci_lo")
        bout_added = sem("ci_bout_added")
        xs = x.rearrange("t (s p) d -> s p t d", p=P)
        CTX_BANKS = 2 * JT // 4
        Z_BANKS = DC * TILES // 4

        def split_into(n):
            q = slice(n % 4 * 512, n % 4 * 512 + 512)
            if n < JT // 4:
                return [a[:, q] for a in cT]
            if n < CTX_BANKS:
                return [cS[:, q], cS[C2:P, q]]
            return [a[:, (n - CTX_BANKS) // 4, q] for a in zT]

        block = ctx.enter_context(nc.Block())

        @block.sync
        def _(sp):
            rows = ctx_in.rearrange("a b c -> (a b) c").rearrange("(m p) c -> p m c", p=P)
            sp.dma_start(cnat[:, :, 0:CD], rows).then_inc(c_in, 16)
            sp.dma_start(cnat[:, :, CD:2 * P], rows[:, :, P:CD]).then_inc(c_in, 16)
            for s in range(HALVES):
                sp.dma_start(xres[:, s * T:(s + 1) * T, :], xs[s]).then_inc(x_in, 16)
            for dst, src in ((gam, ln_g), (bet, ln_b), (bo, bout)):
                sp.dma_start(dst[:], src.unsqueeze(0).to_broadcast([P, D])).then_inc(v_in, 16)

        @block.gpsimd
        def _(pool):
            pool.wait_ge(x_in, 32)
            pool.wait_ge(v_in, 48)
            pool.tensor_tensor(xres[:], xres[:], bet[:].unsqueeze(1).to_broadcast([P, TILES, D]),
                               ALU.add).then_inc(xb_ready, 1)
            pool.wait_ge(z_ready, 1)
            pool.tensor_tensor(hall[:], hall[:], bo[:].unsqueeze(1).to_broadcast([P, TILES, D]),
                               ALU.add).then_inc(bout_added, 1)

        @block.vector
        def _(dve):
            def low_part(n):
                hi, lo = split_into(n)
                rows = slice(C2, P) if JT // 4 <= n < CTX_BANKS else slice(0, P)
                dve.wait_ge(tp_hi, n + 1)
                dve.tensor_tensor(lo, tp[n % 4][rows], hi[rows].bitcast(F32), ALU.subtract).then_inc(tp_lo, 1)

            base = 0
            for stage in range(2):
                for m in range(TILES):
                    dve.bn_stats(st[:, m], hall[:, m]).then_inc(ln, 1)
                for m in range(TILES):
                    dve.wait_ge(ln, base + TILES + m)
                    dve.bn_aggr(mv[:, m], st[:, m]).then_inc(ln, 1)
                dve.wait_ge(ln, base + 2 * TILES)
                dve.tensor_scalar(ve[:, stage], mv[:, :, 1], EPS, None, ALU.add).then_inc(var_ready, 1)
                dve.wait_ge(sd_ready, stage + 1)
                dve.reciprocal(rstd[:, stage], rstd[:, stage]).then_inc(ln, 1)
                dve.wait_ge(ln, base + 2 * TILES + 1)
                newton_rsqrt(dve, ve[:, stage], rstd[:, stage], tmp[:], ln, base + 2 * TILES + 1)
                base += 2 * TILES + 5
                dst = hall if stage == 0 else z
                for m in range(TILES):
                    last = dve.tensor_scalar(dst[:, m], hall[:, m], mv[:, m, 0:1], rstd[:, stage, m:m + 1],
                                             ALU.subtract, ALU.mult)
                if stage == 0:
                    last.then_inc(x1_ready, 1)
                    dve.wait_ge(x1_ready, 1)
                    dve.wait_ge(v_in, 48)
                    dve.tensor_tensor(hall[:], hall[:], gam[:].unsqueeze(1).to_broadcast([P, TILES, D]),
                                      ALU.mult).then_inc(x1_ready, 1)
                    dve.wait_ge(x1_ready, 2)
                    dve.wait_ge(xb_ready, 1)
                    dve.tensor_tensor(hall[:], hall[:], xres[:], ALU.add).then_inc(x1_ready, 1)
                    dve.wait_ge(x1_ready, 3)
                    for n in range(CTX_BANKS):
                        low_part(n)
                else:
                    last.then_inc(z_ready, 1)
                    for n in range(CTX_BANKS, CTX_BANKS + Z_BANKS):
                        low_part(n)

        @block.tensor
        def _(pe):
            pe.wait_ge(c_in, 32)
            for n in range(CTX_BANKS + Z_BANKS):
                if n == CTX_BANKS:
                    pe.wait_ge(z_ready, 1)
                if n >= 4:
                    pe.wait_ge(tp_lo, n - 3)
                for k in range(4):
                    if n < CTX_BANKS:
                        c, m = n // (JT // 4), n % (JT // 4) * 4 + k
                        src = cnat[:, m, c * P:(c + 1) * P]
                    else:
                        c, m = (n - CTX_BANKS) // (TILES // 4), (n - CTX_BANKS) % (TILES // 4) * 4 + k
                        src = z[:, m, c * P:(c + 1) * P]
                    last = pe.transpose(tp[n % 4][:, k * P:(k + 1) * P], src, ident[:])
                last.then_inc(tp_full, 1)

        @block.scalar
        def _(act):
            def root(stage):
                act.wait_ge(var_ready, stage + 1)
                act.activation(rstd[:, stage], ve[:, stage], ACT.Sqrt).then_inc(sd_ready, 1)

            root(0)
            for n in range(CTX_BANKS + Z_BANKS):
                if n == CTX_BANKS:
                    root(1)
                act.wait_ge(tp_full, n + 1)
                act.activation(split_into(n)[HI], tp[n % 4][:], ACT.Copy).then_inc(tp_hi, 1)


def cross_attention_block(nc, w_q, w_k, w_v, w_out, ident, hall, zT, cT, cS):
    with ExitStack() as ctx:
        def sb(name, shape, dt=F32):
            return ctx.enter_context(nc.sbuf_tensor(name, shape, dt))

        def sem(name):
            return ctx.enter_context(nc.semaphore(name))

        WQ, WK, WKS, WV, WVS = 0, 2, 3, 4, 5
        wst = sb("xa_wst", [P, 6, XD])
        w = [sb(f"xa_w{i}", [P, 6, XD], F32R) for i in (HI, LO)]
        woh = sb("xa_wout", [P, D])
        qT = [sb(f"xa_qT{i}", [P, TOK], F32R) for i in (HI, LO)]
        kT = [sb(f"xa_kT{i}", [P, TOK], F32R) for i in (HI, LO)]
        v = [sb(f"xa_v{i}", [P, TOK], F32R) for i in (HI, LO)]
        RING, HALF = 3, TOK // 2
        probs = sb("xa_probs", [P, RING, HALF])
        pT = [sb(f"xa_pT{i}", [P, 2, JT, 2 * P], F32R) for i in (HI, LO)]
        oT = sb("xa_oT", [P, 2 * P])
        mx = sb("xa_mx", [P, 2])
        nb = sb("xa_nb", [P, 2])
        rs = sb("xa_rs", [P, TILES, 2])
        rinv = sb("xa_rinv", [P, TILES])

        S = ctx.enter_context(nc.psum_tensor("xa_S", [P, 4, 512], F32))
        tb = [ctx.enter_context(nc.psum_tensor(f"xa_tb{i}", [P, 512], F32)) for i in range(2)]
        O = ctx.enter_context(nc.psum_tensor("xa_O", [P, 512], F32))
        Y = ctx.enter_context(nc.psum_tensor("xa_Y", [P, 512], F32))

        w_in, wo_in = sem("xa_w_in"), sem("xa_wo_in")
        w_hi, w_lo = sem("xa_w_hi"), sem("xa_w_lo")
        proj_mm, proj_hi, proj_lo = sem("xa_proj_mm"), sem("xa_proj_hi"), sem("xa_proj_lo")
        v_mm, v_hi, v_lo = sem("xa_v_mm"), sem("xa_v_hi"), sem("xa_v_lo")
        sim_done = sem("xa_sim")
        mx_ready, nb_ready = sem("xa_mx_ready"), sem("xa_nb_ready")
        exp_done = sem("xa_exp")
        t_mm = sem("xa_t_mm")
        hi_ready, lo_ready = sem("xa_hi"), sem("xa_lo")
        av_done = sem("xa_av")
        oT_ready = sem("xa_oT_ready")
        y_mm, y_used = sem("xa_y_mm"), sem("xa_y_used")
        r_step = sem("xa_r_step")

        QK = 8
        VU = 4
        W_DMAS = 7
        PAIRS = TILES // 2
        STEPS = TILES + 4
        PARTS = ((HI, HI), (HI, LO), (LO, HI))
        block = ctx.enter_context(nc.Block())

        @block.sync
        def _(sp):
            def load_weights(h):
                cols = bass.ds(h * XD, XD)
                sp.dma_start(wst[:, WQ:WQ + 2], w_q.rearrange("(c p) n -> p c n", p=P)[:, :, cols]).then_inc(w_in, 16)
                for at, src in ((WK, w_k), (WV, w_v)):
                    sp.dma_start(wst[:, at], src[0:P, cols]).then_inc(w_in, 16)
                    for r in (0, C2):
                        sp.dma_start(wst[r:r + C2, at + 1], src[P:CD, cols]).then_inc(w_in, 16)

            def load_out_weights(h):
                sp.dma_start(woh[:], w_out[bass.ds(h * XD, XD), :]).then_inc(wo_in, 16)

            load_weights(0)
            load_out_weights(0)
            with sp.Fori(0, XH - 1) as h:
                sp.wait_ge(w_hi, h + 1)
                sp.wait_ge(w_lo, h + 1)
                load_weights(h + 1)
                sp.wait_ge(y_mm, 1 + (h + 1) * PAIRS)
                load_out_weights(h + 1)

        @block.tensor
        def _(pe):
            pe.sem_inc(y_mm, 1)

            def project_qk(h, u):
                blk = slice(u % 4 * 512, u % 4 * 512 + 512)
                if u == 0:
                    pe.wait_ge(w_lo, h + 1)
                if u >= 4:
                    pe.wait_ge(proj_lo, h * QK + u - 3)
                if u < 4:
                    ops = [(w[a][:, WQ + c], zT[b][:, c, blk]) for c in range(DC) for a, b in PARTS]
                else:
                    ops = [(w[a][:, WK], cT[b][:, blk]) for a, b in PARTS]
                    ops += [(w[HI][:, WKS], cS[:, blk]), (w[LO][0:C2, WKS], cS[0:C2, blk])]
                for n, (a, b) in enumerate(ops):
                    last = pe.matmul(S[:, u % 4], a, b, start=(n == 0), stop=(n == len(ops) - 1))
                last.then_inc(proj_mm, 1)

            def project_v(h, u):
                dst = (Y, O)[u % 2]
                if u == 0:
                    pe.wait_ge(y_used, 1 + h * PAIRS)
                elif u == 1:
                    pe.wait_ge(oT_ready, 1 + h * PAIRS)
                else:
                    pe.wait_ge(v_lo, h * VU + u - 1)
                for k in range(4):
                    j = slice(u * 512 + k * P, u * 512 + (k + 1) * P)
                    ops = [(cT[a][:, j], w[b][:, WV]) for a, b in PARTS]
                    ops += [(cS[:, j], w[HI][:, WVS]), (cS[0:C2, j], w[LO][0:C2, WVS])]
                    for n, (a, b) in enumerate(ops):
                        last = pe.matmul(dst[:, k * P:(k + 1) * P], a, b, start=(n == 0), stop=(n == len(ops) - 1))
                last.then_inc(v_mm, 1)

            def scores(h, i):
                q = slice(i * P, (i + 1) * P)
                if i == 0:
                    pe.wait_ge(proj_lo, (h + 1) * QK)
                for u in range(2):
                    if i:
                        pe.wait_ge(exp_done, h * 2 * TILES + 2 * i - 1 + u)
                    for n, (a, b) in enumerate(PARTS):
                        for k in (2 * u, 2 * u + 1):
                            last = pe.matmul(S[:, k], qT[a][:, q], kT[b][:, k * 512:(k + 1) * 512],
                                             start=(n == 0), stop=(n == 2))
                    last.then_inc(sim_done, 1)

            def transposes(h, i, q):
                unit = 2 * i + q // 2
                if q % 2 == 0:
                    pe.wait_ge(exp_done, h * 2 * TILES + unit + 1)
                if i or q >= 2:
                    pe.wait_ge(lo_ready, h * 4 * TILES + 4 * i + q - 1)
                for k in range(4):
                    j = (4 * (q % 2) + k) * P
                    last = pe.transpose(tb[q % 2][:, k * P:(k + 1) * P], probs[:, unit % RING, j:j + P], ident[:])
                last.then_inc(t_mm, 1)

            def weighted(h, p, half):
                if half == 0:
                    if p == 0:
                        pe.wait_ge(v_lo, (h + 1) * VU)
                    pe.wait_ge(lo_ready, h * 4 * TILES + 8 * (p + 1))
                    pe.wait_ge(oT_ready, 1 + h * PAIRS + p)
                for j in range(half * JT // 2, (half + 1) * JT // 2):
                    vj = slice(j * P, (j + 1) * P)
                    for n, (a, b) in enumerate(PARTS):
                        last = pe.matmul(O[:, 0:2 * P], v[a][:, vj], pT[b][:, p % 2, j],
                                         start=(j == 0 and n == 0), stop=(j == JT - 1 and n == 2))
                if half:
                    last.then_inc(av_done, 1)

            def out_project(h, p):
                if p == 0:
                    pe.wait_ge(wo_in, h * 16 + 16)
                pe.wait_ge(oT_ready, 1 + h * PAIRS + p + 1)
                pe.wait_ge(y_used, 1 + h * PAIRS + p)
                for k in range(2):
                    last = pe.matmul(Y[:, k * D:(k + 1) * D], oT[:, k * P:(k + 1) * P], woh[:], start=True, stop=True)
                last.then_inc(y_mm, 1)

            def head(h, more):
                for i in range(TILES):
                    scores(h, i)
                    if i:
                        transposes(h, i - 1, 0)
                        transposes(h, i - 1, 1)
                    if i < 2:
                        project_v(h, 2 * i)
                        project_v(h, 2 * i + 1)
                    if i >= 3:
                        weighted(h, (i - 3) // 2, (i - 3) % 2)
                    if i:
                        transposes(h, i - 1, 2)
                        transposes(h, i - 1, 3)
                    if i >= 5 and i % 2:
                        out_project(h, (i - 5) // 2)
                weighted(h, PAIRS - 2, 1)
                if more:
                    pe.wait_ge(exp_done, (h + 1) * 2 * TILES - 1)
                for g in (0, 2):
                    transposes(h, TILES - 1, g)
                    transposes(h, TILES - 1, g + 1)
                    if more:
                        project_qk(h + 1, g)
                        project_qk(h + 1, g + 1)
                weighted(h, PAIRS - 1, 0)
                out_project(h, PAIRS - 2)
                if more:
                    for u in range(4, QK):
                        project_qk(h + 1, u)
                weighted(h, PAIRS - 1, 1)
                out_project(h, PAIRS - 1)

            for u in range(QK):
                project_qk(0, u)
            with pe.Fori(0, XH - 1) as h:
                head(h, True)
            head(XH - 1, False)

        @block.scalar
        def _(act):
            act.sem_inc(oT_ready, 1)

            def split_weights(h):
                act.wait_ge(w_in, (h + 1) * 16 * W_DMAS)
                act.activation(w[HI][:], wst[:], ACT.Copy).then_inc(w_hi, 1)

            def split_qk(h, u):
                act.wait_ge(proj_mm, h * QK + u + 1)
                act.activation((qT, kT)[u // 4][HI][:, u % 4 * 512:u % 4 * 512 + 512], S[:, u % 4], ACT.Copy) \
                    .then_inc(proj_hi, 1)

            def split_v(h, u):
                act.wait_ge(v_mm, h * VU + u + 1)
                act.activation(v[HI][:, u * 512:(u + 1) * 512], (Y, O)[u % 2][:], ACT.Copy).then_inc(v_hi, 1)

            def high_part(h, i, q):
                act.wait_ge(t_mm, h * 4 * TILES + 4 * i + q + 1)
                act.activation(pT[HI][:, i // 2 % 2, 4 * q:4 * q + 4, i % 2 * P:(i % 2 + 1) * P],
                               tb[q % 2][:].rearrange("p (k n) -> p k n", k=4), ACT.Copy).then_inc(hi_ready, 1)

            def exponentials(h, i):
                act.wait_ge(nb_ready, h * TILES + i + 1)
                for u in range(2):
                    unit = 2 * i + u
                    if unit >= RING:
                        act.wait_ge(t_mm, h * 4 * TILES + 2 * (unit - RING) + 2)
                    act.activation(probs[:, unit % RING], S[:, 2 * u:2 * u + 2].rearrange("p a b -> p (a b)"),
                                   ACT.Exp, bias=nb[:, i % 2:i % 2 + 1], scale=SOFT_SCALE,
                                   accum_out=rs[:, i, u:u + 1]).then_inc(exp_done, 1)

            def copy_oT(h, p):
                act.wait_ge(av_done, h * PAIRS + p + 1)
                act.wait_ge(y_mm, 1 + h * PAIRS + p)
                act.activation(oT[:], O[:, 0:2 * P], ACT.Copy).then_inc(oT_ready, 1)

            def head(h, more):
                for i in range(TILES):
                    if i:
                        high_part(h, i - 1, 0)
                        high_part(h, i - 1, 1)
                    exponentials(h, i)
                    if i:
                        high_part(h, i - 1, 2)
                        high_part(h, i - 1, 3)
                    if i < 2:
                        split_v(h, 2 * i)
                        split_v(h, 2 * i + 1)
                    if more and i == 7:
                        act.wait_ge(v_mm, (h + 1) * VU)
                        split_weights(h + 1)
                    if i >= 4 and i % 2 == 0:
                        copy_oT(h, (i - 4) // 2)
                for g in (0, 2):
                    high_part(h, TILES - 1, g)
                    if g == 0:
                        copy_oT(h, PAIRS - 2)
                    high_part(h, TILES - 1, g + 1)
                    if more:
                        split_qk(h + 1, g)
                        split_qk(h + 1, g + 1)
                if more:
                    for u in range(4, QK):
                        split_qk(h + 1, u)
                copy_oT(h, PAIRS - 1)

            split_weights(0)
            for u in range(QK):
                split_qk(0, u)
            with act.Fori(0, XH - 1) as h:
                head(h, True)
            head(XH - 1, False)

        @block.vector
        def _(dve):
            dve.sem_inc(y_used, 1)

            def split_weights(h):
                dve.wait_ge(w_hi, h + 1)
                dve.tensor_tensor(w[LO][:], wst[:], w[HI][:].bitcast(F32), ALU.subtract).then_inc(w_lo, 1)

            def split_qk(h, u):
                dst, blk = (qT, kT)[u // 4], slice(u % 4 * 512, u % 4 * 512 + 512)
                dve.wait_ge(proj_hi, h * QK + u + 1)
                dve.tensor_tensor(dst[LO][:, blk], S[:, u % 4], dst[HI][:, blk].bitcast(F32),
                                  ALU.subtract).then_inc(proj_lo, 1)

            def split_v(h, u):
                blk = slice(u * 512, (u + 1) * 512)
                dve.wait_ge(v_hi, h * VU + u + 1)
                dve.tensor_tensor(v[LO][:, blk], (Y, O)[u % 2][:], v[HI][:, blk].bitcast(F32),
                                  ALU.subtract).then_inc(v_lo, 1)

            def low_part(h, i, q):
                dst = (slice(None), i // 2 % 2, slice(4 * q, 4 * q + 4), slice(i % 2 * P, (i % 2 + 1) * P))
                dve.wait_ge(hi_ready, h * 4 * TILES + 4 * i + q + 1)
                dve.tensor_tensor(pT[LO][dst], tb[q % 2][:].rearrange("p (k n) -> p k n", k=4),
                                  pT[HI][dst].bitcast(F32), ALU.subtract).then_inc(lo_ready, 1)

            def maxima(h, i):
                for u in range(2):
                    dve.wait_ge(sim_done, h * 2 * TILES + 2 * i + u + 1)
                    dve.reduce_max(mx[:, u:u + 1], S[:, 2 * u:2 * u + 2].rearrange("p a b -> p (a b)"),
                                   AX).then_inc(mx_ready, 1)
                dve.wait_ge(mx_ready, h * 2 * TILES + 2 * i + 2)
                dve.tensor_scalar(nb[:, i % 2:i % 2 + 1], mx[:, 0:1], mx[:, 1:2], -SOFT_SCALE,
                                  ALU.max, ALU.mult).then_inc(nb_ready, 1)

            def add_output(h, p):
                r0 = h * 2 * PAIRS + 2 * p
                two = slice(2 * p, 2 * p + 2)
                dve.wait_ge(exp_done, h * 2 * TILES + 4 * p + 4)
                dve.tensor_tensor(rinv[:, two], rs[:, two, 0], rs[:, two, 1], ALU.add).then_inc(r_step, 1)
                dve.wait_ge(r_step, r0 + 1)
                dve.reciprocal(rinv[:, two], rinv[:, two]).then_inc(r_step, 1)
                dve.wait_ge(r_step, r0 + 2)
                dve.wait_ge(y_mm, 1 + h * PAIRS + p + 1)
                for m in (2 * p, 2 * p + 1):
                    last = dve.scalar_tensor_tensor(hall[:, m], Y[:, m % 2 * D:(m % 2 + 1) * D], rinv[:, m:m + 1],
                                                    hall[:, m], ALU.mult, ALU.add)
                last.then_inc(y_used, 1)

            def head(h, more):
                for i in range(TILES):
                    maxima(h, i)
                    if i:
                        for q in range(4):
                            low_part(h, i - 1, q)
                    if i < 2:
                        split_v(h, 2 * i)
                        split_v(h, 2 * i + 1)
                    if more and i == 7:
                        split_weights(h + 1)
                    if i >= 5 and i % 2:
                        add_output(h, (i - 5) // 2)
                for g in (0, 2):
                    low_part(h, TILES - 1, g)
                    low_part(h, TILES - 1, g + 1)
                    if more:
                        split_qk(h + 1, g)
                        split_qk(h + 1, g + 1)
                add_output(h, PAIRS - 2)
                if more:
                    for u in range(4, QK):
                        split_qk(h + 1, u)
                add_output(h, PAIRS - 1)

            split_weights(0)
            for u in range(QK):
                split_qk(0, u)
            with dve.Fori(0, XH - 1) as h:
                head(h, True)
            head(XH - 1, False)


def expert_block(nc, r_w, w1, w2, out, ident, hall, xe, ye):
    with ExitStack() as ctx:
        def sb(name, shape, dt=F32):
            return ctx.enter_context(nc.sbuf_tensor(name, shape, dt))

        def pb(name, shape):
            return ctx.enter_context(nc.psum_tensor(name, shape, F32))

        def sem(name):
            return ctx.enter_context(nc.semaphore(name))

        FLAT = [s * T + t for t in range(T) for s in range(HALVES)]
        z = sb("ex_z", [P, TILES, D])
        yg = sb("ex_yg", [P, TILES, D])
        zero = sb("ex_zero", [P, 4 * D])
        zt = sb("ex_zt", [P, 4, 4, P])
        rw = sb("ex_rw", [P, DC, E])
        lg = sb("ex_lg", [P, TILES, E])
        ex = sb("ex_ex", [P, TILES, E])
        oh = sb("ex_oh", [P, TILES, E])
        pre = sb("ex_pre", [P, TILES, E])
        rank = sb("ex_rank", [P, E])
        mx = sb("ex_mx", [P, TILES])
        top = sb("ex_top", [P, TILES])
        gate = sb("ex_gate", [P, TILES])
        pos = sb("ex_pos", [P, TILES])
        slot = sb("ex_slot", [P, TILES])
        sloti = sb("ex_sloti", [P, TILES], I32)
        ones = sb("ex_ones", [P, P])
        before = sb("ex_before", [P, P])
        st = sb("ex_st", [P, TILES, 6])
        mv = sb("ex_mv", [P, TILES, 2])
        ve = sb("ex_ve", [P, TILES])
        rstd = sb("ex_rstd", [P, TILES])
        tmp = sb("ex_tmp", [P, TILES])
        w1b = [sb(f"ex_w1_{i}", [P, DC, F]) for i in range(2)]
        w2b = [sb(f"ex_w2_{i}", [P, FC, D]) for i in range(2)]
        xn = [sb(f"ex_xn{i}", [P, CT, D]) for i in range(2)]
        xT = [sb(f"ex_xT{i}", [P, DC, CAP]) for i in range(2)]
        hid = [sb(f"ex_hid{i}", [P, FC, CAP]) for i in range(2)]
        yb = [sb(f"ex_yb{i}", [P, CT, D]) for i in range(2)]

        tp = [pb(f"ex_tp{i}", [P, 512]) for i in range(2)]
        H = [pb(f"ex_H{i}", [P, 2, CAP]) for i in range(FC // 2)]
        Yp = [pb(f"ex_Y{i}", [P, CT, D]) for i in range(2)]
        rp = Yp[0][:, 0, 0:TILES * E]

        zero_set, zero_out = sem("ex_zero_set"), sem("ex_zero_out")
        consts = sem("ex_consts")
        rw_in = sem("ex_rw_in")
        ln, var_ready, sd_ready = sem("ex_ln"), sem("ex_var"), sem("ex_sd")
        z_ready = sem("ex_z_ready")
        ztp, zt_ready = sem("ex_ztp"), sem("ex_zt_ready")
        logits = sem("ex_logits")
        shifted, expd = sem("ex_shifted"), sem("ex_expd")
        rt = sem("ex_rt")
        oh_ready, pos_mm, slot_ready = sem("ex_oh_ready"), sem("ex_pos_mm"), sem("ex_slot_ready")
        yg_zero = sem("ex_yg_zero")
        scattered = sem("ex_scattered")
        w_in = [sem(f"ex_w_in{i}") for i in range(2)]
        x_in = [sem(f"ex_x_in{i}") for i in range(2)]
        xtp, xT_ready = sem("ex_xtp"), sem("ex_xT_ready")
        h_mm, gelu = sem("ex_h_mm"), sem("ex_gelu")
        y_mm = [sem(f"ex_y_mm{i}") for i in range(2)]
        y_copied = [sem(f"ex_y_copied{i}") for i in range(2)]
        y_out = [sem(f"ex_y_out{i}") for i in range(2)]
        yb_free = [sem(f"ex_yb_free{i}") for i in range(2)]
        gathered = [sem(f"ex_gath{m}") for m in range(TILES)]
        added, stored = sem("ex_added"), sem("ex_stored")

        HU = FC // 2
        block = ctx.enter_context(nc.Block())

        @block.sync
        def _(sp):
            sp.wait_ge(zero_set, 1)
            sp.dma_start(xe.rearrange("(p r) d -> p (r d)", r=4 * 4)[:, 0:4 * D], zero[:]).then_inc(zero_out, 16)
            for k in range(1, 4):
                sp.dma_start(xe.rearrange("(p r) d -> p (r d)", r=4 * 4)[:, k * 4 * D:(k + 1) * 4 * D], zero[:]) \
                    .then_inc(zero_out, 16)
            sp.dma_start(rw[:], r_w.rearrange("(c p) e -> p c e", p=P)).then_inc(rw_in, 16)
            with sp.Fori(0, E // 2) as ep:
                for i in range(2):
                    e = ep * 2 + i
                    sp.wait_ge(y_mm[i], 1 + ep)
                    sp.dma_start(w1b[i][:], w1[bass.ds(e, 1)].rearrange("e (c p) f -> p (e c) f", p=P)) \
                        .then_inc(w_in[i], 16)
                    sp.dma_start(w2b[i][:], w2[bass.ds(e, 1)].rearrange("e (c p) d -> p (e c) d", p=P)) \
                        .then_inc(w_in[i], 16)
                sp.wait_ge(scattered, 16 * TILES)
                for i in range(2):
                    sp.dma_start(xn[i][:], xe[bass.ds((ep * 2 + i) * CAP, CAP)].rearrange("(k p) d -> p k d", p=P)) \
                        .then_inc(x_in[i], 16)

        @block.gpsimd
        def _(pool):
            pool.memset(zero[:], 0.0).then_inc(zero_set, 1)
            pool.memset(ones[:], 1.0).then_inc(consts, 1)
            pool.wait_ge(consts, 1)
            pool.affine_select(out=before[:], in_=ones[:], compare_op=ALU.is_gt, fill=0.0, base=0,
                               pattern=[[1, P]], channel_multiplier=-1).then_inc(consts, 1)
            for e in range(E):
                last = pool.memset(rank[:, e:e + 1], float(E - e))
            last.then_inc(consts, 1)
            pool.memset(yg[:], 0.0).then_inc(yg_zero, 1)
            pool.wait_ge(zero_out, 64)
            pool.wait_ge(slot_ready, 1)
            pool.wait_ge(z_ready, 1)
            for m in range(TILES):
                pool.indirect_dma_start(xe, bass.IndirectOffsetOnAxis(sloti[:, m:m + 1], 0), z[:, m], None,
                                        bounds_check=E * CAP - 1, oob_is_err=False).then_inc(scattered, 16)
            for i in range(2):
                pool.sem_inc(yb_free[i], 1)
            with pool.Fori(0, E // 2) as ep:
                for i in range(2):
                    pool.wait_ge(y_copied[i], 1 + ep + 1)
                    pool.dma_start(ye[bass.ds((ep * 2 + i) * CAP, CAP)].rearrange("(k p) d -> p k d", p=P), yb[i][:]) \
                        .then_inc(y_out[i], 16)
                    pool.wait_ge(y_out[i], 16 * ep + 16)
                    pool.sem_inc(yb_free[i], 1)
            pool.wait_ge(yg_zero, 1)
            for m in range(TILES):
                pool.indirect_dma_start(yg[:, m], None, ye, bass.IndirectOffsetOnAxis(sloti[:, m:m + 1], 0),
                                        bounds_check=E * CAP - 1, oob_is_err=False).then_inc(gathered[m], 16)

        @block.vector
        def _(dve):
            for m in range(TILES):
                dve.bn_stats(st[:, m], hall[:, m]).then_inc(ln, 1)
            for m in range(TILES):
                dve.wait_ge(ln, TILES + m)
                dve.bn_aggr(mv[:, m], st[:, m]).then_inc(ln, 1)
            dve.wait_ge(ln, 2 * TILES)
            dve.tensor_scalar(ve[:], mv[:, :, 1], EPS, None, ALU.add).then_inc(var_ready, 1)
            dve.wait_ge(sd_ready, 1)
            dve.reciprocal(rstd[:], rstd[:]).then_inc(ln, 1)
            dve.wait_ge(ln, 2 * TILES + 1)
            newton_rsqrt(dve, ve[:], rstd[:], tmp[:], ln, 2 * TILES + 1)
            for m in range(TILES):
                last = dve.tensor_scalar(z[:, m], hall[:, m], mv[:, m, 0:1], rstd[:, m:m + 1],
                                         ALU.subtract, ALU.mult)
            last.then_inc(z_ready, 1)
            for n in range(DC * TILES // 4):
                dve.wait_ge(ztp, n + 1)
                if n >= 4:
                    dve.wait_ge(logits, 2 * ((n - 4) // 2 + 1))
                dve.tensor_copy(zt[:, n % 4], tp[n % 2][:].rearrange("p (k n) -> p k n", k=4)).then_inc(zt_ready, 1)

            def wide(a):
                return a.unsqueeze(2).to_broadcast([P, TILES, E])

            dve.wait_ge(logits, TILES // 2)
            dve.tensor_copy(lg[:].rearrange("p m e -> p (m e)"), rp).then_inc(rt, 1)
            dve.wait_ge(rt, 1)
            dve.reduce_max(mx[:], lg[:], AX).then_inc(rt, 1)
            dve.wait_ge(rt, 2)
            dve.tensor_tensor(ex[:], lg[:], wide(mx[:]), ALU.subtract).then_inc(shifted, 1)
            dve.tensor_tensor(oh[:], lg[:], wide(mx[:]), ALU.is_equal).then_inc(rt, 1)
            dve.wait_ge(rt, 3)
            dve.wait_ge(consts, 3)
            dve.tensor_tensor(oh[:], oh[:], rank[:].unsqueeze(1).to_broadcast([P, TILES, E]), ALU.mult).then_inc(rt, 1)
            dve.wait_ge(rt, 4)
            dve.reduce_max(top[:], oh[:], AX).then_inc(rt, 1)
            dve.wait_ge(rt, 5)
            dve.tensor_tensor(oh[:], oh[:], wide(top[:]), ALU.is_equal).then_inc(oh_ready, 1)
            dve.memset(pre[:, FLAT[0]], 0.0).then_inc(rt, 1)
            dve.wait_ge(oh_ready, 1)
            for n in range(1, TILES):
                dve.wait_ge(rt, 5 + n)
                dve.tensor_tensor(pre[:, FLAT[n]], pre[:, FLAT[n - 1]], oh[:, FLAT[n - 1]], ALU.add).then_inc(rt, 1)
            done = 5 + TILES
            dve.wait_ge(expd, 1)
            dve.reduce_sum(gate[:], ex[:], AX).then_inc(rt, 1)
            dve.wait_ge(rt, done + 1)
            dve.reciprocal(gate[:], gate[:]).then_inc(rt, 1)
            dve.wait_ge(pos_mm, 1)
            dve.wait_ge(rt, done + 2)
            dve.tensor_tensor(lg[:].rearrange("p m e -> p (m e)"), rp, oh[:].rearrange("p m e -> p (m e)"),
                              ALU.mult).then_inc(rt, 1)
            dve.wait_ge(rt, done + 3)
            dve.reduce_sum(pos[:], lg[:], AX).then_inc(rt, 1)
            dve.wait_ge(rt, done + 4)
            dve.tensor_scalar(slot[:], pos[:], float(CAP), float(2 * E * CAP), ALU.is_ge, ALU.mult).then_inc(rt, 1)
            dve.tensor_scalar(top[:], top[:], -float(CAP), float(E * CAP), ALU.mult, ALU.add).then_inc(rt, 1)
            dve.wait_ge(rt, done + 6)
            dve.tensor_tensor(slot[:], slot[:], pos[:], ALU.add).then_inc(rt, 1)
            dve.wait_ge(rt, done + 7)
            dve.tensor_tensor(slot[:], slot[:], top[:], ALU.add).then_inc(rt, 1)
            dve.wait_ge(rt, done + 8)
            dve.tensor_copy(sloti[:], slot[:]).then_inc(slot_ready, 1)
            for i in range(2):
                dve.sem_inc(y_copied[i], 1)
            with dve.Fori(0, E // 2) as ep:
                for i in range(2):
                    e = ep * 2 + i
                    for c in range(DC):
                        dve.wait_ge(xtp, e * DC + c + 1)
                        dve.tensor_copy(xT[i][:, c], tp[c][:, 0:CAP]).then_inc(xT_ready, 1)
                    dve.wait_ge(y_mm[i], 1 + ep + 1)
                    dve.wait_ge(yb_free[i], 1 + ep)
                    dve.tensor_copy(yb[i][:], Yp[i][:]).then_inc(y_copied[i], 1)
            for m in range(TILES):
                dve.wait_ge(gathered[m], 16)
                dve.scalar_tensor_tensor(yg[:, m], yg[:, m], gate[:, m:m + 1], hall[:, m],
                                         ALU.mult, ALU.add).then_inc(added, 1)

        @block.scalar
        def _(act):
            act.wait_ge(var_ready, 1)
            act.activation(rstd[:], ve[:], ACT.Sqrt).then_inc(sd_ready, 1)
            act.wait_ge(shifted, 1)
            act.activation(ex[:], ex[:], ACT.Exp).then_inc(expd, 1)
            with act.Fori(0, E // 2) as ep:
                for i in range(2):
                    act.wait_ge(y_mm[i], 1 + ep)
                    for u in range(HU):
                        act.wait_ge(h_mm, (ep * 2 + i) * HU + u + 1)
                        act.activation(hid[i][:, 2 * u:2 * u + 2], H[u][:], ACT.Gelu_apprx_tanh).then_inc(gelu, 1)
            xo = out.rearrange("t (s p) d -> s t p d", p=P)
            for m in range(TILES):
                act.wait_ge(added, m + 1)
                act.dma_start(xo[m // T, m % T], yg[:, m]).then_inc(stored, 16)
            act.wait_ge(stored, 16 * TILES)

        @block.tensor
        def _(pe):
            pe.wait_ge(z_ready, 1)
            pe.wait_ge(rw_in, 16)
            for q in range(TILES // 4):
                for c in range(DC):
                    n = q * DC + c
                    if n >= 2:
                        pe.wait_ge(zt_ready, n - 1)
                    for k in range(4):
                        last = pe.transpose(tp[n % 2][:, k * P:(k + 1) * P], z[:, 4 * q + k, c * P:(c + 1) * P], ident[:])
                    last.then_inc(ztp, 1)
                pe.wait_ge(zt_ready, (q + 1) * DC)
                for k in range(4):
                    m = 4 * q + k
                    for c in range(DC):
                        last = pe.matmul(rp[:, m * E:(m + 1) * E], zt[:, (q * DC + c) % 4, k], rw[:, c],
                                         start=(c == 0), stop=(c == DC - 1))
                    if k % 2:
                        last.then_inc(logits, 1)
            pe.wait_ge(consts, 3)
            pe.wait_ge(oh_ready, 1)
            pe.wait_ge(rt, 5 + TILES)
            pe.matmul(rp, before[:], oh[:].rearrange("p m e -> p (m e)"), start=True, stop=False)
            pe.matmul(rp, ones[:], pre[:].rearrange("p m e -> p (m e)"), start=False, stop=True).then_inc(pos_mm, 1)
            for i in range(2):
                pe.sem_inc(y_mm[i], 1)
            with pe.Fori(0, E // 2) as ep:
                for i in range(2):
                    e = ep * 2 + i
                    pe.wait_ge(x_in[i], ep * 16 + 16)
                    for c in range(DC):
                        for k in range(CT):
                            last = pe.transpose(tp[c][:, k * P:(k + 1) * P], xn[i][:, k, c * P:(c + 1) * P], ident[:])
                        last.then_inc(xtp, 1)
                    pe.wait_ge(w_in[i], ep * 32 + 32)
                    pe.wait_ge(xT_ready, e * DC + DC)
                    for u in range(HU):
                        for k in range(2):
                            f = (2 * u + k) * P
                            for c in range(DC):
                                last = pe.matmul(H[u][:, k], w1b[i][:, c, f:f + P], xT[i][:, c],
                                                 start=(c == 0), stop=(c == DC - 1))
                        last.then_inc(h_mm, 1)
                    pe.wait_ge(y_copied[i], 1 + ep)
                    for f in range(FC):
                        if f % 2 == 0:
                            pe.wait_ge(gelu, e * HU + f // 2 + 1)
                        for k in range(CT):
                            last = pe.matmul(Yp[i][:, k], hid[i][:, f, k * P:(k + 1) * P], w2b[i][:, f],
                                             start=(f == 0 and k == 0), stop=(f == FC - 1), skip_group_check=True)
                    last.then_inc(y_mm[i], 1)


def decoder_kernel(nc, x, context, w_qkvb, w_o, ln_g, ln_b, w_q, w_k, w_v, w_out, b_out, router_w, w1, w2, out):
    xe = nc.dram_tensor("expert_in", [E * CAP, D], F32, kind="Internal").ap()
    ye = nc.dram_tensor("expert_out", [E * CAP, D], F32, kind="Internal").ap()
    with ExitStack() as ctx:
        ident = ctx.enter_context(nc.sbuf_tensor("ident", [P, P], F32))
        hall = ctx.enter_context(nc.sbuf_tensor("hall", [P, TILES, D], F32))
        fast_weight_block(nc, x, w_qkvb, w_o, ident, hall)
        with ExitStack() as cross:
            zT = [cross.enter_context(nc.sbuf_tensor(f"zT{i}", [P, DC, TOK], F32R)) for i in (HI, LO)]
            cT = [cross.enter_context(nc.sbuf_tensor(f"cT{i}", [P, TOK], F32R)) for i in (HI, LO)]
            cS = cross.enter_context(nc.sbuf_tensor("cS", [P, TOK], F32R))
            cross_inputs_block(nc, x, context, ln_g, ln_b, b_out, ident, hall, zT, cT, cS)
            cross_attention_block(nc, w_q, w_k, w_v, w_out, ident, hall, zT, cT, cS)
        expert_block(nc, router_w, w1, w2, out, ident, hall, xe, ye)


_INS = ['x', 'ctx_768', 'L0_attn_W_qkvb', 'L0_attn_W_o', 'L0_attn_ln_g', 'L0_attn_ln_b', 'L0_xattn_Wq', 'L0_xattn_Wk',
        'L0_xattn_Wv', 'L0_xattn_Wout', 'L0_xattn_bout', 'L0_ffn_router_w', 'L0_ffn_w1', 'L0_ffn_w2']


def kernel(**inputs):
    import numpy as _np
    import concourse.bacc as _bacc
    from concourse import mybir as _mybir
    from concourse.bass_utils import run_bass_kernel_spmd as _run

    nc = _bacc.Bacc("TRN2", target_bir_lowering=False, num_devices=1)
    arrays, args = {}, []
    for name in _INS:
        a = _np.ascontiguousarray(inputs[name])
        arrays[f"in_{name}_dram"] = a
        args.append(nc.dram_tensor(f"in_{name}_dram", a.shape, _mybir.dt.from_np(a.dtype), kind="ExternalInput").ap())
    args.append(nc.dram_tensor("out_0_dram", (T, B, D), F32, kind="ExternalOutput").ap())
    decoder_kernel(nc, *args)
    r = _run(nc, [arrays], core_ids=[0])
    return r.results[0]["out_0_dram"]
```

```python
from contextlib import ExitStack

import concourse.bass as bass
from concourse import mybir

F32 = mybir.dt.float32
F32R = mybir.dt.float32r
I32 = mybir.dt.int32
ALU = mybir.AluOpType
ACT = mybir.ActivationFunctionType
AX = mybir.AxisListType.X

P = 128
D = 256
DC = D // P
T, B = 8, 256
HALVES = B // P
TILES = T * HALVES
TOK = T * B
EPS = 1e-5

NH, DH = 16, 64
HW = 3 * DH + 1
INNER = NH * DH
FAST_SCALE = 1.0 / 8.0
GH = 4
GROUPS = NH // GH

XH, XD = 8, 128
CD = 192
C2 = CD - P
JT = TOK // P
SOFT_SCALE = 1.5 * XD ** -0.5

HI, LO = 0, 1

E, F = 8, 1024
FC = F // P
CAP = TOK // E
CT = CAP // P
X1, GATE, TOKEN, ROW = D, 2 * D, 2 * D + 1, 2 * D + 2


def newton_rsqrt(dve, ve, y, t, done, base):
    dve.tensor_tensor(t, y, y, ALU.mult).then_inc(done, 1)
    dve.wait_ge(done, base + 1)
    dve.tensor_tensor(t, t, ve, ALU.mult).then_inc(done, 1)
    dve.wait_ge(done, base + 2)
    dve.tensor_scalar(t, t, -0.5, 1.5, ALU.mult, ALU.add).then_inc(done, 1)
    dve.wait_ge(done, base + 3)
    dve.tensor_tensor(y, y, t, ALU.mult).then_inc(done, 1)
    dve.wait_ge(done, base + 4)


def fast_weight_block(nc, x, w_qkvb, w_o, ident, hall):
    with ExitStack() as ctx:
        def sb(name, shape, dt=F32):
            return ctx.enter_context(nc.sbuf_tensor(name, shape, dt))

        def pb(name, shape):
            return ctx.enter_context(nc.psum_tensor(name, shape, F32))

        def sem(name):
            return ctx.enter_context(nc.semaphore(name))

        wq = sb("fw_wqkvb", [P, DC, NH * HW])
        wo = sb("fw_wo", [P, INNER // P, D])
        hT = sb("fw_hT", [P, 2, DC, P])
        ebuf = sb("fw_ebuf", [P, 2, GH, 2 * DH])
        vbuf = sb("fw_vbuf", [P, NH, DH])
        qcur = sb("fw_qcur", [P, 2, NH, DH])
        kall = sb("fw_kall", [P, T + 1, NH, DH])
        dall = sb("fw_dall", [P, T, NH, DH])
        prod = sb("fw_prod", [P, T, NH, DH])
        prodp = sb("fw_prodp", [P, T, NH, DH])
        oT = sb("fw_oT", [P, INNER // P, P])
        eb = sb("fw_eb", [P, 2, NH])
        beta = sb("fw_beta", [P, 2, NH])
        nrm = sb("fw_nrm", [P, 2, NH])
        rq = sb("fw_rq", [P, 2, NH])
        rk = sb("fw_rk", [P, T + 1, NH])
        nbk = sb("fw_nbk", [P, 2, NH])
        ck = sb("fw_ck", [P, T, NH])
        cq = sb("fw_cq", [P, 2, T, NH])
        st = sb("fw_st", [P, TILES, 6])
        mv = sb("fw_mv", [P, TILES, 2])
        ve = sb("fw_ve", [P, TILES])
        rstd = sb("fw_rstd", [P, TILES])
        tmp = sb("fw_tmp", [P, TILES])

        pp = [pb(f"fw_pp{i}", [P, GH, 256]) for i in range(2)]
        po = pb("fw_po", [P, INNER // P, P])
        ph = pb("fw_ph", [P, DC, P])
        pa = pb("fw_pa", [P, D])

        x_in = [sem(f"x_in{s}") for s in range(HALVES)]
        wq_in = [sem(f"wq_in{g}") for g in range(GROUPS)]
        wo_in = sem("wo_in")
        id_ready = sem("id_ready")
        ln = sem("ln")
        var_ready, sd_ready = sem("var_ready"), sem("sd_ready")
        h_ready = sem("h_ready")
        res_done = sem("res_done")
        hT_ps, hT_ready = sem("hT_ps"), sem("hT_ready")
        proj_done = sem("proj_done")
        u_ready = sem("u_ready")
        e_ready = sem("e_ready")
        vb_ready = sem("vb_ready")
        f_done = sem("f_done")
        norm = sem("norm")
        beta_ready = sem("beta_ready")
        bv_ready = sem("bv_ready")
        kk = sem("kk")
        kk_pool = sem("kk_pool")
        delta_ready = sem("delta_ready")
        qk_mul, qk0_mul = sem("qk_mul"), sem("qk0_mul")
        cq_step = sem("cq_step")
        cq_ready = sem("cq_ready")
        po_slot = sem("po_slot")
        po_slot_v = sem("po_slot_v")
        po_read = sem("po_read")
        oT_ready = sem("oT_ready")
        att_done = sem("att_done")

        cum = [t * (t + 1) // 2 for t in range(T + 1)]
        KK_POOL = [0, 0, 1, 2, 3, 4, 4, 2]
        LAST_V = T // 2

        def po_slots(n, i):
            return n // T * cum[T] + cum[n % T] + i

        def dot_parts(n):
            return sum(0 if i % T == 0 else 1 if i % T == 1 else 2 for i in range(n + 1))

        def kk_steps(n):
            return sum(KK_POOL[i % T] > 0 for i in range(n + 1))

        xs = x.rearrange("t (s p) d -> s p t d", p=P)

        def at(s, i):
            return T - 1 - i if s else i

        def places(s, a, b):
            return slice(T - b, T - a) if s else slice(a, b)

        def key_at(s, i):
            return T - i if s else i

        def key_places(s, a, b):
            return slice(T + 1 - b, T + 1 - a) if s else slice(a, b)

        def read_order(n):
            return range(n % T, -1, -1) if n == T - 1 else range(n % T + 1)

        block = ctx.enter_context(nc.Block())

        @block.sync
        def _(sp):
            wq_rows = w_qkvb.rearrange("(c p) n -> p c n", p=P)
            for g in range(GROUPS):
                if g < HALVES:
                    sp.dma_start(hall[:, g * T:(g + 1) * T, :], xs[g]).then_inc(x_in[g], 16)
                cols = slice(g * GH * HW, (g + 1) * GH * HW)
                sp.dma_start(wq[:, :, cols], wq_rows[:, :, cols]).then_inc(wq_in[g], 16)
            sp.dma_start(wo[:], w_o.rearrange("(c p) n -> p c n", p=P)).then_inc(wo_in, 16)

        @block.gpsimd
        def _(pool):
            pool.memset(ident[:], 0.0).then_inc(id_ready, 1)
            pool.wait_ge(id_ready, 1)
            pool.affine_select(out=ident[:], in_=ident[:], compare_op=ALU.not_equal, fill=1.0, base=0,
                               pattern=[[-1, P]], channel_multiplier=1).then_inc(id_ready, 1)
            for n in range(TILES):
                s, t = n // T, n % T
                if t == 0 and n:
                    pool.wait_ge(po_read, po_slots(n - 1, T))
                if t:
                    pool.wait_ge(f_done, (n + 1) * GROUPS)
                    cut = t // 2
                    for a, b in ((0, cut), (cut, t + 1)):
                        if b:
                            pool.wait_ge(po_read, po_slots(n - 1, min(b, t)))
                            pool.tensor_tensor(prodp[:, places(s, a, b)], kall[:, key_places(s, a, b)],
                                               qcur[:, t % 2].unsqueeze(1).to_broadcast([P, b - a, NH, DH]),
                                               ALU.mult).then_inc(qk_mul, 1)
                if t + 1 < T:
                    u = t + 1
                    pool.wait_ge(vb_ready, (n + 2) * GROUPS)
                    pool.wait_ge(beta_ready, n + 2)
                    pool.tensor_tensor(prod[:, at(s, u)], prod[:, at(s, u)],
                                       beta[:, u % 2].unsqueeze(2).to_broadcast([P, NH, DH]),
                                       ALU.mult).then_inc(bv_ready, 1)
                    if KK_POOL[u]:
                        pool.wait_ge(f_done, (n + 2) * GROUPS)
                        pool.wait_ge(delta_ready, n + 1)
                        part = (s, u - KK_POOL[u], u)
                        pool.tensor_tensor(prod[:, places(*part)], kall[:, key_places(*part)],
                                           kall[:, key_at(s, u)].unsqueeze(1).to_broadcast([P, KK_POOL[u], NH, DH]),
                                           ALU.mult).then_inc(kk_pool, 1)
                pool.wait_ge(cq_ready, n + 1)
                pool.wait_ge(delta_ready, n + 1)
                for i in read_order(n):
                    if n < TILES - 1 or i < LAST_V:
                        pool.tensor_tensor(prodp[:, at(s, i)], dall[:, at(s, i)],
                                           cq[:, t % 2, at(s, i)].unsqueeze(2).to_broadcast([P, NH, DH]),
                                           ALU.mult).then_inc(po_slot, 1)

        @block.scalar
        def _(act):
            for s in range(HALVES):
                half = slice(s * T, (s + 1) * T)
                act.wait_ge(var_ready, s + 1)
                act.activation(rstd[:, half], ve[:, half], ACT.Sqrt).then_inc(sd_ready, 1)

            def copy_h(n):
                act.wait_ge(hT_ps, n + 1)
                act.activation(hT[:, n % 2], ph[:], ACT.Copy).then_inc(hT_ready, 1)

            def group(n, g):
                m = n * GROUPS + g
                ps = pp[g % 2]
                act.wait_ge(proj_done, m + 1)
                if m >= 2:
                    act.wait_ge(f_done, m - 1)
                act.activation(ebuf[:, g % 2], ps[:, :, 0:2 * DH], ACT.Relu, scale=-1.0).then_inc(u_ready, 1)
                if g == 0 and n >= 2:
                    act.wait_ge(bv_ready, n - 1)
                if g == 0 and n == T + 1:
                    act.wait_ge(delta_ready, T)
                hs = slice(GH * g, GH * g + GH)
                v = vbuf[:, hs] if n % T == 0 else prod[:, at(n // T, n % T), hs]
                act.activation(v, ps[:, :, 2 * DH:3 * DH], ACT.Copy)
                act.activation(eb[:, n % 2, hs].unsqueeze(2), ps[:, :, 3 * DH:HW], ACT.Exp, scale=-1.0) \
                    .then_inc(vb_ready, 1)
                act.wait_ge(u_ready, m + 1)
                act.activation(ebuf[:, g % 2], ebuf[:, g % 2], ACT.Exp, scale=-1.0).then_inc(e_ready, 1)

            def copy_oT(n):
                act.wait_ge(po_read, po_slots(n, n % T + 1 if n < TILES - 1 else LAST_V + 1))
                if n:
                    act.wait_ge(att_done, n)
                act.activation(oT[:], po[:], ACT.Copy).then_inc(oT_ready, 1)

            copy_h(0)
            for g in range(GROUPS):
                group(0, g)
            for n in range(TILES):
                if n + 1 < TILES:
                    copy_h(n + 1)
                    for g in range(GROUPS):
                        group(n + 1, g)
                if n:
                    copy_oT(n - 1)
            copy_oT(TILES - 1)

        @block.tensor
        def _(pe):
            pe.wait_ge(id_ready, 2)

            def transpose_h(n):
                pe.wait_ge(h_ready, n // T + 1)
                for c in range(DC):
                    last = pe.transpose(ph[:, c], hall[:, n, c * P:(c + 1) * P], ident[:])
                last.then_inc(hT_ps, 1)
                pe.wait_ge(hT_ready, n + 1)

            def project(n, g):
                m = n * GROUPS + g
                if n == 0:
                    pe.wait_ge(wq_in[g], 16)
                if m >= 2:
                    pe.wait_ge(f_done, m - 1)
                    pe.wait_ge(vb_ready, m - 1)
                for b in range(2):
                    c0 = (GH * g + 2 * b) * HW
                    for c in range(DC):
                        last = pe.matmul(pp[g % 2][:, 2 * b:2 * b + 2, 0:HW], hT[:, n % 2, c],
                                         wq[:, c, c0:c0 + 2 * HW].rearrange("p (h n) -> p h n", n=HW),
                                         start=(c == 0), stop=(c == DC - 1))
                last.then_inc(proj_done, 1)

            def read_out(n):
                s, t = n // T, n % T
                count = t + 1 if n < TILES - 1 else LAST_V + 1
                if n:
                    pe.wait_ge(oT_ready, n)
                for k in range(count):
                    if n == TILES - 1 and k == LAST_V:
                        pe.wait_ge(po_slot_v, 3)
                        row = prod[:, 0].rearrange("p h c -> p (h c)")
                    else:
                        pe.wait_ge(po_slot, po_slots(n, k + 1))
                        row = prodp[:, at(s, read_order(n)[k])].rearrange("p h c -> p (h c)")
                    for c in range(INNER // P):
                        last = pe.matmul(po[:, c], row[:, c * P:(c + 1) * P], ident[:],
                                         start=(k == 0 and c % 4 == 0), stop=(k == count - 1),
                                         skip_group_check=True)
                    last.then_inc(po_read, 1)
                pe.wait_ge(oT_ready, n + 1)
                if n:
                    pe.wait_ge(res_done, n)
                for c in range(INNER // P):
                    last = pe.matmul(pa[:], oT[:, c], wo[:, c], start=(c == 0), stop=(c == INNER // P - 1))
                last.then_inc(att_done, 1)

            transpose_h(0)
            for g in range(GROUPS):
                project(0, g)
            pe.wait_ge(wo_in, 16)
            for n in range(TILES):
                if n + 1 < TILES:
                    transpose_h(n + 1)
                    for g in range(GROUPS):
                        project(n + 1, g)
                if n:
                    read_out(n - 1)
            read_out(TILES - 1)

        @block.vector
        def _(dve):
            for s in range(HALVES):
                half = slice(s * T, (s + 1) * T)
                base = s * (T + 6)
                dve.wait_ge(x_in[s], 16)
                for m in range(s * T, (s + 1) * T):
                    dve.bn_stats(st[:, m], hall[:, m]).then_inc(ln, 1)
                dve.wait_ge(ln, base + T)
                for m in range(s * T, (s + 1) * T):
                    last = dve.bn_aggr(mv[:, m], st[:, m])
                last.then_inc(ln, 1)
                dve.wait_ge(ln, base + T + 1)
                dve.tensor_scalar(ve[:, half], mv[:, half, 1], EPS, None, ALU.add).then_inc(var_ready, 1)
                dve.wait_ge(sd_ready, s + 1)
                dve.reciprocal(rstd[:, half], rstd[:, half]).then_inc(ln, 1)
                dve.wait_ge(ln, base + T + 2)
                newton_rsqrt(dve, ve[:, half], rstd[:, half], tmp[:, half], ln, base + T + 2)
                for m in range(s * T, (s + 1) * T):
                    last = dve.tensor_scalar(hall[:, m], hall[:, m], mv[:, m, 0:1], rstd[:, m:m + 1],
                                             ALU.subtract, ALU.mult)
                last.then_inc(h_ready, 1)

            def features(n, g):
                s, t = n // T, n % T
                ps = pp[g % 2]
                hs = slice(GH * g, GH * g + GH)
                dve.wait_ge(e_ready, n * GROUPS + g + 1)
                dve.scalar_tensor_tensor(qcur[:, t % 2, hs], ps[:, :, 0:DH], 1.0, ebuf[:, g % 2, :, 0:DH],
                                         ALU.add, ALU.max)
                dve.scalar_tensor_tensor(kall[:, key_at(s, t), hs], ps[:, :, DH:2 * DH], 1.0, ebuf[:, g % 2, :, DH:2 * DH],
                                         ALU.add, ALU.max).then_inc(f_done, 1)

            def residual(n):
                dve.wait_ge(att_done, n + 1)
                dve.tensor_tensor(hall[:, n], pa[:], hall[:, n], ALU.add).then_inc(res_done, 1)

            def betas(n):
                b = n % 2
                dve.wait_ge(vb_ready, (n + 1) * GROUPS)
                dve.tensor_scalar(eb[:, b], eb[:, b], 1.0, None, ALU.add).then_inc(norm, 1)
                dve.wait_ge(norm, 6 * n + 1)
                if n >= 2:
                    dve.wait_ge(bv_ready, n - 1)
                dve.reciprocal(beta[:, b], eb[:, b]).then_inc(beta_ready, 1)

            def norms(n):
                b, own = n % 2, key_at(n // T, n % T)
                dve.wait_ge(f_done, (n + 1) * GROUPS)
                dve.reduce_sum(nrm[:, 0], qcur[:, b], AX)
                dve.reduce_sum(nrm[:, 1], kall[:, own], AX).then_inc(norm, 1)
                dve.wait_ge(norm, 6 * n + 2)
                dve.reciprocal(rq[:, b], nrm[:, 0]).then_inc(norm, 1)
                dve.reciprocal(rk[:, own], nrm[:, 1]).then_inc(norm, 1)
                dve.wait_ge(norm, 6 * n + 4)
                dve.wait_ge(beta_ready, n + 1)
                dve.tensor_scalar(rq[:, b], rq[:, b], FAST_SCALE, None, ALU.mult).then_inc(norm, 1)
                dve.scalar_tensor_tensor(nbk[:, b], beta[:, b], -1.0, rk[:, own], ALU.mult, ALU.mult).then_inc(norm, 1)

            for g in range(GROUPS):
                features(0, g)
            betas(0)
            norms(0)
            for n in range(TILES):
                s, t = n // T, n % T
                before, keys = places(s, 0, t), key_places(s, 0, t)
                upto, keys_upto = places(s, 0, t + 1), key_places(s, 0, t + 1)
                ahead = n + 1 < TILES
                if ahead:
                    features(n + 1, 0)
                    features(n + 1, 1)
                if t:
                    k0 = (s * (T - 1) + t - 1) * 5
                    own = t - KK_POOL[t]
                    dve.tensor_tensor(prod[:, places(s, 0, own)], kall[:, key_places(s, 0, own)],
                                      kall[:, key_at(s, t)].unsqueeze(1).to_broadcast([P, own, NH, DH]),
                                      ALU.mult).then_inc(kk, 1)
                    dve.wait_ge(kk, k0 + 1)
                    if KK_POOL[t]:
                        dve.wait_ge(kk_pool, kk_steps(n))
                    dve.reduce_sum(ck[:, before], prod[:, before], AX).then_inc(kk, 1)
                    dve.wait_ge(kk, k0 + 2)
                    dve.tensor_tensor(ck[:, before], ck[:, before], rk[:, keys], ALU.mult).then_inc(kk, 1)
                    dve.wait_ge(kk, k0 + 3)
                    dve.wait_ge(norm, 6 * n + 6)
                    dve.tensor_tensor(ck[:, before], ck[:, before], nbk[:, t % 2].unsqueeze(1).to_broadcast([P, t, NH]),
                                      ALU.mult).then_inc(kk, 1)
                elif s:
                    dve.wait_ge(po_slot, po_slots(n - 1, 1))
                if t == 0:
                    dve.tensor_tensor(dall[:, at(s, 0)], vbuf[:], beta[:, 0].unsqueeze(2).to_broadcast([P, NH, DH]),
                                      ALU.mult).then_inc(bv_ready, 1)
                if ahead:
                    features(n + 1, 2)
                    if not t:
                        features(n + 1, 3)
                        betas(n + 1)
                if t == 0:
                    dve.wait_ge(norm, 6 * n + 6)
                    dve.wait_ge(bv_ready, n + 1)
                    dve.sem_inc(delta_ready, 1)
                else:
                    dve.wait_ge(kk, k0 + 4)
                    dve.tensor_tensor(prod[:, before], dall[:, before],
                                      ck[:, before].unsqueeze(3).to_broadcast([P, t, NH, DH]),
                                      ALU.mult).then_inc(kk, 1)
                    if ahead:
                        features(n + 1, 3)
                        betas(n + 1)
                    dve.wait_ge(kk, k0 + 5)
                    dve.wait_ge(bv_ready, n + 1)
                    if s:
                        dve.wait_ge(po_slot, po_slots(s * T - 1, t + 1))
                    dve.reduce_sum(dall[:, at(s, t)].rearrange("p h c -> p (h c)"),
                                   prod[:, upto].rearrange("p s h c -> p (h c) s"),
                                   AX).then_inc(delta_ready, 1)
                if ahead:
                    norms(n + 1)
                if t == 1 and s:
                    residual(n - 2)
                if t:
                    residual(n - 1)
                if t:
                    dots = prodp[:, upto]
                    dve.wait_ge(qk_mul, dot_parts(n))
                else:
                    dots = prod[:, upto]
                    dve.tensor_tensor(prod[:, at(s, 0)], kall[:, key_at(s, 0)], qcur[:, 0], ALU.mult).then_inc(qk0_mul, 1)
                    dve.wait_ge(qk0_mul, s + 1)
                dve.reduce_sum(cq[:, t % 2, upto], dots, AX).then_inc(cq_step, 1)
                dve.wait_ge(cq_step, 2 * n + 1)
                dve.tensor_tensor(cq[:, t % 2, upto], cq[:, t % 2, upto], rk[:, keys_upto],
                                  ALU.mult).then_inc(cq_step, 1)
                dve.wait_ge(cq_step, 2 * n + 2)
                dve.tensor_tensor(cq[:, t % 2, upto], cq[:, t % 2, upto],
                                  rq[:, t % 2].unsqueeze(1).to_broadcast([P, t + 1, NH]),
                                  ALU.mult).then_inc(cq_ready, 1)
            dve.wait_ge(cq_ready, TILES)
            share = places(HALVES - 1, LAST_V, T)
            dve.tensor_tensor(prod[:, share], dall[:, share],
                              cq[:, (T - 1) % 2, share].unsqueeze(3).to_broadcast([P, T - LAST_V, NH, DH]),
                              ALU.mult).then_inc(po_slot_v, 1)
            dve.wait_ge(po_slot_v, 1)
            dve.tensor_tensor(prod[:, 0:2], prod[:, 0:2], prod[:, 2:4], ALU.add).then_inc(po_slot_v, 1)
            dve.wait_ge(po_slot_v, 2)
            dve.tensor_tensor(prod[:, 0], prod[:, 0], prod[:, 1], ALU.add).then_inc(po_slot_v, 1)
            residual(TILES - 1)


WQ, WK, WKS, WV, WVS = 0, 2, 3, 4, 5
W_DMAS = 7


def load_head_weights(sp, w_q, w_k, w_v, wst, h, w_in):
    cols = bass.ds(h * XD, XD)
    sp.dma_start(wst[:, WQ:WQ + 2], w_q.rearrange("(c p) n -> p c n", p=P)[:, :, cols]).then_inc(w_in, 16)
    for at, src in ((WK, w_k), (WV, w_v)):
        sp.dma_start(wst[:, at], src[0:P, cols]).then_inc(w_in, 16)
        for r in (0, C2):
            sp.dma_start(wst[r:r + C2, at + 1], src[P:CD, cols]).then_inc(w_in, 16)


def cross_inputs_block(nc, x, ctx_in, ln_g, ln_b, bout, w_q, w_k, w_v, ident, hall, zT, cT, cS, wst, w):
    with ExitStack() as ctx:
        def sb(name, shape, dt=F32):
            return ctx.enter_context(nc.sbuf_tensor(name, shape, dt))

        def sem(name):
            return ctx.enter_context(nc.semaphore(name))

        xres = sb("ci_x", [P, TILES, D])
        z = sb("ci_z", [P, TILES, D])
        cnat = sb("ci_ctx", [P, JT, 2 * P])
        gam = sb("ci_gamma", [P, D])
        bet = sb("ci_beta", [P, D])
        bo = sb("ci_bout", [P, D])
        st = sb("ci_st", [P, TILES, 6])
        mv = sb("ci_mv", [P, TILES, 2])
        ve = sb("ci_ve", [P, 2, TILES])
        rstd = sb("ci_rstd", [P, 2, TILES])
        tmp = sb("ci_tmp", [P, TILES])
        shift = sb("ci_shift", [P, T])
        tp = [ctx.enter_context(nc.psum_tensor(f"ci_tp{i}", [P, 512], F32)) for i in range(4)]

        x_in = [sem(f"ci_x_in{s}") for s in range(HALVES)]
        c_in, v_in = sem("ci_c_in"), sem("ci_v_in")
        xb_ready = sem("ci_xb")
        ln = sem("ci_ln")
        var_ready, sd_ready = sem("ci_var"), sem("ci_sd")
        z_ready = [sem(f"ci_z_ready{s}") for s in range(HALVES)]
        shift_ready = sem("ci_shift_ready")
        rstd_ready = sem("ci_rstd_ready")
        x1_ready = sem("ci_x1")
        x1_pool = sem("ci_x1_pool")
        tp_full, tp_hi, tp_lo = sem("ci_full"), sem("ci_hi"), sem("ci_lo")
        bout_added = sem("ci_bout_added")
        w_in, w_hi, w_lo = sem("ci_w_in"), sem("ci_w_hi"), sem("ci_w_lo")
        xs = x.rearrange("t (s p) d -> s p t d", p=P)
        CTX_BANKS = 2 * JT // 4
        Z_BANKS = DC * TILES // 4

        def split_into(n):
            q = slice(n % 4 * 512, n % 4 * 512 + 512)
            if n < JT // 4:
                return [a[:, q] for a in cT]
            if n < CTX_BANKS:
                return [cS[:, q], cS[C2:P, q]]
            return [a[:, (n - CTX_BANKS) // 4, q] for a in zT]

        block = ctx.enter_context(nc.Block())

        @block.sync
        def _(sp):
            for dst, src in ((gam, ln_g), (bet, ln_b), (bo, bout)):
                sp.dma_start(dst[:], src.unsqueeze(0).to_broadcast([P, D])).then_inc(v_in, 16)
            for s in range(HALVES):
                sp.dma_start(xres[:, s * T:(s + 1) * T, :], xs[s]).then_inc(x_in[s], 16)
            rows = ctx_in.rearrange("a b c -> (a b) c").rearrange("(m p) c -> p m c", p=P)
            sp.dma_start(cnat[:, :, 0:CD], rows).then_inc(c_in, 16)
            sp.dma_start(cnat[:, :, CD:2 * P], rows[:, :, P:CD]).then_inc(c_in, 16)
            load_head_weights(sp, w_q, w_k, w_v, wst, 0, w_in)

        @block.gpsimd
        def _(pool):
            pool.wait_ge(v_in, 48)
            for s in range(HALVES):
                half = slice(s * T, (s + 1) * T)
                pool.wait_ge(x_in[s], 16)
                pool.tensor_tensor(xres[:, half], xres[:, half], bet[:].unsqueeze(1).to_broadcast([P, T, D]),
                                   ALU.add).then_inc(xb_ready, 1)
            pool.wait_ge(xb_ready, HALVES)
            pool.wait_ge(rstd_ready, 1)
            for i in range(2):
                part = slice(T + i * T // 2, T + (i + 1) * T // 2)
                pool.tensor_tensor(hall[:, part], hall[:, part],
                                   rstd[:, 0, part].unsqueeze(2).to_broadcast([P, T // 2, D]),
                                   ALU.mult).then_inc(x1_pool, 1)
                pool.wait_ge(x1_pool, 2 * i + 1)
                pool.tensor_tensor(hall[:, part], hall[:, part], xres[:, part], ALU.add).then_inc(x1_pool, 1)
            pool.wait_ge(w_hi, 1)
            pool.tensor_tensor(w[LO][:], wst[:], w[HI][:].bitcast(F32), ALU.subtract).then_inc(w_lo, 1)
            for s in range(HALVES):
                half = slice(s * T, (s + 1) * T)
                pool.wait_ge(z_ready[s], 1)
                pool.tensor_tensor(hall[:, half], hall[:, half], bo[:].unsqueeze(1).to_broadcast([P, T, D]),
                                   ALU.add).then_inc(bout_added, 1)

        @block.vector
        def _(dve):
            def low_part(n):
                hi, lo = split_into(n)
                rows = slice(C2, P) if JT // 4 <= n < CTX_BANKS else slice(0, P)
                dve.wait_ge(tp_hi, n + 1)
                dve.tensor_tensor(lo, tp[n % 4][rows], hi[rows].bitcast(F32), ALU.subtract).then_inc(tp_lo, 1)

            def row_stats(tiles):
                for m in tiles:
                    dve.bn_stats(st[:, m], hall[:, m]).then_inc(ln, 1)

            def variances(stage, base):
                dve.wait_ge(ln, base)
                for m in range(TILES):
                    last = dve.bn_aggr(mv[:, m], st[:, m])
                last.then_inc(ln, 1)
                dve.wait_ge(ln, base + 1)
                dve.tensor_scalar(ve[:, stage], mv[:, :, 1], EPS, None, ALU.add).then_inc(var_ready, 1)

            def deviations(stage, base):
                dve.wait_ge(sd_ready, stage + 1)
                dve.reciprocal(rstd[:, stage], rstd[:, stage]).then_inc(ln, 1)
                dve.wait_ge(ln, base + 2)
                newton_rsqrt(dve, ve[:, stage], rstd[:, stage], tmp[:], ln, base + 2)

            row_stats(range(TILES))
            variances(0, TILES)
            dve.wait_ge(v_in, 48)
            for m in range(TILES):
                dve.scalar_tensor_tensor(hall[:, m], hall[:, m], mv[:, m, 0:1], gam[:],
                                         ALU.subtract, ALU.mult).then_inc(x1_ready, 1)
            deviations(0, TILES)
            base = TILES + 6
            dve.wait_ge(x1_ready, TILES)
            dve.sem_inc(rstd_ready, 1)
            dve.wait_ge(xb_ready, 1)
            for m in range(T):
                dve.scalar_tensor_tensor(hall[:, m], hall[:, m], rstd[:, 0, m:m + 1], xres[:, m],
                                         ALU.mult, ALU.add).then_inc(x1_ready, 1)
            dve.wait_ge(x1_ready, TILES + T)
            row_stats(range(T))
            dve.wait_ge(x1_pool, 2)
            row_stats(range(T, T + T // 2))
            dve.wait_ge(x1_pool, 4)
            row_stats(range(T + T // 2, TILES))
            variances(1, base + TILES)
            deviations(1, base + TILES)
            dve.scalar_tensor_tensor(shift[:], mv[:, T:TILES, 0], -1.0, rstd[:, 1, T:TILES],
                                     ALU.mult, ALU.mult).then_inc(shift_ready, 1)
            for m in range(T):
                last = dve.tensor_scalar(z[:, m], hall[:, m], mv[:, m, 0:1], rstd[:, 1, m:m + 1],
                                         ALU.subtract, ALU.mult)
            last.then_inc(z_ready[0], 1)
            for n in range(CTX_BANKS + Z_BANKS):
                low_part(n)

        @block.tensor
        def _(pe):
            pe.wait_ge(c_in, 32)
            for n in range(CTX_BANKS + Z_BANKS):
                if n == CTX_BANKS:
                    pe.wait_ge(z_ready[0], 1)
                if n == CTX_BANKS + Z_BANKS // 4:
                    pe.wait_ge(z_ready[1], 1)
                if n >= 4:
                    pe.wait_ge(tp_lo, n - 3)
                for k in range(4):
                    if n < CTX_BANKS:
                        c, m = n // (JT // 4), n % (JT // 4) * 4 + k
                        src = cnat[:, m, c * P:(c + 1) * P]
                    else:
                        c, m = (n - CTX_BANKS) // (TILES // 4), (n - CTX_BANKS) % (TILES // 4) * 4 + k
                        src = z[:, m, c * P:(c + 1) * P]
                    last = pe.transpose(tp[n % 4][:, k * P:(k + 1) * P], src, ident[:])
                last.then_inc(tp_full, 1)

        @block.scalar
        def _(act):
            def root(stage):
                act.wait_ge(var_ready, stage + 1)
                act.activation(rstd[:, stage], ve[:, stage], ACT.Sqrt).then_inc(sd_ready, 1)

            def high_part(n):
                act.wait_ge(tp_full, n + 1)
                act.activation(split_into(n)[HI], tp[n % 4][:], ACT.Copy).then_inc(tp_hi, 1)

            root(0)
            for n in range(4):
                high_part(n)
            root(1)
            act.wait_ge(shift_ready, 1)
            for m in range(T, TILES):
                last = act.activation(z[:, m], hall[:, m], ACT.Identity, bias=shift[:, m - T:m - T + 1],
                                      scale=rstd[:, 1, m:m + 1])
            last.then_inc(z_ready[1], 1)
            act.wait_ge(w_in, 16 * W_DMAS)
            act.activation(w[HI][:], wst[:], ACT.Copy).then_inc(w_hi, 1)
            for n in range(4, CTX_BANKS + Z_BANKS):
                high_part(n)


def cross_attention_block(nc, w_q, w_k, w_v, w_out, ident, hall, zT, cT, cS, wst, w, stats, xe):
    with ExitStack() as ctx:
        def sb(name, shape, dt=F32):
            return ctx.enter_context(nc.sbuf_tensor(name, shape, dt))

        def sem(name):
            return ctx.enter_context(nc.semaphore(name))

        woh = sb("xa_wout", [P, D])
        qT = [sb(f"xa_qT{i}", [P, TOK], F32R) for i in (HI, LO)]
        kT = [sb(f"xa_kT{i}", [P, TOK], F32R) for i in (HI, LO)]
        v = [sb(f"xa_v{i}", [P, TOK], F32R) for i in (HI, LO)]
        RING, HALF = 3, TOK // 2
        probs = sb("xa_probs", [P, RING, HALF])
        pT = [sb(f"xa_pT{i}", [P, 2, JT, 2 * P], F32R) for i in (HI, LO)]
        oT = sb("xa_oT", [P, 2 * P])
        mx = sb("xa_mx", [P, 2])
        nb = sb("xa_nb", [P, 2])
        rs = stats
        rinv = sb("xa_rinv", [P, TILES])
        bn = sb("xa_bn", [P, 6])
        nobody = sb("xa_nobody", [P, 2])

        S = ctx.enter_context(nc.psum_tensor("xa_S", [P, 4, 512], F32))
        tb = [ctx.enter_context(nc.psum_tensor(f"xa_tb{i}", [P, 512], F32)) for i in range(2)]
        O = ctx.enter_context(nc.psum_tensor("xa_O", [P, 512], F32))
        Y = ctx.enter_context(nc.psum_tensor("xa_Y", [P, 512], F32))

        w_in, wo_in = sem("xa_w_in"), sem("xa_wo_in")
        w_hi, w_lo = sem("xa_w_hi"), sem("xa_w_lo")
        proj_mm, proj_hi, proj_lo = sem("xa_proj_mm"), sem("xa_proj_hi"), sem("xa_proj_lo")
        v_mm, v_hi, v_lo = sem("xa_v_mm"), sem("xa_v_hi"), sem("xa_v_lo")
        sim_done = sem("xa_sim")
        mx_ready, nb_ready = sem("xa_mx_ready"), sem("xa_nb_ready")
        exp_done = sem("xa_exp")
        t_mm = sem("xa_t_mm")
        hi_ready, lo_ready = sem("xa_hi"), sem("xa_lo")
        av_done = sem("xa_av")
        oT_ready = sem("xa_oT_ready")
        y_mm, y_used = sem("xa_y_mm"), sem("xa_y_used")
        r_step = sem("xa_r_step")
        ln = sem("xa_ln")
        nobody_set, filled = sem("xa_nobody_set"), sem("xa_filled")

        QK = 8
        VU = 4
        V_UNITS = [[0, 1], [2], [3]] + [[]] * (TILES - 3)
        PAIRS = TILES // 2
        PARTS = ((HI, HI), (HI, LO), (LO, HI))
        block = ctx.enter_context(nc.Block())

        @block.sync
        def _(sp):
            def load_out_weights(h):
                sp.dma_start(woh[:], w_out[bass.ds(h * XD, XD), :]).then_inc(wo_in, 16)

            load_out_weights(0)
            sp.wait_ge(nobody_set, 1)
            slots = xe.rearrange("(p r) d -> p r d", p=P)
            for c in range(0, GATE, P):
                sp.dma_start(slots[:, :, c:c + P], ident[:].unsqueeze(1).to_broadcast([P, E * CAP // P, P])) \
                    .then_inc(filled, 16)
            sp.dma_start(slots[:, :, GATE:ROW], nobody[:].unsqueeze(1).to_broadcast([P, E * CAP // P, ROW - GATE])) \
                .then_inc(filled, 16)
            with sp.Fori(0, XH - 1) as h:
                sp.wait_ge(w_hi, h + 1)
                sp.wait_ge(w_lo, h + 1)
                load_head_weights(sp, w_q, w_k, w_v, wst, h + 1, w_in)
                sp.wait_ge(y_mm, 1 + (h + 1) * PAIRS)
                load_out_weights(h + 1)
            sp.wait_ge(filled, 16 * (GATE // P + 1))

        @block.gpsimd
        def _(pool):
            pool.memset(nobody[:], float(2 * TOK)).then_inc(nobody_set, 1)

        @block.tensor
        def _(pe):
            pe.sem_inc(y_mm, 1)

            def project_qk(h, u):
                blk = slice(u % 4 * 512, u % 4 * 512 + 512)
                if u == 0:
                    pe.wait_ge(w_lo, h + 1)
                if u >= 4:
                    pe.wait_ge(proj_lo, h * QK + u - 3)
                if u < 4:
                    ops = [(w[a][:, WQ + c], zT[b][:, c, blk]) for c in range(DC) for a, b in PARTS]
                else:
                    ops = [(w[a][:, WK], cT[b][:, blk]) for a, b in PARTS]
                    ops += [(w[HI][:, WKS], cS[:, blk]), (w[LO][0:C2, WKS], cS[0:C2, blk])]
                for n, (a, b) in enumerate(ops):
                    last = pe.matmul(S[:, u % 4], a, b, start=(n == 0), stop=(n == len(ops) - 1))
                last.then_inc(proj_mm, 1)

            def project_v(h, u):
                dst = (Y, O)[u % 2]
                if u == 0:
                    pe.wait_ge(y_used, 1 + h * PAIRS)
                elif u == 1:
                    pe.wait_ge(oT_ready, 1 + h * PAIRS)
                else:
                    pe.wait_ge(v_lo, h * VU + u - 1)
                for k in range(4):
                    j = slice(u * 512 + k * P, u * 512 + (k + 1) * P)
                    ops = [(cT[a][:, j], w[b][:, WV]) for a, b in PARTS]
                    ops += [(cS[:, j], w[HI][:, WVS]), (cS[0:C2, j], w[LO][0:C2, WVS])]
                    for n, (a, b) in enumerate(ops):
                        last = pe.matmul(dst[:, k * P:(k + 1) * P], a, b, start=(n == 0), stop=(n == len(ops) - 1))
                last.then_inc(v_mm, 1)

            def scores(h, i):
                q = slice(i * P, (i + 1) * P)
                if i == 0:
                    pe.wait_ge(proj_lo, (h + 1) * QK)
                for u in range(2):
                    if i:
                        pe.wait_ge(exp_done, h * 2 * TILES + 2 * i - 1 + u)
                    for n, (a, b) in enumerate(PARTS):
                        for k in (2 * u, 2 * u + 1):
                            last = pe.matmul(S[:, k], qT[a][:, q], kT[b][:, k * 512:(k + 1) * 512],
                                             start=(n == 0), stop=(n == 2))
                    last.then_inc(sim_done, 1)

            def transposes(h, i, q):
                unit = 2 * i + q // 2
                if q % 2 == 0:
                    pe.wait_ge(exp_done, h * 2 * TILES + unit + 1)
                if i or q >= 2:
                    pe.wait_ge(lo_ready, h * 4 * TILES + 4 * i + q - 1)
                for k in range(4):
                    j = (4 * (q % 2) + k) * P
                    last = pe.transpose(tb[q % 2][:, k * P:(k + 1) * P], probs[:, unit % RING, j:j + P], ident[:])
                last.then_inc(t_mm, 1)

            def weighted(h, p, half):
                if half == 0:
                    if p == 0:
                        pe.wait_ge(v_lo, (h + 1) * VU)
                    pe.wait_ge(lo_ready, h * 4 * TILES + 8 * (p + 1))
                    pe.wait_ge(oT_ready, 1 + h * PAIRS + p)
                for j in range(half * JT // 2, (half + 1) * JT // 2):
                    vj = slice(j * P, (j + 1) * P)
                    for n, (a, b) in enumerate(PARTS):
                        last = pe.matmul(O[:, 0:2 * P], v[a][:, vj], pT[b][:, p % 2, j],
                                         start=(j == 0 and n == 0), stop=(j == JT - 1 and n == 2))
                if half:
                    last.then_inc(av_done, 1)

            def out_project(h, p):
                if p == 0:
                    pe.wait_ge(wo_in, h * 16 + 16)
                pe.wait_ge(oT_ready, 1 + h * PAIRS + p + 1)
                pe.wait_ge(y_used, 1 + h * PAIRS + p)
                for k in range(2):
                    last = pe.matmul(Y[:, k * D:(k + 1) * D], oT[:, k * P:(k + 1) * P], woh[:], start=True, stop=True)
                last.then_inc(y_mm, 1)

            def head(h, more):
                for i in range(TILES):
                    scores(h, i)
                    if i:
                        transposes(h, i - 1, 0)
                        transposes(h, i - 1, 1)
                    for u in V_UNITS[i]:
                        project_v(h, u)
                    if i >= 3:
                        weighted(h, (i - 3) // 2, (i - 3) % 2)
                    if i:
                        transposes(h, i - 1, 2)
                        transposes(h, i - 1, 3)
                    if i >= 5 and i % 2:
                        out_project(h, (i - 5) // 2)
                weighted(h, PAIRS - 2, 1)
                if more:
                    pe.wait_ge(exp_done, (h + 1) * 2 * TILES - 1)
                for g in (0, 2):
                    transposes(h, TILES - 1, g)
                    transposes(h, TILES - 1, g + 1)
                    if more:
                        project_qk(h + 1, g)
                        project_qk(h + 1, g + 1)
                weighted(h, PAIRS - 1, 0)
                out_project(h, PAIRS - 2)
                if more:
                    for u in range(4, QK):
                        project_qk(h + 1, u)
                weighted(h, PAIRS - 1, 1)
                out_project(h, PAIRS - 1)

            for u in range(QK):
                project_qk(0, u)
            with pe.Fori(0, XH - 1) as h:
                head(h, True)
            head(XH - 1, False)

        @block.scalar
        def _(act):
            act.sem_inc(oT_ready, 1)
            act.sem_inc(w_hi, 1)

            def split_weights(h):
                act.wait_ge(w_in, h * 16 * W_DMAS)
                act.activation(w[HI][:], wst[:], ACT.Copy).then_inc(w_hi, 1)

            def split_qk(h, u):
                act.wait_ge(proj_mm, h * QK + u + 1)
                act.activation((qT, kT)[u // 4][HI][:, u % 4 * 512:u % 4 * 512 + 512], S[:, u % 4], ACT.Copy) \
                    .then_inc(proj_hi, 1)

            def split_v(h, u):
                act.wait_ge(v_mm, h * VU + u + 1)
                act.activation(v[HI][:, u * 512:(u + 1) * 512], (Y, O)[u % 2][:], ACT.Copy).then_inc(v_hi, 1)

            def high_part(h, i, q):
                act.wait_ge(t_mm, h * 4 * TILES + 4 * i + q + 1)
                act.activation(pT[HI][:, i // 2 % 2, 4 * q:4 * q + 4, i % 2 * P:(i % 2 + 1) * P],
                               tb[q % 2][:].rearrange("p (k n) -> p k n", k=4), ACT.Copy).then_inc(hi_ready, 1)

            def exponentials(h, i):
                act.wait_ge(nb_ready, h * TILES + i + 1)
                for u in range(2):
                    unit = 2 * i + u
                    if unit >= RING:
                        act.wait_ge(t_mm, h * 4 * TILES + 2 * (unit - RING) + 2)
                    act.activation(probs[:, unit % RING], S[:, 2 * u:2 * u + 2].rearrange("p a b -> p (a b)"),
                                   ACT.Exp, bias=nb[:, i % 2:i % 2 + 1], scale=SOFT_SCALE,
                                   accum_out=rs[:, i, u:u + 1]).then_inc(exp_done, 1)

            def copy_oT(h, p):
                act.wait_ge(av_done, h * PAIRS + p + 1)
                act.wait_ge(y_mm, 1 + h * PAIRS + p)
                act.activation(oT[:], O[:, 0:2 * P], ACT.Copy).then_inc(oT_ready, 1)

            def head(h, more):
                for i in range(TILES):
                    if i:
                        high_part(h, i - 1, 0)
                        high_part(h, i - 1, 1)
                    exponentials(h, i)
                    if i:
                        high_part(h, i - 1, 2)
                        high_part(h, i - 1, 3)
                    for u in V_UNITS[i]:
                        split_v(h, u)
                    if more and i == 7:
                        act.wait_ge(v_mm, (h + 1) * VU)
                        split_weights(h + 1)
                    if i >= 4 and i % 2 == 0:
                        copy_oT(h, (i - 4) // 2)
                for g in (0, 2):
                    high_part(h, TILES - 1, g)
                    if g == 0:
                        copy_oT(h, PAIRS - 2)
                    high_part(h, TILES - 1, g + 1)
                    if more:
                        split_qk(h + 1, g)
                        split_qk(h + 1, g + 1)
                if more:
                    for u in range(4, QK):
                        split_qk(h + 1, u)
                copy_oT(h, PAIRS - 1)

            for u in range(QK):
                split_qk(0, u)
            with act.Fori(0, XH - 1) as h:
                head(h, True)
            head(XH - 1, False)

        @block.vector
        def _(dve):
            dve.sem_inc(y_used, 1)
            dve.sem_inc(w_lo, 1)

            def split_weights(h):
                dve.wait_ge(w_hi, h + 1)
                dve.tensor_tensor(w[LO][:], wst[:], w[HI][:].bitcast(F32), ALU.subtract).then_inc(w_lo, 1)

            def split_qk(h, u):
                dst, blk = (qT, kT)[u // 4], slice(u % 4 * 512, u % 4 * 512 + 512)
                dve.wait_ge(proj_hi, h * QK + u + 1)
                dve.tensor_tensor(dst[LO][:, blk], S[:, u % 4], dst[HI][:, blk].bitcast(F32),
                                  ALU.subtract).then_inc(proj_lo, 1)

            def split_v(h, u):
                blk = slice(u * 512, (u + 1) * 512)
                dve.wait_ge(v_hi, h * VU + u + 1)
                dve.tensor_tensor(v[LO][:, blk], (Y, O)[u % 2][:], v[HI][:, blk].bitcast(F32),
                                  ALU.subtract).then_inc(v_lo, 1)

            def low_part(h, i, q):
                dst = (slice(None), i // 2 % 2, slice(4 * q, 4 * q + 4), slice(i % 2 * P, (i % 2 + 1) * P))
                dve.wait_ge(hi_ready, h * 4 * TILES + 4 * i + q + 1)
                dve.tensor_tensor(pT[LO][dst], tb[q % 2][:].rearrange("p (k n) -> p k n", k=4),
                                  pT[HI][dst].bitcast(F32), ALU.subtract).then_inc(lo_ready, 1)

            def maxima(h, i):
                for u in range(2):
                    dve.wait_ge(sim_done, h * 2 * TILES + 2 * i + u + 1)
                    dve.reduce_max(mx[:, u:u + 1], S[:, 2 * u:2 * u + 2].rearrange("p a b -> p (a b)"),
                                   AX).then_inc(mx_ready, 1)
                dve.wait_ge(mx_ready, h * 2 * TILES + 2 * i + 2)
                dve.tensor_scalar(nb[:, i % 2:i % 2 + 1], mx[:, 0:1], mx[:, 1:2], -SOFT_SCALE,
                                  ALU.max, ALU.mult).then_inc(nb_ready, 1)

            def add_output(h, p):
                r0 = h * 2 * PAIRS + 2 * p
                two = slice(2 * p, 2 * p + 2)
                dve.wait_ge(exp_done, h * 2 * TILES + 4 * p + 4)
                dve.tensor_tensor(rinv[:, two], rs[:, two, 0], rs[:, two, 1], ALU.add).then_inc(r_step, 1)
                dve.wait_ge(r_step, r0 + 1)
                dve.reciprocal(rinv[:, two], rinv[:, two]).then_inc(r_step, 1)
                dve.wait_ge(r_step, r0 + 2)
                dve.wait_ge(y_mm, 1 + h * PAIRS + p + 1)
                for m in (2 * p, 2 * p + 1):
                    last = dve.scalar_tensor_tensor(hall[:, m], Y[:, m % 2 * D:(m % 2 + 1) * D], rinv[:, m:m + 1],
                                                    hall[:, m], ALU.mult, ALU.add)
                last.then_inc(y_used, 1)

            def row_stats(p):
                dve.wait_ge(y_used, 1 + (XH - 1) * PAIRS + p + 1)
                for m in (2 * p, 2 * p + 1):
                    dve.bn_stats(bn[:], hall[:, m]).then_inc(ln, 1)
                    dve.wait_ge(ln, 2 * m + 1)
                    dve.bn_aggr(rs[:, m], bn[:]).then_inc(ln, 1)
                    dve.wait_ge(ln, 2 * m + 2)

            def head(h, more):
                for i in range(TILES):
                    maxima(h, i)
                    if i:
                        for q in range(4):
                            low_part(h, i - 1, q)
                    for u in V_UNITS[i]:
                        split_v(h, u)
                    if more and i == 7:
                        split_weights(h + 1)
                    if i >= 5 and i % 2:
                        add_output(h, (i - 5) // 2)
                        if not more:
                            row_stats((i - 5) // 2)
                for g in (0, 2):
                    low_part(h, TILES - 1, g)
                    low_part(h, TILES - 1, g + 1)
                    if more:
                        split_qk(h + 1, g)
                        split_qk(h + 1, g + 1)
                add_output(h, PAIRS - 2)
                if more:
                    for u in range(4, QK):
                        split_qk(h + 1, u)
                else:
                    row_stats(PAIRS - 2)
                add_output(h, PAIRS - 1)
                if not more:
                    row_stats(PAIRS - 1)

            for u in range(QK):
                split_qk(0, u)
            with dve.Fori(0, XH - 1) as h:
                head(h, True)
            head(XH - 1, False)


def expert_block(nc, r_w, w1, w2, out, ident, hall, stats, xe):
    with ExitStack() as ctx:
        def sb(name, shape, dt=F32):
            return ctx.enter_context(nc.sbuf_tensor(name, shape, dt))

        def pb(name, shape):
            return ctx.enter_context(nc.psum_tensor(name, shape, F32))

        def sem(name):
            return ctx.enter_context(nc.semaphore(name))

        FLAT = [s * T + t for t in range(T) for s in range(HALVES)]
        QUADS = TILES // 4
        z = sb("ex_z", [P, TILES, ROW])
        rw = sb("ex_rw", [P, DC, E])
        lg = sb("ex_lg", [P, TILES, E])
        ex = sb("ex_ex", [P, TILES, E])
        oh = sb("ex_oh", [P, TILES, E])
        pre = sb("ex_pre", [P, TILES, E])
        rank = sb("ex_rank", [P, E])
        mx = sb("ex_mx", [P, TILES])
        top = sb("ex_top", [P, TILES])
        gate = sb("ex_gate", [P, TILES])
        token = sb("ex_token", [P, TILES], I32)
        pos = sb("ex_pos", [P, TILES])
        slot = sb("ex_slot", [P, TILES])
        sloti = sb("ex_sloti", [P, TILES], I32)
        ones = sb("ex_ones", [P, P])
        before = sb("ex_before", [P, P])
        ve = sb("ex_ve", [P, TILES])
        rstd = sb("ex_rstd", [P, TILES])
        tmp = sb("ex_tmp", [P, TILES])
        w1s = [sb(f"ex_w1s{i}", [P, DC, F]) for i in range(2)]
        w2s = [sb(f"ex_w2s{i}", [P, FC, D]) for i in range(2)]
        w1p = [[sb(f"ex_w1p{i}{a}", [P, DC, F], F32R) for a in (HI, LO)] for i in range(2)]
        w2p = [[sb(f"ex_w2p{i}{a}", [P, FC, D], F32R) for a in (HI, LO)] for i in range(2)]
        xn = [sb(f"ex_xn{i}", [P, CT, ROW]) for i in range(2)]
        xT = [[sb(f"ex_xT{i}{a}", [P, DC, CAP], F32R) for a in (HI, LO)] for i in range(2)]
        hid = [[sb(f"ex_hid{i}{a}", [P, FC, CAP], F32R) for a in (HI, LO)] for i in range(2)]
        yb = [z[:, i * CT:(i + 1) * CT, 0:D] for i in range(2)]
        to = [sb(f"ex_to{i}", [P, CT], I32) for i in range(2)]
        zt = w2s[1][:].rearrange("p f d -> p (f d)").rearrange("p (a b n) -> p a b n", b=4, n=P)

        tp = [pb(f"ex_tp{i}", [P, 512]) for i in range(2)]
        H = [pb(f"ex_H{i}", [P, 2, CAP]) for i in range(FC // 2)]
        Yp = [pb(f"ex_Y{i}", [P, CT, D]) for i in range(2)]
        banks = (tp[0][:], tp[1][:], Yp[0][:].rearrange("p k d -> p (k d)"), Yp[1][:].rearrange("p k d -> p (k d)"))
        rp = [bank[:, 0:4 * E].rearrange("p (s t e) -> p s t e", s=HALVES, e=E) for bank in banks]

        x1_copied, x1_out = sem("ex_x1_copied"), sem("ex_x1_out")
        consts = sem("ex_consts")
        rw_in = sem("ex_rw_in")
        ln, var_ready, sd_ready = sem("ex_ln"), sem("ex_var"), sem("ex_sd")
        z_ready = sem("ex_z_ready")
        ztp = sem("ex_ztp")
        zt_ready = [sem(f"ex_zt_ready{c}") for c in range(DC)]
        logits = sem("ex_logits")
        shifted, expd = sem("ex_shifted"), sem("ex_expd")
        rt = sem("ex_rt")
        oh_ready, pos_mm, slot_ready = sem("ex_oh_ready"), sem("ex_pos_mm"), sem("ex_slot_ready")
        scattered = sem("ex_scattered")
        w1_in = [sem(f"ex_w1_in{i}") for i in range(2)]
        w2_in = [sem(f"ex_w2_in{i}") for i in range(2)]
        x_in = [sem(f"ex_x_in{i}") for i in range(2)]
        y_out = sem("ex_y_out")
        w1_hi, w1_lo, w2_hi, w2_lo = sem("ex_w1_hi"), sem("ex_w1_lo"), sem("ex_w2_hi"), sem("ex_w2_lo")
        y_mm = sem("ex_y_mm")
        y_ready, y_stored = sem("ex_y_ready"), sem("ex_y_stored")
        y_sent = sem("ex_y_sent")
        xtp, xT_hi, xT_lo = sem("ex_xtp"), sem("ex_xT_hi"), sem("ex_xT_lo")
        h_mm, gelu, hid_hi, hid_lo = sem("ex_h_mm"), sem("ex_gelu"), sem("ex_hid_hi"), sem("ex_hid_lo")

        HU = FC // 2
        PARTS = ((HI, HI), (HI, LO), (LO, HI))
        block = ctx.enter_context(nc.Block())

        def quad(a, q):
            steps = slice(2 * q, 2 * q + 2)
            if len(a.shape) == 3:
                return a.rearrange("p (s t) e -> p s t e", s=HALVES)[:, :, steps]
            return a.rearrange("p (s t) -> p s t", s=HALVES)[:, :, steps]

        def experts(eng, body):
            with eng.Fori(0, E // 2 - 1) as ep:
                body(ep * 2, 0, 2)
                body(ep * 2 + 1, 1, 2)
            body(E - 2, 0, 1)
            body(E - 1, 1, 0)

        @block.sync
        def _(sp):
            def load_w1(e, i):
                sp.dma_start(w1s[i][:], w1[bass.ds(e, 1)].rearrange("e (c p) f -> p (e c) f", p=P)).then_inc(w1_in[i], 16)

            def load_w2(e, i):
                sp.dma_start(w2s[i][:], w2[bass.ds(e, 1)].rearrange("e (c p) d -> p (e c) d", p=P)).then_inc(w2_in[i], 16)

            def load_x(e, i):
                sp.dma_start(xn[i][:], xe[bass.ds(e * CAP, CAP)].rearrange("(k p) d -> p k d", p=P)).then_inc(x_in[i], 16)

            sp.dma_start(rw[:], r_w.rearrange("(c p) e -> p c e", p=P)).then_inc(rw_in, 16)
            load_w1(0, 0)
            load_w2(0, 0)
            load_w1(1, 1)
            for s in range(HALVES):
                sp.dma_start(out.rearrange("t (s p) d -> s p t d", p=P)[s], hall[:, s * T:(s + 1) * T]) \
                    .then_inc(x1_out, 16)
            sp.wait_ge(logits, TILES // 4)
            load_w2(1, 1)
            sp.wait_ge(scattered, 16 * TILES)
            for i in range(2):
                load_x(i, i)
            with sp.Fori(0, E // 2 - 1) as ep:
                for i in range(2):
                    e = ep * 2 + i
                    sp.wait_ge(w1_lo, e + 1)
                    load_w1(e + 2, i)
                    sp.wait_ge(w2_lo, e + 1)
                    load_w2(e + 2, i)
                    sp.wait_ge(y_ready, 2 + e + 1)
                    load_x(e + 2, i)

        @block.gpsimd
        def _(pool):
            def split_low(e, i):
                pool.wait_ge(w1_hi, e + 1)
                pool.tensor_tensor(w1p[i][LO][:], w1s[i][:], w1p[i][HI][:].bitcast(F32),
                                   ALU.subtract).then_inc(w1_lo, 1)

            pool.memset(ones[:], 1.0).then_inc(consts, 1)
            pool.wait_ge(consts, 1)
            pool.affine_select(out=before[:], in_=ones[:], compare_op=ALU.is_gt, fill=0.0, base=0,
                               pattern=[[1, P]], channel_multiplier=-1).then_inc(consts, 1)
            for e in range(E):
                last = pool.memset(rank[:, e:e + 1], float(E - e))
            last.then_inc(consts, 1)
            pool.iota(token[:], pattern=[[P, HALVES], [B, T]], base=0, channel_multiplier=1).then_inc(consts, 1)
            pool.wait_ge(x1_copied, 1)
            for n, m in enumerate(FLAT):
                if n % 4 == 0:
                    pool.wait_ge(slot_ready, n // 4 + 1)
                pool.indirect_dma_start(xe, bass.IndirectOffsetOnAxis(sloti[:, m:m + 1], 0), z[:, m], None,
                                        bounds_check=E * CAP - 1, oob_is_err=False).then_inc(scattered, 16)
            split_low(0, 0)
            split_low(1, 1)
            pool.wait_ge(scattered, 16 * TILES)
            pool.wait_ge(x1_out, 16 * HALVES)
            out_rows = out.rearrange("t b d -> (t b) d")

            def expert(e, i, more):
                pool.wait_ge(y_ready, 2 + e + 1)
                pool.sem_inc(y_sent, 1)
                for k in range(CT):
                    pool.indirect_dma_start(out_rows, bass.IndirectOffsetOnAxis(to[i][:, k:k + 1], 0), yb[i][:, k],
                                            None, bounds_check=TOK - 1, oob_is_err=False).then_inc(y_out, 16)
                if more == 2:
                    split_low(e + 2, i)
                pool.wait_ge(y_out, (e + 1) * 16 * CT)
                pool.sem_inc(y_stored, 1)

            pool.sem_inc(y_stored, 2)
            experts(pool, expert)

        @block.vector
        def _(dve):
            def split_low(e, i):
                dve.wait_ge(w2_hi, e + 1)
                dve.tensor_tensor(w2p[i][LO][:], w2s[i][:], w2p[i][HI][:].bitcast(F32),
                                  ALU.subtract).then_inc(w2_lo, 1)

            dve.tensor_scalar(ve[:], stats[:, :, 1], EPS, None, ALU.add).then_inc(var_ready, 1)
            dve.wait_ge(sd_ready, 1)
            dve.reciprocal(rstd[:], rstd[:]).then_inc(ln, 1)
            dve.wait_ge(ln, 1)
            newton_rsqrt(dve, ve[:], rstd[:], tmp[:], ln, 1)
            for n, m in enumerate(FLAT):
                last = dve.tensor_scalar(z[:, m, 0:D], hall[:, m], stats[:, m, 0:1], rstd[:, m:m + 1],
                                         ALU.subtract, ALU.mult)
                if n % 4 == 3:
                    last.then_inc(z_ready, 1)
            dve.wait_ge(consts, 4)
            dve.tensor_copy(z[:, :, TOKEN], token[:])
            rt_count = [0]

            def then(instruction):
                instruction.then_inc(rt, 1)
                rt_count[0] += 1
                dve.wait_ge(rt, rt_count[0])

            def wide(a):
                return a.unsqueeze(3).to_broadcast([P, HALVES, 2, E])

            def copy_zt(q):
                dve.wait_ge(ztp, 2 * q + 1)
                if q >= 2:
                    dve.wait_ge(logits, q - 1)
                dve.tensor_copy(zt[:, 2 * q % 4], H[2 * q % 4][:].rearrange("p a (b n) -> p (a b) n", n=P)) \
                    .then_inc(zt_ready[0], 1)

            def choose(q):
                lq, oq, mq, tq = quad(lg[:], q), quad(oh[:], q), quad(mx[:], q), quad(top[:], q)
                dve.wait_ge(logits, q + 1)
                then(dve.tensor_copy(lq, rp[q]))
                then(dve.reduce_max(mq, lq, AX))
                dve.tensor_tensor(quad(ex[:], q), lq, wide(mq), ALU.subtract).then_inc(shifted, 1)
                then(dve.tensor_tensor(oq, lq, wide(mq), ALU.is_equal))
                then(dve.tensor_tensor(oq, oq, rank[:].unsqueeze(1).unsqueeze(1).to_broadcast([P, HALVES, 2, E]),
                                       ALU.mult))
                then(dve.reduce_max(tq, oq, AX))
                then(dve.tensor_tensor(oq, oq, wide(tq), ALU.is_equal))
                for n in range(4 * q, 4 * q + 4):
                    if n == 0:
                        then(dve.memset(pre[:, FLAT[0]], 0.0))
                    else:
                        then(dve.tensor_tensor(pre[:, FLAT[n]], pre[:, FLAT[n - 1]], oh[:, FLAT[n - 1]], ALU.add))
                dve.sem_inc(oh_ready, 1)

            def place(q):
                lq, oq, tq = quad(lg[:], q), quad(oh[:], q), quad(top[:], q)
                gq, pq, sq = quad(gate[:], q), quad(pos[:], q), quad(slot[:], q)
                dve.wait_ge(expd, q + 1)
                then(dve.reduce_sum(gq, quad(ex[:], q), AX))
                dve.reciprocal(quad(z[:, :, GATE], q), gq)
                dve.wait_ge(pos_mm, q + 1)
                then(dve.tensor_tensor(lq, rp[q], oq, ALU.mult))
                then(dve.reduce_sum(pq, lq, AX))
                dve.tensor_scalar(sq, pq, float(CAP), float(2 * E * CAP), ALU.is_ge, ALU.mult)
                then(dve.tensor_scalar(tq, tq, -float(CAP), float(E * CAP), ALU.mult, ALU.add))
                then(dve.tensor_tensor(sq, sq, pq, ALU.add))
                then(dve.tensor_tensor(sq, sq, tq, ALU.add))
                dve.tensor_copy(quad(sloti[:], q), sq).then_inc(slot_ready, 1)

            for q in range(QUADS + 2):
                if q < QUADS:
                    copy_zt(q)
                if 1 <= q <= QUADS:
                    choose(q - 1)
                if q >= 2:
                    place(q - 2)

            def split_x(e, i):
                for c in range(DC):
                    dve.wait_ge(xT_hi, e * DC + c + 1)
                    dve.tensor_tensor(xT[i][LO][:, c], tp[c][:, 0:CAP], xT[i][HI][:, c].bitcast(F32),
                                      ALU.subtract).then_inc(xT_lo, 1)

            def expert(e, i, more):
                j = 1 - i
                for u in range(HU):
                    dve.wait_ge(hid_hi, e * HU + u + 1)
                    part = slice(2 * u, 2 * u + 2)
                    dve.tensor_tensor(hid[i][LO][:, part], H[u][:], hid[i][HI][:, part].bitcast(F32),
                                      ALU.subtract).then_inc(hid_lo, 1)
                if more:
                    split_x(e + 1, j)
                    split_low(e + 1, j)
                dve.wait_ge(y_stored, e + 1)
                dve.tensor_copy(to[i][:], xn[i][:, :, TOKEN])
                dve.wait_ge(y_mm, 2 + e + 1)
                for k in range(CT):
                    last = dve.scalar_tensor_tensor(yb[i][:, k], Yp[i][:, k], xn[i][:, k, GATE:GATE + 1],
                                                    xn[i][:, k, X1:X1 + D], ALU.mult, ALU.add)
                last.then_inc(y_ready, 1)

            split_low(0, 0)
            dve.sem_inc(y_ready, 2)
            split_x(0, 0)
            experts(dve, expert)

        @block.scalar
        def _(act):
            act.wait_ge(var_ready, 1)
            act.activation(rstd[:], ve[:], ACT.Sqrt).then_inc(sd_ready, 1)
            act.activation(z[:, :, X1:X1 + D], hall[:], ACT.Copy).then_inc(x1_copied, 1)
            for q in range(QUADS + 1):
                if q < QUADS:
                    act.wait_ge(ztp, 2 * q + 2)
                    if q >= 2:
                        act.wait_ge(logits, q - 1)
                    act.activation(zt[:, (2 * q + 1) % 4], H[(2 * q + 1) % 4][:].rearrange("p a (b n) -> p (a b) n", n=P),
                                   ACT.Copy).then_inc(zt_ready[1], 1)
                if q:
                    act.wait_ge(shifted, q)
                    act.activation(quad(ex[:], q - 1), quad(ex[:], q - 1), ACT.Exp).then_inc(expd, 1)

            def split_w1(e, i, arrived):
                act.wait_ge(w1_in[i], arrived)
                act.activation(w1p[i][HI][:], w1s[i][:], ACT.Copy).then_inc(w1_hi, 1)

            def split_w2(e, i, arrived):
                act.wait_ge(w2_in[i], arrived)
                act.activation(w2p[i][HI][:], w2s[i][:], ACT.Copy).then_inc(w2_hi, 1)

            split_w1(0, 0, 16)
            split_w1(1, 1, 16)
            split_w2(0, 0, 16)

            def split_x(e, i):
                for c in range(DC):
                    act.wait_ge(xtp, e * DC + c + 1)
                    act.activation(xT[i][HI][:, c], tp[c][:, 0:CAP], ACT.Copy).then_inc(xT_hi, 1)

            def expert(e, i, more):
                act.wait_ge(y_mm, e + 1)
                for u in range(HU):
                    act.wait_ge(h_mm, e * HU + u + 1)
                    act.activation(H[u][:], H[u][:], ACT.Gelu_apprx_tanh).then_inc(gelu, 1)
                    act.wait_ge(gelu, e * HU + u + 1)
                    act.activation(hid[i][HI][:, 2 * u:2 * u + 2], H[u][:], ACT.Copy).then_inc(hid_hi, 1)
                if more:
                    split_x(e + 1, 1 - i)
                    split_w2(e + 1, 1 - i, (e + 2 + i) * 8)
                if more == 2:
                    split_w1(e + 2, i, (e - i) * 8 + 32)

            split_x(0, 0)
            experts(act, expert)

        @block.tensor
        def _(pe):
            pe.sem_inc(y_mm, 2)
            pe.wait_ge(rw_in, 16)

            def row_transposes(q):
                pe.wait_ge(z_ready, q + 1)
                for c in range(DC):
                    for k in range(4):
                        last = pe.transpose(H[(2 * q + c) % 4][:, k // 2, k % 2 * P:(k % 2 + 1) * P],
                                            z[:, FLAT[4 * q + k], c * P:(c + 1) * P], ident[:])
                    last.then_inc(ztp, 1)

            def row_logits(q):
                for c in range(DC):
                    pe.wait_ge(zt_ready[c], q + 1)
                for k in range(4):
                    for c in range(DC):
                        last = pe.matmul(rp[q][:, k % 2, k // 2], zt[:, (2 * q + c) % 4, k], rw[:, c],
                                         start=(c == 0), stop=(c == DC - 1))
                last.then_inc(logits, 1)

            def positions(q):
                pe.wait_ge(oh_ready, q + 1)
                pe.matmul(rp[q], before[:], quad(oh[:], q), start=True, stop=False)
                pe.matmul(rp[q], ones[:], quad(pre[:], q), start=False, stop=True).then_inc(pos_mm, 1)

            pe.wait_ge(consts, 2)
            for q in range(QUADS + 2):
                if q < QUADS:
                    row_transposes(q)
                if 1 <= q <= QUADS:
                    row_logits(q - 1)
                if q >= 2:
                    positions(q - 2)

            def transpose_x(i, arrivals):
                pe.wait_ge(x_in[i], arrivals)
                for c in range(DC):
                    for k in range(CT):
                        last = pe.transpose(tp[c][:, k * P:(k + 1) * P], xn[i][:, k, c * P:(c + 1) * P], ident[:])
                    last.then_inc(xtp, 1)

            def expert(e, i, more):
                pe.wait_ge(w1_lo, e + 1)
                pe.wait_ge(xT_lo, (e + 1) * DC)
                for u in range(HU):
                    for k in range(2):
                        f = (2 * u + k) * P
                        for c in range(DC):
                            for n, (a, b) in enumerate(PARTS):
                                last = pe.matmul(H[u][:, k], w1p[i][a][:, c, f:f + P], xT[i][b][:, c],
                                                 start=(c == 0 and n == 0), stop=(c == DC - 1 and n == 2))
                    last.then_inc(h_mm, 1)
                if more:
                    transpose_x(1 - i, (e + 2 + i) * 8)
                pe.wait_ge(w2_lo, e + 1)
                pe.wait_ge(y_ready, e + 1)
                for f in range(FC):
                    if f % 2 == 0:
                        pe.wait_ge(hid_lo, e * HU + f // 2 + 1)
                    for k in range(CT):
                        for n, (a, b) in enumerate(PARTS):
                            last = pe.matmul(Yp[i][:, k], hid[i][a][:, f, k * P:(k + 1) * P], w2p[i][b][:, f],
                                             start=(f == 0 and k == 0 and n == 0), stop=(f == FC - 1 and n == 2),
                                             skip_group_check=True)
                last.then_inc(y_mm, 1)

            transpose_x(0, 16)
            experts(pe, expert)


def decoder_kernel(nc, x, context, w_qkvb, w_o, ln_g, ln_b, w_q, w_k, w_v, w_out, b_out, router_w, w1, w2, out):
    xe = nc.dram_tensor("expert_in", [E * CAP, ROW], F32, kind="Internal").ap()
    with ExitStack() as ctx:
        ident = ctx.enter_context(nc.sbuf_tensor("ident", [P, P], F32))
        hall = ctx.enter_context(nc.sbuf_tensor("hall", [P, TILES, D], F32))
        stats = ctx.enter_context(nc.sbuf_tensor("stats", [P, TILES, 2], F32))
        fast_weight_block(nc, x, w_qkvb, w_o, ident, hall)
        with ExitStack() as cross:
            zT = [cross.enter_context(nc.sbuf_tensor(f"zT{i}", [P, DC, TOK], F32R)) for i in (HI, LO)]
            cT = [cross.enter_context(nc.sbuf_tensor(f"cT{i}", [P, TOK], F32R)) for i in (HI, LO)]
            cS = cross.enter_context(nc.sbuf_tensor("cS", [P, TOK], F32R))
            wst = cross.enter_context(nc.sbuf_tensor("wst", [P, 6, XD], F32))
            w = [cross.enter_context(nc.sbuf_tensor(f"w{i}", [P, 6, XD], F32R)) for i in (HI, LO)]
            cross_inputs_block(nc, x, context, ln_g, ln_b, b_out, w_q, w_k, w_v, ident, hall, zT, cT, cS, wst, w)
            cross_attention_block(nc, w_q, w_k, w_v, w_out, ident, hall, zT, cT, cS, wst, w, stats, xe)
        expert_block(nc, router_w, w1, w2, out, ident, hall, stats, xe)


_INS = ['x', 'ctx_768', 'L0_attn_W_qkvb', 'L0_attn_W_o', 'L0_attn_ln_g', 'L0_attn_ln_b', 'L0_xattn_Wq', 'L0_xattn_Wk',
        'L0_xattn_Wv', 'L0_xattn_Wout', 'L0_xattn_bout', 'L0_ffn_router_w', 'L0_ffn_w1', 'L0_ffn_w2']


def kernel(**inputs):
    import numpy as _np
    import concourse.bacc as _bacc
    from concourse import mybir as _mybir
    from concourse.bass_utils import run_bass_kernel_spmd as _run

    nc = _bacc.Bacc("TRN2", target_bir_lowering=False, num_devices=1)
    arrays, args = {}, []
    for name in _INS:
        a = _np.ascontiguousarray(inputs[name])
        arrays[f"in_{name}_dram"] = a
        args.append(nc.dram_tensor(f"in_{name}_dram", a.shape, _mybir.dt.from_np(a.dtype), kind="ExternalInput").ap())
    args.append(nc.dram_tensor("out_0_dram", (T, B, D), F32, kind="ExternalOutput").ap())
    decoder_kernel(nc, *args)
    r = _run(nc, [arrays], core_ids=[0])
    return r.results[0]["out_0_dram"]
```
